# Optimizing a Trainium2 kernel written in Bass

```python
import numpy as np
import jax
import jax.numpy as jnp

def _softmax(x, axis=-1):
    return jax.nn.softmax(x, axis=axis)

def _gelu(x):
    return jax.nn.gelu(x, approximate=True)

def _silu(x):
    return jax.nn.silu(x)

def _sigmoid(x):
    return jax.nn.sigmoid(x)

def _layernorm(x, axis=-1, eps=1e-05):
    m = jnp.mean(x, axis=axis, keepdims=True)
    v = jnp.var(x, axis=axis, keepdims=True)
    return (x - m) / jnp.sqrt(v + eps)

def _scatter_add(tgt, idx, src, axis=0):
    return tgt.at[idx].add(src)

def _segment_sum(src, seg, n):
    return jax.ops.segment_sum(src, seg, n)
kernel_name = 'mk_adj_resnorm_d4_adj_r2_62e921'

def setup_inputs(seed: int=0):
    np.random.seed(seed)
    _w = jnp.asarray

    def _rec_inputs():
        import jax
        import jax.numpy as jnp
        _gk = jax.random.key(seed)
        x = -0.0005207 + 1.001 * jax.random.normal(jax.random.fold_in(_gk, 1), (64, 128, 128), jnp.float32)
        _a = jax.random.bernoulli(jax.random.fold_in(_gk, 2), 0.0625, (64, 128, 128))
        _a = jnp.logical_or(_a, jnp.eye(128, dtype=bool))
        _af = _a.astype(jnp.float32)
        adj = _af
        return (x, adj)
    x, adj = _rec_inputs()

    def _L0_gnn_setup():
        import jax, jax.numpy as jnp
        import numpy as np
        B, N, H, F = (4, 2048, 128, 128)
        ADJ_DENSITY = 0.01
        key = jax.random.key(seed)
        kx, ka, kq, kk, kv = jax.random.split(key, 5)
        x = jax.random.normal(kx, (B, N, H), dtype=jnp.float32)
        adj = (jax.random.uniform(ka, (B, N, N)) < ADJ_DENSITY).astype(jnp.float32)
        adj = jnp.maximum(adj, jnp.eye(N, dtype=jnp.float32)[None, :, :])
        s = 0.02
        Wq = jax.random.normal(kq, (F, H), dtype=jnp.float32) * s
        Wk = jax.random.normal(kk, (F, H), dtype=jnp.float32) * s
        Wv = jax.random.normal(kv, (F, H), dtype=jnp.float32) * s
        return {'x': x, 'adj': adj, 'Wq': Wq, 'Wk': Wk, 'Wv': Wv}
    _L0_gnn_all = _L0_gnn_setup()
    _L0_gnn_in = {k: v for k, v in _L0_gnn_all.items() if k in ('Wq', 'Wk', 'Wv')}
    del _L0_gnn_all

    def _L1_gnn_setup():
        import jax, jax.numpy as jnp
        import numpy as np
        B, N, IN_F = (4, 256, 128)
        H, F = (8, 16)
        SLOPE = 0.2
        key = jax.random.key(seed)
        k1, k2, k3, k4, k5 = jax.random.split(key, 5)
        h = jax.random.normal(k1, (B, N, IN_F), dtype=jnp.float32)
        adj = jax.random.randint(k2, (B, N, N), 0, 2).astype(jnp.float32)
        eye = jnp.eye(N, dtype=jnp.float32)[None]
        adj = jnp.maximum(adj, eye)
        W_l = jax.random.normal(k3, (H * F, IN_F), dtype=jnp.float32) * 0.05
        W_r = jax.random.normal(k4, (H * F, IN_F), dtype=jnp.float32) * 0.05
        w_attn = jax.random.normal(k5, (F,), dtype=jnp.float32) * 0.05
        return {'h': h, 'adj_mat': adj, 'W_l': W_l, 'W_r': W_r, 'w_attn': w_attn}
    _L1_gnn_all = _L1_gnn_setup()
    _L1_gnn_in = {k: v for k, v in _L1_gnn_all.items() if k in ('W_l', 'W_r', 'w_attn')}
    del _L1_gnn_all

    def _L2_gnn_setup():
        import jax, jax.numpy as jnp
        import numpy as np
        B, S, H, HID = (1, 512, 128, 128)
        LN_EPS = 1e-05

        def _layernorm(y, gamma, beta):
            mu = jnp.mean(y, axis=-1, keepdims=True)
            var = jnp.mean(jnp.square(y - mu), axis=-1, keepdims=True)
            return (y - mu) * jax.lax.rsqrt(var + LN_EPS) * gamma + beta
        key = jax.random.key(seed)
        ks = jax.random.split(key, 8)
        x = jax.random.normal(ks[0], (B, S, H), dtype=jnp.float32)
        adj = jax.random.uniform(ks[1], (B, S, S), dtype=jnp.float32)
        W1 = jax.random.normal(ks[2], (2 * H, HID), dtype=jnp.float32) / np.sqrt(2 * H)
        b1 = jnp.zeros((HID,), dtype=jnp.float32)
        W2 = jax.random.normal(ks[3], (HID, HID), dtype=jnp.float32) / np.sqrt(HID)
        b2 = jnp.zeros((HID,), dtype=jnp.float32)
        gamma = jnp.ones((HID,), dtype=jnp.float32)
        beta = jnp.zeros((HID,), dtype=jnp.float32)
        return {'x': x, 'adj': adj, 'W1': W1, 'b1': b1, 'W2': W2, 'b2': b2, 'gamma': gamma, 'beta': beta}
    _L2_gnn_all = _L2_gnn_setup()
    _L2_gnn_in = {k: v for k, v in _L2_gnn_all.items() if k in ('W1', 'b1', 'W2', 'b2', 'gamma', 'beta')}
    del _L2_gnn_all

    def _L3_gnn_setup():
        import jax, jax.numpy as jnp
        import numpy as np

        def _normalize_adjacency(adj):
            N = adj.shape[-1]
            adj_self = adj + jnp.eye(N, dtype=adj.dtype)
            rowsum = adj_self.sum(axis=2)
            d_inv_sqrt = rowsum ** (-0.5)
            d_inv_sqrt = jnp.where(jnp.isinf(d_inv_sqrt), 0.0, d_inv_sqrt)
            return adj_self * d_inv_sqrt[:, :, None] * d_inv_sqrt[:, None, :]
        key = jax.random.key(seed)
        k1, k2, k3 = jax.random.split(key, 3)
        B, N, Fin, Fout = (32, 512, 128, 128)
        x = jax.random.normal(k1, (B, N, Fin), dtype=jnp.float32)
        adj = jax.random.uniform(k2, (B, N, N), dtype=jnp.float32)
        limit = float(np.sqrt(6.0 / (Fin + Fout)))
        weight = jax.random.uniform(k3, (Fin, Fout), dtype=jnp.float32, minval=-limit, maxval=limit)
        bias = jnp.zeros((Fout,), dtype=jnp.float32)
        return {'x': x, 'adj': adj, 'weight': weight, 'bias': bias}
    _L3_gnn_all = _L3_gnn_setup()
    _L3_gnn_in = {k: v for k, v in _L3_gnn_all.items() if k in ('weight', 'bias')}
    del _L3_gnn_all
    return {'x': x, 'adj': adj, 'L0_gnn_Wq': _L0_gnn_in['Wq'], 'L0_gnn_Wk': _L0_gnn_in['Wk'], 'L0_gnn_Wv': _L0_gnn_in['Wv'], 'L1_gnn_W_l': _L1_gnn_in['W_l'], 'L1_gnn_W_r': _L1_gnn_in['W_r'], 'L1_gnn_w_attn': _L1_gnn_in['w_attn'], 'L2_gnn_W1': _L2_gnn_in['W1'], 'L2_gnn_b1': _L2_gnn_in['b1'], 'L2_gnn_W2': _L2_gnn_in['W2'], 'L2_gnn_b2': _L2_gnn_in['b2'], 'L2_gnn_gamma': _L2_gnn_in['gamma'], 'L2_gnn_beta': _L2_gnn_in['beta'], 'L3_gnn_weight': _L3_gnn_in['weight'], 'L3_gnn_bias': _L3_gnn_in['bias']}

def reference(x, adj, L0_gnn_Wq, L0_gnn_Wk, L0_gnn_Wv, L1_gnn_W_l, L1_gnn_W_r, L1_gnn_w_attn, L2_gnn_W1, L2_gnn_b1, L2_gnn_W2, L2_gnn_b2, L2_gnn_gamma, L2_gnn_beta, L3_gnn_weight, L3_gnn_bias):
    import jax
    import jax.numpy as jnp

    def _L0_gnn_ref(x, adj, Wq, Wk, Wv):
        import jax, jax.numpy as jnp
        import numpy as np
        B, N, H, F = (4, 2048, 128, 128)
        ADJ_DENSITY = 0.01
        q = jnp.einsum('bnh,fh->bnf', x, Wq)
        k = jnp.einsum('bnh,fh->bnf', x, Wk)
        v = jnp.einsum('bnh,fh->bnf', x, Wv)
        scale = k.shape[-1] ** (-0.5)
        wei = jnp.einsum('bnf,bmf->bnm', q, k) * scale
        wei = jnp.where(adj == 0, -jnp.inf, wei)
        wei = jax.nn.softmax(wei, axis=-1)
        wei = wei + adj
        out = jnp.einsum('bnm,bmf->bnf', wei, v)
        return out

    def _L1_gnn_ref(h, adj_mat, W_l, W_r, w_attn):
        import jax, jax.numpy as jnp
        import numpy as np
        B, N, IN_F = (4, 256, 128)
        H, F = (8, 16)
        SLOPE = 0.2
        b, n, _ = h.shape
        g_l = (h @ W_l.T).reshape(b, n, H, F)
        g_r = (h @ W_r.T).reshape(b, n, H, F)
        g_sum = g_r[:, :, None, :, :] + g_l[:, None, :, :, :]
        e = jnp.einsum('bijhf,f->bijh', jax.nn.leaky_relu(g_sum, SLOPE), w_attn)
        mask = adj_mat[..., None]
        e = e * mask
        e = jnp.where(mask == 0, -jnp.inf, e)
        a = jax.nn.softmax(e, axis=2)
        attn_res = jnp.einsum('bijh,bjhf->bihf', a, g_r)
        out = jax.nn.leaky_relu(attn_res.reshape(b, n, H * F), SLOPE)
        return out

    def _L2_gnn_ref(x, adj, W1, b1, W2, b2, gamma, beta):
        import jax, jax.numpy as jnp
        import numpy as np
        B, S, H, HID = (1, 512, 128, 128)
        LN_EPS = 1e-05

        def _layernorm(y, gamma, beta):
            mu = jnp.mean(y, axis=-1, keepdims=True)
            var = jnp.mean(jnp.square(y - mu), axis=-1, keepdims=True)
            return (y - mu) * jax.lax.rsqrt(var + LN_EPS) * gamma + beta
        hi = jnp.einsum('bsh,hk->bsk', x, W1[:H])
        hj = jnp.einsum('bsh,hk->bsk', x, W1[H:])
        h = jax.nn.relu(hi[:, :, None, :] + hj[:, None, :, :] + b1)
        y = jnp.einsum('bijk,kl->bijl', h, W2) + b2
        y = _layernorm(y, gamma, beta)
        out = jnp.einsum('bij,bijh->bih', adj, y)
        return out

    def _L3_gnn_ref(x, adj, weight, bias):
        import jax, jax.numpy as jnp
        import numpy as np

        def _normalize_adjacency(adj):
            N = adj.shape[-1]
            adj_self = adj + jnp.eye(N, dtype=adj.dtype)
            rowsum = adj_self.sum(axis=2)
            d_inv_sqrt = rowsum ** (-0.5)
            d_inv_sqrt = jnp.where(jnp.isinf(d_inv_sqrt), 0.0, d_inv_sqrt)
            return adj_self * d_inv_sqrt[:, :, None] * d_inv_sqrt[:, None, :]
        adj_norm = _normalize_adjacency(adj)
        support = jnp.einsum('bni,io->bno', x, weight)
        out = jnp.einsum('bnm,bmo->bno', adj_norm, support) + bias
        return out
    x = _layernorm(x + _L0_gnn_ref(x, adj, L0_gnn_Wq, L0_gnn_Wk, L0_gnn_Wv), axis=-1)
    x = _layernorm(x + _L1_gnn_ref(x, adj, L1_gnn_W_l, L1_gnn_W_r, L1_gnn_w_attn), axis=-1)
    x = _layernorm(x + _L2_gnn_ref(x, adj, L2_gnn_W1, L2_gnn_b1, L2_gnn_W2, L2_gnn_b2, L2_gnn_gamma, L2_gnn_beta), axis=-1)
    x = _layernorm(x + _L3_gnn_ref(x, adj, L3_gnn_weight, L3_gnn_bias), axis=-1)
    return x

_drawn_inputs = setup_inputs


def setup_inputs(seed=0):
    import zlib

    import numpy as np

    out = dict(_drawn_inputs(seed))
    spreads = {'L2_gnn_b1': (0.0, 0.1),
     'L2_gnn_b2': (0.0, 0.1),
     'L2_gnn_gamma': (1.0, 0.2),
     'L2_gnn_beta': (0.0, 0.1),
     'L3_gnn_bias': (0.0, 0.1)}
    factors = {'L0_gnn_Wq': 8.0, 'L0_gnn_Wk': 8.0, 'L1_gnn_W_l': 7.958, 'L1_gnn_w_attn': 7.872}
    for name, (base, spread) in spreads.items():
        noise = np.random.default_rng([zlib.crc32(name.encode()), seed]).standard_normal(out[name].shape)
        drawn = base * np.exp(spread * noise) if base else spread * noise
        out[name] = jnp.asarray(drawn.astype(out[name].dtype))
    for name, factor in factors.items():
        out[name] = (out[name] * factor).astype(out[name].dtype)
    return out
```

```python
from contextlib import ExitStack

import concourse.bass as bass
from concourse import mybir

F32 = mybir.dt.float32
ALU = mybir.AluOpType
ACT = mybir.ActivationFunctionType
AX = mybir.AxisListType

P = 128
B = 64
HEADS = 8
HF = P // HEADS
SLOPE = 0.2
EPS = 1e-5
NEG = -1e30
G = 4
NG = B // G
RT = P // HEADS
NRT = P // RT
RS = 4



class Shared:
    pass


class Steps:

    def __init__(self, eng, sem, base=0):
        self.eng, self.sem, self.base, self.n = eng, sem, base, 0

    def add(self, instruction):
        instruction.then_inc(self.sem, 1)
        self.n += 1

    def wait(self):
        self.eng.wait_ge(self.sem, self.base + self.n)


def layer0(nc, e):
    c = ExitStack()
    with c:
        def sb(name, shape, dt=F32):
            return c.enter_context(nc.sbuf_tensor("a_" + name, shape, dt))

        def sem(name):
            return c.enter_context(nc.semaphore("a_" + name))

        cur, ident = e.cur, e.ident
        xin = sb("xin", [P, 2, G, P])
        ain = sb("ain", [P, 2, G, P])
        xT = sb("xT", [P, 2, G, P])
        tT = sb("tT", [P, 2, G, P])
        xv = sb("xv", [P, 2, G, P])
        drop = sb("drop", [P, G, P])
        sm = sb("sm", [P, 2, G, P])
        top = sb("top", [P, 2, G])
        ex = sb("ex", [P, 2, G, P])
        den = sb("den", [P, 2, G])
        rden = sb("rden", [P, G])
        pr = sb("pr", [P, 2, G, P])
        prT = sb("prT", [P, 2, G, P])
        res = sb("res", [P, G, P])
        mean = sb("mean", [P, G])
        junk = sb("junk", [P, P])
        x_in = [sem(f"x_in{b}") for b in range(2)]
        xT_mm, xT_ok, t_mm, t_ok, xv_mm, xv_ok, s_mm = (sem(k) for k in (
            "xT_mm", "xT_ok", "t_mm", "t_ok", "xv_mm", "xv_ok", "s_mm"))
        top_ok, ex_ok, pr_ok, prT_mm, prT_ok, o_mm, cen_ok, sq_ok = (sem(k) for k in (
            "top_ok", "ex_ok", "pr_ok", "prT_mm", "prT_ok", "o_mm", "cen_ok", "sq_ok"))
        res_ok, seq_f, seq_b = sem("res_ok"), sem("seq_f"), sem("seq_b")
        bX, bT, bV, bS, bP, bO = e.banks[:6]

        def grp(t):
            return t[:, :].rearrange("p (g f) -> p g f", g=G)

        def pipeline(eng, front, back):
            front(0, 0)
            front(1, 1)
            back(0, 0)
            with eng.Fori(0, NG // 2 - 1) as k:
                front(2 * k + 2, 0)
                back(2 * k + 1, 1)
                front(2 * k + 3, 1)
                back(2 * k + 2, 0)
            back(NG - 1, 1)

        with nc.Block() as block:
            @block.sync
            def _(sp):
                def load(n, b):
                    sp.dma_start(xin[:, b, :, :], e.x_v[:, bass.ds(n * G, G), :]).then_inc(x_in[b], 16)
                    sp.dma_start(ain[:, b, :, :], e.adj_v[:, bass.ds(n * G, G), :]).then_inc(x_in[b], 16)
                load(0, 0)
                load(1, 1)
                with sp.Fori(0, NG // 2 - 1) as k:
                    for b in range(2):
                        sp.wait_ge(res_ok, 2 * k + b + 1)
                        load(2 * k + 2 + b, b)

            @block.tensor
            def _(pe):
                def front(n, b):
                    pe.wait_ge(x_in[b], 16 * (n - b) + 32)
                    if not (isinstance(n, int) and n == 0):
                        pe.wait_ge(xT_ok, n)
                    for g in range(G):
                        m = pe.transpose(bX[:, P * g:P * g + P], xin[:, b, g, :], ident[:, :])
                    m.then_inc(xT_mm, 1)
                    pe.wait_ge(xT_ok, n + 1)
                    if not (isinstance(n, int) and n == 0):
                        pe.wait_ge(t_ok, n)
                        pe.wait_ge(xv_ok, n)
                    pe.matmul(bT[:, :], e.M[:, :], xT[:, b, :, :], start=True, stop=True).then_inc(t_mm, 1)
                    for g in range(G):
                        m = pe.matmul(bV[:, P * g:P * g + P], xT[:, b, g, :], e.WvT[:, :], start=True, stop=True)
                    m.then_inc(xv_mm, 1)
                    pe.wait_ge(t_ok, n + 1)
                    if not (isinstance(n, int) and n == 0):
                        pe.wait_ge(top_ok, n)
                    for g in range(G):
                        m = pe.matmul(bS[:, P * g:P * g + P], tT[:, b, g, :], xT[:, b, g, :], start=True, stop=True)
                    m.then_inc(s_mm, 1)

                def back(n, b):
                    pe.wait_ge(pr_ok, n + 1)
                    if not (isinstance(n, int) and n == 0):
                        pe.wait_ge(prT_ok, n)
                    for g in range(G):
                        m = pe.transpose(bP[:, P * g:P * g + P], pr[:, b, g, :], ident[:, :])
                    m.then_inc(prT_mm, 1)
                    pe.wait_ge(prT_ok, n + 1)
                    pe.wait_ge(xv_ok, n + 1)
                    if not (isinstance(n, int) and n == 0):
                        pe.wait_ge(res_ok, n)
                    for g in range(G):
                        m = pe.matmul(bO[:, P * g:P * g + P], prT[:, b, g, :], xv[:, b, g, :], start=True, stop=True)
                    m.then_inc(o_mm, 1)

                pipeline(pe, front, back)

            @block.scalar
            def _(act):
                def front(n, b):
                    act.wait_ge(xT_mm, n + 1)
                    if not isinstance(n, int) or n >= 2:
                        act.wait_ge(s_mm, n - 1)
                    act.copy(xT[:, b, :, :], grp(bX)).then_inc(xT_ok, 1)
                    act.wait_ge(xv_mm, n + 1)
                    if not isinstance(n, int) or n >= 2:
                        act.wait_ge(o_mm, n - 1)
                    act.copy(xv[:, b, :, :], grp(bV)).then_inc(xv_ok, 1)
                    act.wait_ge(top_ok, n + 1)
                    if not isinstance(n, int) or n >= 2:
                        act.wait_ge(pr_ok, n - 1)
                    for g in range(G):
                        act.activation(ex[:, b, g, :], sm[:, b, g, :], ACT.Exp, bias=top[:, b, g:g + 1],
                                       accum_out=den[:, b, g:g + 1]).then_inc(ex_ok, 1)

                def back(n, b):
                    act.wait_ge(prT_mm, n + 1)
                    act.copy(prT[:, b, :, :], grp(bP)).then_inc(prT_ok, 1)
                    act.wait_ge(cen_ok, n + 1)
                    for g in range(G):
                        if isinstance(n, int) and n == 0 and g == 0:
                            pass
                        else:
                            act.wait_ge(sq_ok, G * n + g)
                        act.activation(junk[:, :], cur[:, n * G + g, :], ACT.Square,
                                       accum_out=e.sqsum[:, bass.ds(n * G + g, 1)]).then_inc(sq_ok, 1)

                pipeline(act, front, back)

            @block.vector
            def _(v):
                def front(n, b):
                    v.wait_ge(x_in[b], 16 * (n - b) + 32)
                    q = Steps(v, seq_f, 2 * n)
                    v.wait_ge(t_mm, n + 1)
                    if not isinstance(n, int) or n >= 2:
                        v.wait_ge(s_mm, n - 1)
                    v.tensor_copy(tT[:, b, :, :], grp(bT)).then_inc(t_ok, 1)
                    q.add(v.tensor_scalar(drop[:, :, :], ain[:, b, :, :], 0.0, NEG, ALU.is_equal, ALU.mult))
                    v.wait_ge(s_mm, n + 1)
                    q.wait()
                    if not isinstance(n, int) or n >= 2:
                        v.wait_ge(ex_ok, G * (n - 1))
                    q.add(v.tensor_tensor(sm[:, b, :, :], grp(bS), drop[:, :, :], ALU.add))
                    q.wait()
                    v.tensor_reduce(top[:, b, :], sm[:, b, :, :], AX.X, ALU.max, negate=True).then_inc(top_ok, 1)

                def back(n, b):
                    q = Steps(v, seq_b, 3 * n)
                    v.wait_ge(ex_ok, G * (n + 1))
                    if not isinstance(n, int) or n >= 2:
                        v.wait_ge(prT_mm, n - 1)
                    q.add(v.reciprocal(rden[:, :], den[:, b, :]))
                    q.wait()
                    for g in range(G):
                        m = v.scalar_tensor_tensor(pr[:, b, g, :], ex[:, b, g, :], rden[:, g:g + 1], ain[:, b, g, :],
                                                   ALU.mult, ALU.add)
                    m.then_inc(pr_ok, 1)
                    v.wait_ge(o_mm, n + 1)
                    v.tensor_tensor(res[:, :, :], grp(bO), xin[:, b, :, :], ALU.add).then_inc(res_ok, 1)
                    v.wait_ge(res_ok, n + 1)
                    q.add(v.tensor_reduce(mean[:, :], res[:, :, :], AX.X, ALU.add))
                    q.wait()
                    q.add(v.tensor_scalar(mean[:, :], mean[:, :], 1.0 / P, None, ALU.mult))
                    q.wait()
                    v.tensor_tensor(cur[:, bass.ds(n * G, G), :], res[:, :, :],
                                    mean[:, :].unsqueeze(2).broadcast_to([P, G, P]), ALU.subtract).then_inc(cen_ok, 1)
                    v.wait_ge(cen_ok, n + 1)

                pipeline(v, front, back)


def layer1_dense(nc, e):
    c = ExitStack()
    with c:
        def sb(name, shape, dt=F32):
            return c.enter_context(nc.sbuf_tensor("b_" + name, shape, dt))

        def sem(name):
            return c.enter_context(nc.semaphore("b_" + name))

        cur, ident = e.cur, e.ident
        ain = sb("ain", [P, P])
        xin = sb("xin", [P, P])
        xT = sb("xT", [P, P])
        gT = sb("gT", [P, 2, P])
        gr = sb("gr", [P, P])
        u = sb("u", [P, 2, RS, P])
        lk = sb("lk", [P, 2, RS, P])
        arep = sb("arep", [P, P])
        drop = sb("drop", [P, P])
        sc = sb("sc", [P, P])
        top = sb("top", [P, 1])
        ex = sb("ex", [P, P])
        den = sb("den", [P, 1])
        aT = sb("aT", [P, P])
        od = sb("od", [P, P])
        res = sb("res", [P, P])
        mean = sb("mean", [P, 1])
        junk = sb("junk", [P, P])
        (a_in, x_ok, xT_mm, xT_ok, g_mm, gT_ok, lk_ok, lk_used, e_mm, rep_mm, arep_ok, top_ok, ex_ok, a_ok, aT_mm, aT_ok,
         o_mm, od_ok, out_mm, cen_ok, sq_ok, seq_g, seq_s, seq_t) = (sem(k) for k in (
             "a_in", "x_ok", "xT_mm", "xT_ok", "g_mm", "gT_ok", "lk_ok", "lk_used", "e_mm", "rep_mm", "arep_ok", "top_ok",
             "ex_ok", "a_ok", "aT_mm", "aT_ok", "o_mm", "od_ok", "out_mm", "cen_ok", "sq_ok", "seq_g", "seq_s", "seq_t"))
        seq_x = sem("seq_x")
        bX, bG, bE, bR, bT, bO, bZ = e.banks[:7]
        NS = P // RS

        with nc.Block() as block:
            @block.sync
            def _(sp):
                sp.dma_start(ain[:, :], e.adj_v[:, 0, :]).then_inc(a_in, 16)
                with sp.Fori(1, B) as n:
                    sp.wait_ge(rep_mm, NRT * n)
                    sp.dma_start(ain[:, :], e.adj_v[:, n, :]).then_inc(a_in, 16)

            @block.tensor
            def _(pe):
                with pe.Fori(0, B) as n:
                    pe.wait_ge(x_ok, n + 1)
                    pe.transpose(bX[:, 0:P], xin[:, :], ident[:, :]).then_inc(xT_mm, 1)
                    pe.wait_ge(xT_ok, n + 1)
                    pe.matmul(bG[:, 0:P], e.WlT[:, :], xT[:, :], start=True, stop=True)
                    pe.matmul(bG[:, P:2 * P], e.WrT[:, :], xT[:, :], start=True, stop=True)
                    pe.matmul(bG[:, 2 * P:3 * P], xT[:, :], e.WrT[:, :], start=True, stop=True).then_inc(g_mm, 1)
                    pe.wait_ge(a_in, 16 * n + 16)
                    pe.wait_ge(gT_ok, n + 1)
                    for t in range(NRT):
                        m = NRT * n + t
                        pe.matmul(bR[:, 0:P], e.Rep[:, :, :].rearrange("i r h -> i (r h)")[:, P * t:P * t + P],
                                  ain[:, :], start=True, stop=True).then_inc(rep_mm, 1)
                        for k in range(RT // RS):
                            s = NS * n + (RT // RS) * t + k
                            pe.wait_ge(lk_ok, s + 1)
                            for r in range(RS):
                                row = RS * k + r
                                w = e.Wpad[:, P - HEADS - HEADS * row:2 * P - HEADS - HEADS * row]
                                q = pe.matmul(bE[:, 0:P], w, lk[:, k % 2, r, :], start=(row == 0), stop=(row == RT - 1))
                            q.then_inc(lk_used, 1)
                        pe.wait_ge(a_ok, m + 1)
                        pe.transpose(bT[:, 0:P], ex[:, :], ident[:, :]).then_inc(aT_mm, 1)
                        pe.wait_ge(aT_ok, m + 1)
                        pe.matmul(bO[:, 0:P], aT[:, :], gr[:, :], start=True, stop=True).then_inc(o_mm, 1)
                        pe.wait_ge(od_ok, m + 1)
                        pe.matmul(bZ[:, 0:P], e.RepT[:, t, :], od[:, :], start=(t == 0), stop=(t == NRT - 1)).then_inc(out_mm, 1)

            @block.scalar
            def _(act):
                with act.Fori(0, B) as n:
                    act.wait_ge(xT_mm, n + 1)
                    act.copy(xT[:, :], bX[:, 0:P]).then_inc(xT_ok, 1)
                    act.wait_ge(g_mm, n + 1)
                    act.copy(gT[:, :, :], bG[:, 0:2 * P].rearrange("p (a f) -> p a f", a=2)).then_inc(gT_ok, 1)
                    act.copy(gr[:, :], bG[:, 2 * P:3 * P]).then_inc(seq_g, 1)
                    act.wait_ge(seq_g, n + 1)
                    for t in range(NRT):
                        m = NRT * n + t
                        act.wait_ge(top_ok, m + 1)
                        act.activation(ex[:, :], sc[:, :], ACT.Exp, bias=top[:, 0:1], accum_out=den[:, 0:1]).then_inc(ex_ok, 1)
                        act.wait_ge(aT_mm, m + 1)
                        act.copy(aT[:, :], bT[:, 0:P]).then_inc(aT_ok, 1)
                    act.wait_ge(cen_ok, n + 1)
                    act.activation(junk[:, :], cur[:, n, :], ACT.Square, accum_out=e.sqsum[:, bass.ds(n, 1)]).then_inc(sq_ok, 1)
                    act.wait_ge(sq_ok, n + 1)

            @block.vector
            def _(v):
                with v.Fori(0, B) as n:
                    v.tensor_copy(xin[:, :], cur[:, n, :]).then_inc(x_ok, 1)
                    v.wait_ge(gT_ok, n + 1)
                    v.wait_ge(seq_g, n + 1)
                    for t in range(NRT):
                        m = NRT * n + t
                        for k in range(RT // RS):
                            s = NS * n + (RT // RS) * t + k
                            q = Steps(v, seq_s, s)
                            b = k % 2
                            for r in range(RS):
                                i = RT * t + RS * k + r
                                d = v.tensor_scalar(u[:, b, r, :], gT[:, 0, :], gT[:, 1, i:i + 1], None, ALU.add)
                            q.add(d)
                            q.wait()
                            if t == 0 and k < 2:
                                v.wait_ge(out_mm, NRT * n)
                            else:
                                v.wait_ge(lk_used, s - 1)
                            v.scalar_tensor_tensor(lk[:, b, :, :], u[:, b, :, :], SLOPE, u[:, b, :, :],
                                                   ALU.mult, ALU.max).then_inc(lk_ok, 1)
                        q = Steps(v, seq_t, 5 * m)
                        v.wait_ge(rep_mm, m + 1)
                        q.add(v.tensor_copy(arep[:, :], bR[:, 0:P]))
                        q.wait()
                        q.add(v.tensor_scalar(drop[:, :], arep[:, :], 0.0, NEG, ALU.is_equal, ALU.mult))
                        v.wait_ge(lk_used, NS * n + (RT // RS) * (t + 1))
                        q.add(v.tensor_tensor(sc[:, :], bE[:, 0:P], arep[:, :], ALU.mult))
                        q.wait()
                        q.add(v.tensor_tensor(sc[:, :], sc[:, :], drop[:, :], ALU.add))
                        q.wait()
                        v.tensor_reduce(top[:, :], sc[:, :], AX.X, ALU.max, negate=True).then_inc(top_ok, 1)
                        v.wait_ge(ex_ok, m + 1)
                        q.add(v.reciprocal(den[:, :], den[:, :]))
                        q.wait()
                        v.tensor_scalar(ex[:, :], ex[:, :], den[:, 0:1], None, ALU.mult).then_inc(a_ok, 1)
                        v.wait_ge(o_mm, m + 1)
                        v.tensor_tensor(od[:, :], bO[:, 0:P], e.diag[:, :], ALU.mult).then_inc(od_ok, 1)
                    v.wait_ge(out_mm, NRT * (n + 1))
                    q = Steps(v, seq_x, 5 * n)
                    q.add(v.tensor_copy(res[:, :], bZ[:, 0:P]))
                    q.wait()
                    q.add(v.scalar_tensor_tensor(res[:, :], res[:, :], SLOPE, res[:, :], ALU.mult, ALU.max))
                    q.wait()
                    q.add(v.tensor_tensor(res[:, :], res[:, :], xin[:, :], ALU.add))
                    q.wait()
                    q.add(v.tensor_reduce(mean[:, :], res[:, :], AX.X, ALU.add))
                    q.wait()
                    q.add(v.tensor_scalar(mean[:, :], mean[:, :], 1.0 / P, None, ALU.mult))
                    q.wait()
                    v.tensor_scalar(cur[:, n, :], res[:, :], mean[:, 0:1], None, ALU.subtract).then_inc(cen_ok, 1)
                    v.wait_ge(cen_ok, n + 1)


def layer2_dense(nc, e):
    c = ExitStack()
    with c:
        def sb(name, shape, dt=F32):
            return c.enter_context(nc.sbuf_tensor("c_" + name, shape, dt))

        def sem(name):
            return c.enter_context(nc.semaphore("c_" + name))

        cur, ident = e.cur, e.ident
        ain = sb("ain", [P, P])
        aT = sb("aT", [P, P])
        xin = sb("xin", [P, P])
        xT = sb("xT", [P, P])
        hT = sb("hT", [P, 2, P])
        h = sb("h", [P, 2, RS, P])
        y = sb("y", [P, P, P])
        ysq = sb("ysq", [P, 2, RS, P])
        cf = sb("cf", [P, P])
        zT = sb("zT", [P, P])
        asum = sb("asum", [P, 1])
        bb = sb("bb", [P, P])
        res = sb("res", [P, P])
        mean = sb("mean", [P, 1])
        junk = sb("junk", [P, P])
        (a_in, x_ok, xT_mm, xT_ok, g_mm, h1_ok, h_ok, y_mm, y_ok, ysq_ok, var_ok, cf_root, cf_ok, aT_ok, z_mm, zT_ok,
         zt_mm, cen_ok, sq_ok, seq_c, seq_x) = (sem(k) for k in (
             "a_in", "x_ok", "xT_mm", "xT_ok", "g_mm", "h1_ok", "h_ok", "y_mm", "y_ok", "ysq_ok", "var_ok", "cf_root",
             "cf_ok", "aT_ok", "z_mm", "zT_ok", "zt_mm", "cen_ok", "sq_ok", "seq_c", "seq_x"))
        bX, bG, bY0, bY1, bZ, bZT = e.banks[:6]
        bY = (bY0, bY1)
        NS = P // RS

        with nc.Block() as block:
            @block.sync
            def _(sp):
                sp.dma_start(ain[:, :], e.adj_v[:, 0, :]).then_inc(a_in, 16)
                with sp.Fori(1, B) as n:
                    sp.wait_ge(cen_ok, n)
                    sp.dma_start(ain[:, :], e.adj_v[:, n, :]).then_inc(a_in, 16)

            @block.tensor
            def _(pe):
                with pe.Fori(0, B) as n:
                    pe.wait_ge(x_ok, n + 1)
                    pe.wait_ge(a_in, 16 * n + 16)
                    pe.transpose(bX[:, 0:P], xin[:, :], ident[:, :])
                    pe.transpose(bX[:, P:2 * P], ain[:, :], ident[:, :]).then_inc(xT_mm, 1)
                    pe.wait_ge(xT_ok, n + 1)
                    pe.matmul(bG[:, 0:P], e.W1s[:, 0, :], xT[:, :], start=True, stop=True)
                    pe.matmul(bG[:, P:2 * P], e.W1s[:, 1, :], xT[:, :], start=True, stop=True).then_inc(g_mm, 1)
                    for k in range(NS):
                        s = NS * n + k
                        pe.wait_ge(h_ok, s + 1)
                        if k >= 2:
                            pe.wait_ge(y_ok, s - 1)
                        for r in range(RS):
                            q = pe.matmul(bY[k % 2][:, P * r:P * r + P], h[:, k % 2, r, :], e.W2c[:, :], start=True, stop=True)
                        q.then_inc(y_mm, 1)
                    pe.wait_ge(cf_ok, n + 1)
                    for i in range(P):
                        q = pe.matmul(bZ[:, i:i + 1], y[:, i, :], cf[:, i:i + 1], start=True, stop=True)
                    q.then_inc(z_mm, 1)
                    pe.wait_ge(zT_ok, n + 1)
                    pe.transpose(bZT[:, 0:P], zT[:, :], ident[:, :]).then_inc(zt_mm, 1)

            @block.scalar
            def _(act):
                with act.Fori(0, B) as n:
                    act.wait_ge(xT_mm, n + 1)
                    act.copy(aT[:, :], bX[:, P:2 * P]).then_inc(aT_ok, 1)
                    act.copy(xT[:, :], bX[:, 0:P]).then_inc(xT_ok, 1)
                    for k in range(NS):
                        s = NS * n + k
                        act.wait_ge(y_ok, s + 1)
                        if k >= 2:
                            act.wait_ge(var_ok, s - 1)
                        act.activation(ysq[:, k % 2, :, :], y[:, RS * k:RS * k + RS, :], ACT.Square).then_inc(ysq_ok, 1)
                    act.wait_ge(var_ok, NS * (n + 1))
                    act.activation(cf[:, :], cf[:, :], ACT.Sqrt, bias=e.eps[:, 0:1], scale=1.0 / P).then_inc(cf_root, 1)
                    act.wait_ge(z_mm, n + 1)
                    act.copy(zT[:, :], bZ[:, 0:P]).then_inc(zT_ok, 1)
                    act.wait_ge(cen_ok, n + 1)
                    act.activation(junk[:, :], cur[:, n, :], ACT.Square, accum_out=e.sqsum[:, bass.ds(n, 1)]).then_inc(sq_ok, 1)
                    act.wait_ge(sq_ok, n + 1)

            @block.vector
            def _(v):
                with v.Fori(0, B) as n:
                    v.tensor_copy(xin[:, :], cur[:, n, :]).then_inc(x_ok, 1)
                    v.wait_ge(g_mm, n + 1)
                    v.tensor_copy(hT[:, 0, :], bG[:, 0:P]).then_inc(h1_ok, 1)
                    v.tensor_scalar(hT[:, 1, :], bG[:, P:2 * P], e.b1c[:, 0:1], None, ALU.add).then_inc(h1_ok, 1)
                    v.wait_ge(h1_ok, 2 * n + 2)

                    def variance(k):
                        v.wait_ge(ysq_ok, NS * n + k + 1)
                        v.tensor_reduce(cf[:, RS * k:RS * k + RS], ysq[:, k % 2, :, :], AX.X, ALU.add).then_inc(var_ok, 1)

                    def evacuate(k):
                        v.wait_ge(y_mm, NS * n + k + 1)
                        v.tensor_tensor(y[:, RS * k:RS * k + RS, :], bY[k % 2][:, :].rearrange("p (r f) -> p r f", r=RS),
                                        e.b2c[:, :].unsqueeze(1).broadcast_to([P, RS, P]), ALU.add).then_inc(y_ok, 1)

                    for k in range(NS):
                        if k >= 2:
                            v.wait_ge(y_mm, NS * n + k - 1)
                        for r in range(RS):
                            i = RS * k + r
                            d = v.tensor_scalar(h[:, k % 2, r, :], hT[:, 1, :], hT[:, 0, i:i + 1], 0.0, ALU.add, ALU.max)
                        d.then_inc(h_ok, 1)
                        if k >= 1:
                            evacuate(k - 1)
                        if k >= 2:
                            variance(k - 2)
                    evacuate(NS - 1)
                    variance(NS - 2)
                    variance(NS - 1)
                    q = Steps(v, seq_c, n)
                    v.wait_ge(cf_root, n + 1)
                    q.add(v.reciprocal(cf[:, :], cf[:, :]))
                    q.wait()
                    v.wait_ge(aT_ok, n + 1)
                    v.tensor_tensor(cf[:, :], cf[:, :], aT[:, :], ALU.mult).then_inc(cf_ok, 1)
                    q = Steps(v, seq_x, 6 * n)
                    q.add(v.tensor_reduce(asum[:, :], ain[:, :], AX.X, ALU.add))
                    q.wait()
                    q.add(v.scalar_tensor_tensor(bb[:, :], e.bet[:, :], asum[:, 0:1], xin[:, :], ALU.mult, ALU.add))
                    v.wait_ge(zt_mm, n + 1)
                    q.add(v.tensor_tensor(res[:, :], bZT[:, 0:P], e.gam[:, :], ALU.mult))
                    q.wait()
                    q.add(v.tensor_tensor(res[:, :], res[:, :], bb[:, :], ALU.add))
                    q.wait()
                    q.add(v.tensor_reduce(mean[:, :], res[:, :], AX.X, ALU.add))
                    q.wait()
                    q.add(v.tensor_scalar(mean[:, :], mean[:, :], 1.0 / P, None, ALU.mult))
                    q.wait()
                    v.tensor_scalar(cur[:, n, :], res[:, :], mean[:, 0:1], None, ALU.subtract).then_inc(cen_ok, 1)
                    v.wait_ge(cen_ok, n + 1)


def layer3(nc, e):
    c = ExitStack()
    with c:
        def sb(name, shape, dt=F32):
            return c.enter_context(nc.sbuf_tensor("d_" + name, shape, dt))

        def sem(name):
            return c.enter_context(nc.semaphore("d_" + name))

        cur, ident = e.cur, e.ident
        ain = sb("ain", [P, 2, G, P])
        dg = sb("dg", [P, 2, G])
        nz = sb("nz", [P, 2, G])
        xd = sb("xd", [P, 2, G, P])
        aT = sb("aT", [P, 2, G, P])
        gT = sb("gT", [P, 2, G, P])
        res = sb("res", [P, G, P])
        mean = sb("mean", [P, G])
        junk = sb("junk", [P, P])
        a_in = [sem(f"a_in{b}") for b in range(2)]
        self_ok, sum_ok, root_ok, xd_ok, aT_mm, aT_ok, g_mm, g_ok, o_mm, res_ok, cen_ok, sq_ok, seq_f, seq_b = (
            sem(k) for k in ("self_ok", "sum_ok", "root_ok", "xd_ok", "aT_mm", "aT_ok", "g_mm", "g_ok", "o_mm",
                             "res_ok", "cen_ok", "sq_ok", "seq_f", "seq_b"))
        bA, bG, bO = e.banks[:3]

        def grp(t):
            return t[:, :].rearrange("p (g f) -> p g f", g=G)

        def pipeline(eng, front, back):
            front(0, 0)
            front(1, 1)
            back(0, 0)
            with eng.Fori(0, NG // 2 - 1) as k:
                front(2 * k + 2, 0)
                back(2 * k + 1, 1)
                front(2 * k + 3, 1)
                back(2 * k + 2, 0)
            back(NG - 1, 1)

        with nc.Block() as block:
            @block.sync
            def _(sp):
                def load(n, b):
                    sp.dma_start(ain[:, b, :, :], e.adj_v[:, bass.ds(n * G, G), :]).then_inc(a_in[b], 16)
                load(0, 0)
                load(1, 1)
                with sp.Fori(0, NG // 2 - 1) as k:
                    for b in range(2):
                        sp.wait_ge(aT_mm, 2 * k + b + 1)
                        sp.wait_ge(seq_f, 5 * (2 * k + b) + 1)
                        load(2 * k + 2 + b, b)

            @block.tensor
            def _(pe):
                def front(n, b):
                    pe.wait_ge(self_ok, n + 1)
                    if not (isinstance(n, int) and n == 0):
                        pe.wait_ge(aT_ok, n)
                    for g in range(G):
                        m = pe.transpose(bA[:, P * g:P * g + P], ain[:, b, g, :], ident[:, :])
                    m.then_inc(aT_mm, 1)
                    pe.wait_ge(aT_ok, n + 1)
                    pe.wait_ge(xd_ok, n + 1)
                    if not (isinstance(n, int) and n == 0):
                        pe.wait_ge(g_ok, n)
                    for g in range(G):
                        m = pe.matmul(bG[:, P * g:P * g + P], xd[:, b, g, :], aT[:, b, g, :], start=True, stop=True)
                    m.then_inc(g_mm, 1)

                def back(n, b):
                    pe.wait_ge(g_ok, n + 1)
                    if not (isinstance(n, int) and n == 0):
                        pe.wait_ge(res_ok, n)
                    for g in range(G):
                        m = pe.matmul(bO[:, P * g:P * g + P], gT[:, b, g, :], e.W3[:, :], start=True, stop=True)
                    m.then_inc(o_mm, 1)

                pipeline(pe, front, back)

            @block.scalar
            def _(act):
                def front(n, b):
                    act.wait_ge(sum_ok, n + 1)
                    act.activation(dg[:, b, :], dg[:, b, :], ACT.Sqrt).then_inc(root_ok, 1)
                    act.wait_ge(aT_mm, n + 1)
                    if not isinstance(n, int) or n >= 2:
                        act.wait_ge(g_mm, n - 1)
                    act.copy(aT[:, b, :, :], grp(bA)).then_inc(aT_ok, 1)
                    act.wait_ge(g_mm, n + 1)
                    if not isinstance(n, int) or n >= 2:
                        act.wait_ge(o_mm, n - 1)
                    act.copy(gT[:, b, :, :], grp(bG)).then_inc(g_ok, 1)

                def back(n, b):
                    act.wait_ge(cen_ok, n + 1)
                    for g in range(G):
                        if not (isinstance(n, int) and n == 0 and g == 0):
                            act.wait_ge(sq_ok, G * n + g)
                        act.activation(junk[:, :], cur[:, n * G + g, :], ACT.Square,
                                       accum_out=e.sqsum[:, bass.ds(n * G + g, 1)]).then_inc(sq_ok, 1)

                pipeline(act, front, back)

            @block.vector
            def _(v):
                def front(n, b):
                    q = Steps(v, seq_f, 5 * n)
                    v.wait_ge(a_in[b], 8 * (n - b) + 16)
                    v.tensor_tensor(ain[:, b, :, :], ain[:, b, :, :],
                                    ident[:, :].unsqueeze(1).broadcast_to([P, G, P]), ALU.add).then_inc(self_ok, 1)
                    v.wait_ge(self_ok, n + 1)
                    q.add(v.tensor_reduce(dg[:, b, :], ain[:, b, :, :], AX.X, ALU.add))
                    q.wait()
                    q.add(v.tensor_scalar(nz[:, b, :], dg[:, b, :], 0.0, None, ALU.is_equal))
                    q.wait()
                    v.tensor_tensor(dg[:, b, :], dg[:, b, :], nz[:, b, :], ALU.add).then_inc(sum_ok, 1)
                    v.wait_ge(root_ok, n + 1)
                    q.add(v.tensor_scalar(nz[:, b, :], nz[:, b, :], -1.0, 1.0, ALU.mult, ALU.add))
                    q.add(v.reciprocal(dg[:, b, :], dg[:, b, :]))
                    q.wait()
                    q.add(v.tensor_tensor(dg[:, b, :], dg[:, b, :], nz[:, b, :], ALU.mult))
                    q.wait()
                    if not isinstance(n, int) or n >= 2:
                        v.wait_ge(g_mm, n - 1)
                    v.tensor_tensor(xd[:, b, :, :], cur[:, bass.ds(n * G, G), :],
                                    dg[:, b, :].unsqueeze(2).broadcast_to([P, G, P]), ALU.mult).then_inc(xd_ok, 1)

                def back(n, b):
                    q = Steps(v, seq_b, 4 * n)
                    v.wait_ge(o_mm, n + 1)
                    q.add(v.tensor_tensor(res[:, :, :], grp(bO), dg[:, b, :].unsqueeze(2).broadcast_to([P, G, P]),
                                          ALU.mult))
                    q.wait()
                    v.tensor_tensor(res[:, :, :], res[:, :, :], cur[:, bass.ds(n * G, G), :], ALU.add).then_inc(res_ok, 1)
                    v.wait_ge(res_ok, n + 1)
                    q.add(v.tensor_tensor(res[:, :, :], res[:, :, :],
                                          e.bia[:, :].unsqueeze(1).broadcast_to([P, G, P]), ALU.add))
                    q.wait()
                    q.add(v.tensor_reduce(mean[:, :], res[:, :, :], AX.X, ALU.add))
                    q.wait()
                    q.add(v.tensor_scalar(mean[:, :], mean[:, :], 1.0 / P, None, ALU.mult))
                    q.wait()
                    v.tensor_tensor(cur[:, bass.ds(n * G, G), :], res[:, :, :],
                                    mean[:, :].unsqueeze(2).broadcast_to([P, G, P]), ALU.subtract).then_inc(cen_ok, 1)
                    v.wait_ge(cen_ok, n + 1)

                pipeline(v, front, back)


def normalise(nc, e, last=False):
    c = ExitStack()
    with c:
        tag = f"n{e.norms}_"
        e.norms += 1
        root_ok, rstd_ok, scaled, stored = (c.enter_context(nc.semaphore(tag + k)) for k in (
            "root_ok", "rstd_ok", "scaled", "stored"))
        with nc.Block() as block:
            @block.scalar
            def _(act):
                act.activation(e.rstd[:, :], e.sqsum[:, :], ACT.Sqrt, bias=e.eps[:, 0:1],
                               scale=1.0 / P).then_inc(root_ok, 1)

            @block.vector
            def _(v):
                v.wait_ge(root_ok, 1)
                v.reciprocal(e.rstd[:, :], e.rstd[:, :]).then_inc(rstd_ok, 1)
                v.wait_ge(rstd_ok, 1)
                with v.Fori(0, NG) as n:
                    part = e.cur[:, bass.ds(n * G, G), :]
                    v.tensor_tensor(part, part, e.rstd[:, bass.ds(n * G, G)].unsqueeze(2).broadcast_to([P, G, P]),
                                    ALU.mult).then_inc(scaled, 1)

            @block.sync
            def _(sp):
                if last:
                    with sp.Fori(0, NG) as n:
                        sp.wait_ge(scaled, n + 1)
                        sp.dma_start(e.out_v[:, bass.ds(n * G, G), :], e.cur[:, bass.ds(n * G, G), :]).then_inc(stored, 16)
                    sp.wait_ge(stored, 16 * NG)


def adjacency_stack(nc, x, adj, Wq, Wk, Wv, W_l, W_r, w_attn, W1, b1, W2, b2, gamma, beta,
                    weight, bias, out):
    ctx = ExitStack()
    with ctx:
        def sb(name, shape, dt=F32):
            return ctx.enter_context(nc.sbuf_tensor(name, shape, dt))

        def pb(name, shape, dt=F32):
            return ctx.enter_context(nc.psum_tensor(name, shape, dt))

        def sem(name):
            return ctx.enter_context(nc.semaphore(name))

        x_v = x.rearrange("b n f -> n b f")
        adj_v = adj.rearrange("b n m -> n b m")
        out_v = out.rearrange("b n f -> n b f")

        cur = sb("cur", [P, B, P])
        sqsum = sb("sqsum", [P, B])
        rstd = sb("rstd", [P, B])
        eps = sb("eps", [P, 1])
        ident = sb("ident", [P, P])
        M = sb("M", [P, P])
        WvT = sb("WvT", [P, P])
        WlT = sb("WlT", [P, P])
        WrT = sb("WrT", [P, P])
        W1s = sb("W1s", [P, 2, P])
        W2c = sb("W2c", [P, P])
        b2c = sb("b2c", [P, P])
        b1c = sb("b1c", [P, 1])
        gam = sb("gam", [P, P])
        bet = sb("bet", [P, P])
        W3 = sb("W3", [P, P])
        bia = sb("bia", [P, P])
        Wpad = sb("Wpad", [P, 2 * P - HEADS])
        Rep = sb("Rep", [P, P, HEADS])
        RepT = sb("RepT", [P, NRT, P])
        diag = sb("diag", [P, P])

        banks = [pb(f"bank{i}", [P, 512]) for i in range(8)]

        with ExitStack() as c0:
            raw = c0.enter_context(nc.sbuf_tensor("raw", [P, 5, P], F32))
            b2r = c0.enter_context(nc.sbuf_tensor("b2r", [P, P], F32))
            wcol = c0.enter_context(nc.sbuf_tensor("wcol", [P, 1], F32))
            rmean = c0.enter_context(nc.sbuf_tensor("rmean", [P, 2], F32))
            hsel = c0.enter_context(nc.sbuf_tensor("hsel", [P, HEADS], F32))
            hselT = c0.enter_context(nc.sbuf_tensor("hselT", [HEADS, P], F32))
            rep8 = c0.enter_context(nc.sbuf_tensor("rep8", [HEADS, P], F32))
            weights_in = sem("weights_in")
            made = sem("made")
            masks = sem("masks")
            w_ready = sem("w_ready")
            w_seq = sem("w_seq")
            with nc.Block() as block:
                @block.sync
                def _(sp):
                    for k, w in enumerate((Wq, Wk, Wv, W_l, W_r)):
                        sp.dma_start(raw[:, k, :], w).then_inc(weights_in, 16)
                    sp.dma_start(W1s[:, :, :], W1.rearrange("(a h) k -> h a k", a=2)).then_inc(weights_in, 16)
                    sp.dma_start(W2c[:, :], W2).then_inc(weights_in, 16)
                    sp.dma_start(W3[:, :], weight).then_inc(weights_in, 16)
                    for dst, v in ((b2r, b2), (gam, gamma), (bet, beta), (bia, bias)):
                        sp.dma_start(dst[:, :], v.partition_broadcast(P)).then_inc(weights_in, 16)
                    sp.dma_start(b1c[:, :], b1.rearrange("(k a) -> k a", a=1)).then_inc(weights_in, 16)
                    for h in range(HEADS):
                        sp.dma_start(wcol[HF * h:HF * (h + 1), :],
                                     w_attn.rearrange("(f a) -> f a", a=1)).then_inc(weights_in, 16)

                NW = 16 * (13 + HEADS)

                @block.gpsimd
                def _(pool):
                    n = 0
                    for t, v in ((ident, 0.0), (eps, EPS), (Wpad, 0.0)):
                        pool.memset(t[:, :], v).then_inc(masks, 1)
                    pool.memset(hsel[:, :], 1.0).then_inc(masks, 1)
                    pool.memset(Rep[:, :, :], 0.0).then_inc(masks, 1)
                    pool.memset(RepT[:, :, :], 1.0).then_inc(masks, 1)
                    pool.memset(diag[:, :], 1.0).then_inc(masks, 1)
                    pool.wait_ge(masks, 7)
                    pool.affine_select(out=ident[:, :], in_=ident[:, :], compare_op=ALU.not_equal, fill=1.0,
                                       base=0, pattern=[[-1, P]], channel_multiplier=1).then_inc(masks, 1)
                    pool.affine_select(out=Rep[:, :, :], in_=Rep[:, :, :], compare_op=ALU.not_equal, fill=1.0,
                                       base=0, pattern=[[-1, P], [0, HEADS]], channel_multiplier=1).then_inc(masks, 1)
                    pool.affine_select(out=RepT[:, :, :], in_=RepT[:, :, :], compare_op=ALU.is_ge, fill=0.0,
                                       base=0, pattern=[[P, NRT], [-HEADS, P]], channel_multiplier=1).then_inc(masks, 1)
                    pool.wait_ge(masks, 10)
                    pool.affine_select(out=RepT[:, :, :], in_=RepT[:, :, :], compare_op=ALU.is_ge, fill=0.0,
                                       base=HEADS - 1, pattern=[[-P, NRT], [HEADS, P]], channel_multiplier=-1).then_inc(masks, 1)
                    pool.affine_select(out=hsel[:, :], in_=hsel[:, :], compare_op=ALU.is_ge, fill=0.0,
                                       base=0, pattern=[[-HF, HEADS]], channel_multiplier=1).then_inc(masks, 1)
                    pool.wait_ge(masks, 12)
                    pool.affine_select(out=hsel[:, :], in_=hsel[:, :], compare_op=ALU.is_ge, fill=0.0,
                                       base=HF - 1, pattern=[[HF, HEADS]], channel_multiplier=-1).then_inc(masks, 1)

                @block.tensor
                def _(pe):
                    pe.wait_ge(weights_in, NW)
                    pe.wait_ge(masks, 13)
                    pe.matmul(banks[0][:, 0:P], raw[:, 0, :], raw[:, 1, :], start=True, stop=True)
                    pe.transpose(banks[0][:, P:2 * P], raw[:, 2, :], ident[:, :])
                    pe.transpose(banks[0][:, 2 * P:3 * P], raw[:, 3, :], ident[:, :])
                    pe.transpose(banks[0][:, 3 * P:4 * P], raw[:, 4, :], ident[:, :])
                    pe.transpose(banks[1][0:HEADS, 0:P], hsel[:, :], ident[:, :]).then_inc(w_ready, 1)
                    pe.wait_ge(made, 2)
                    pe.matmul(banks[2][:, 0:P],
                              rep8[:, :],
                              hselT[0:HEADS, :], start=True, stop=True).then_inc(w_ready, 1)

                @block.vector
                def _(v):
                    v.wait_ge(w_ready, 1)
                    v.tensor_copy(rep8[:, :].rearrange("k (r h) -> k r h", h=HEADS),
                                  ident[0:HEADS, 0:HEADS].unsqueeze(1).broadcast_to([HEADS, RT, HEADS])).then_inc(made, 1)
                    v.tensor_copy(hselT[0:HEADS, :], banks[1][0:HEADS, 0:P]).then_inc(made, 1)
                    v.tensor_scalar(M[:, :], banks[0][:, 0:P], float(P) ** -0.5, None, ALU.mult)
                    v.tensor_copy(WvT[:, :], banks[0][:, P:2 * P])
                    v.tensor_copy(WlT[:, :], banks[0][:, 2 * P:3 * P])
                    v.tensor_copy(WrT[:, :], banks[0][:, 3 * P:4 * P])
                    v.wait_ge(masks, 13)
                    v.wait_ge(weights_in, NW)
                    v.tensor_scalar(Wpad[:, P - HEADS:P], hsel[:, :], wcol[:, 0:1], None, ALU.mult)
                    v.tensor_reduce(rmean[:, 0:1], W2c[:, :], AX.X, ALU.add).then_inc(w_seq, 1)
                    v.tensor_reduce(rmean[:, 1:2], b2r[:, :], AX.X, ALU.add).then_inc(w_seq, 1)
                    v.wait_ge(w_seq, 2)
                    v.tensor_scalar(rmean[:, :], rmean[:, :], -1.0 / P, None, ALU.mult).then_inc(w_seq, 1)
                    v.wait_ge(w_seq, 3)
                    v.tensor_scalar(W2c[:, :], W2c[:, :], rmean[:, 0:1], None, ALU.add)
                    v.tensor_scalar(b2c[:, :], b2r[:, :], rmean[:, 1:2], None, ALU.add)
                    v.wait_ge(w_ready, 2)
                    v.tensor_copy(diag[:, :], banks[2][:, 0:P])


        e = Shared()
        e.cur = cur
        e.sqsum = sqsum
        e.rstd = rstd
        e.eps = eps
        e.ident = ident
        e.M = M
        e.WvT = WvT
        e.WlT = WlT
        e.WrT = WrT
        e.W1s = W1s
        e.W2c = W2c
        e.b2c = b2c
        e.b1c = b1c
        e.gam = gam
        e.bet = bet
        e.W3 = W3
        e.bia = bia
        e.Wpad = Wpad
        e.Rep = Rep
        e.RepT = RepT
        e.diag = diag
        e.banks = banks
        e.x_v = x_v
        e.adj_v = adj_v
        e.out_v = out_v
        e.norms = 0
        for k in range(4):
            LAYERS[k](nc, e)
            normalise(nc, e, last=(k == 3))


LAYERS = [layer0, layer1_dense, layer2_dense, layer3]

_INS = ['x', 'adj', 'L0_gnn_Wq', 'L0_gnn_Wk', 'L0_gnn_Wv', 'L1_gnn_W_l', 'L1_gnn_W_r', 'L1_gnn_w_attn',
        'L2_gnn_W1', 'L2_gnn_b1', 'L2_gnn_W2', 'L2_gnn_b2', 'L2_gnn_gamma', 'L2_gnn_beta',
        'L3_gnn_weight', 'L3_gnn_bias']
_OUTS = [((B, P, P), 'float32')]


def kernel(**inputs):
    import numpy as _np
    import concourse.bacc as _bacc
    from concourse import mybir as _mybir
    from concourse.bass_utils import run_bass_kernel_spmd as _run

    nc = _bacc.Bacc("TRN2", target_bir_lowering=False, num_devices=1)
    arrays, args = {}, []
    for name in _INS:
        a = _np.ascontiguousarray(inputs[name])
        arrays[f"in_{name}_dram"] = a
        args.append(nc.dram_tensor(f"in_{name}_dram", a.shape, _mybir.dt.from_np(a.dtype), kind="ExternalInput").ap())
    for i, (shape, dtype) in enumerate(_OUTS):
        dt = _mybir.dt.from_np(_np.dtype(dtype))
        args.append(nc.dram_tensor(f"out_{i}_dram", shape, dt, kind="ExternalOutput").ap())
    adjacency_stack(nc, *args)
    r = _run(nc, [arrays], core_ids=[0])
    got = tuple(r.results[0][f"out_{i}_dram"] for i in range(len(_OUTS)))
    return got[0]
```

```python
from contextlib import ExitStack

import concourse.bass as bass
from concourse import mybir

F32 = mybir.dt.float32
ALU = mybir.AluOpType
ACT = mybir.ActivationFunctionType
AX = mybir.AxisListType

P = 128
B = 64
HEADS = 8
HF = P // HEADS
SLOPE = 0.2
EPS = 1e-5
NEG = -1e30
G = 4
NG = B // G
RT = P // HEADS
NRT = P // RT
RS = 4
TILES = 10
ECAP = TILES * P
CHUNK = 512
CHUNKS = -(-ECAP // CHUNK)
Q = 4
MARK = 2.0 ** 100
LOWEST = -1e35
F32R = mybir.dt.float32r
BF16 = mybir.dt.bfloat16
I32 = mybir.dt.int32



class Shared:
    pass


class Steps:

    def __init__(self, eng, sem, base=0):
        self.eng, self.sem, self.base, self.n = eng, sem, base, 0

    def add(self, instruction):
        instruction.then_inc(self.sem, 1)
        self.n += 1

    def wait(self):
        self.eng.wait_ge(self.sem, self.base + self.n)


def layer0(nc, e):
    c = ExitStack()
    with c:
        def sb(name, shape, dt=F32):
            return c.enter_context(nc.sbuf_tensor("a_" + name, shape, dt))

        def sem(name):
            return c.enter_context(nc.semaphore("a_" + name))

        cur, ident = e.cur, e.ident
        xin = sb("xin", [P, 2, G, P])
        ain = sb("ain", [P, 2, G, P])
        xT = sb("xT", [P, 2, G, P])
        tT = sb("tT", [P, 2, G, P])
        xv = sb("xv", [P, 2, G, P])
        drop = sb("drop", [P, G, P])
        edge = sb("edge", [P, G, P])
        odd = sb("odd", [P, G, P])
        sm = sb("sm", [P, 2, G, P])
        top = sb("top", [P, 2, G])
        ex = sb("ex", [P, 2, G, P])
        den = sb("den", [P, 2, G])
        rden = sb("rden", [P, G])
        pr = sb("pr", [P, 2, G, P])
        prT = sb("prT", [P, 2, G, P])
        res = sb("res", [P, G, P])
        mean = sb("mean", [P, G])
        junk = sb("junk", [P, P])
        x_in = [sem(f"x_in{b}") for b in range(2)]
        xT_mm, xT_ok, t_mm, t_ok, xv_mm, xv_ok, s_mm = (sem(k) for k in (
            "xT_mm", "xT_ok", "t_mm", "t_ok", "xv_mm", "xv_ok", "s_mm"))
        top_ok, ex_ok, pr_ok, prT_mm, prT_ok, o_mm, cen_ok, sq_ok = (sem(k) for k in (
            "top_ok", "ex_ok", "pr_ok", "prT_mm", "prT_ok", "o_mm", "cen_ok", "sq_ok"))
        res_ok, seq_f, seq_b = sem("res_ok"), sem("seq_f"), sem("seq_b")
        bX, bT, bV, bS, bP, bO = e.banks[:6]

        def grp(t):
            return t[:, :].rearrange("p (g f) -> p g f", g=G)

        def pipeline(eng, front, back):
            front(0, 0)
            front(1, 1)
            back(0, 0)
            with eng.Fori(0, NG // 2 - 1) as k:
                front(2 * k + 2, 0)
                back(2 * k + 1, 1)
                front(2 * k + 3, 1)
                back(2 * k + 2, 0)
            back(NG - 1, 1)

        with nc.Block() as block:
            @block.sync
            def _(sp):
                def load(n, b):
                    sp.dma_start(xin[:, b, :, :], e.x_v[:, bass.ds(n * G, G), :]).then_inc(x_in[b], 16)
                    sp.dma_start(ain[:, b, :, :], e.adj_v[:, bass.ds(n * G, G), :]).then_inc(x_in[b], 16)
                load(0, 0)
                load(1, 1)
                with sp.Fori(0, NG // 2 - 1) as k:
                    for b in range(2):
                        sp.wait_ge(res_ok, 2 * k + b + 1)
                        load(2 * k + 2 + b, b)

            @block.tensor
            def _(pe):
                def front(n, b):
                    pe.wait_ge(x_in[b], 16 * (n - b) + 32)
                    if not (isinstance(n, int) and n == 0):
                        pe.wait_ge(xT_ok, n)
                    for g in range(G):
                        m = pe.transpose(bX[:, P * g:P * g + P], xin[:, b, g, :], ident[:, :])
                    m.then_inc(xT_mm, 1)
                    pe.wait_ge(xT_ok, n + 1)
                    if not (isinstance(n, int) and n == 0):
                        pe.wait_ge(t_ok, n)
                        pe.wait_ge(xv_ok, n)
                    pe.matmul(bT[:, :], e.M[:, :], xT[:, b, :, :], start=True, stop=True).then_inc(t_mm, 1)
                    for g in range(G):
                        m = pe.matmul(bV[:, P * g:P * g + P], xT[:, b, g, :], e.WvT[:, :], start=True, stop=True)
                    m.then_inc(xv_mm, 1)
                    pe.wait_ge(t_ok, n + 1)
                    if not (isinstance(n, int) and n == 0):
                        pe.wait_ge(top_ok, n)
                    for g in range(G):
                        m = pe.matmul(bS[:, P * g:P * g + P], tT[:, b, g, :], xT[:, b, g, :], start=True, stop=True)
                    m.then_inc(s_mm, 1)

                def back(n, b):
                    pe.wait_ge(pr_ok, n + 1)
                    if not (isinstance(n, int) and n == 0):
                        pe.wait_ge(prT_ok, n)
                    for g in range(G):
                        m = pe.transpose(bP[:, P * g:P * g + P], pr[:, b, g, :], ident[:, :])
                    m.then_inc(prT_mm, 1)
                    pe.wait_ge(prT_ok, n + 1)
                    pe.wait_ge(xv_ok, n + 1)
                    if not (isinstance(n, int) and n == 0):
                        pe.wait_ge(res_ok, n)
                    for g in range(G):
                        m = pe.matmul(bO[:, P * g:P * g + P], prT[:, b, g, :], xv[:, b, g, :], start=True, stop=True)
                    m.then_inc(o_mm, 1)

                pipeline(pe, front, back)

            @block.scalar
            def _(act):
                def front(n, b):
                    act.wait_ge(xT_mm, n + 1)
                    if not isinstance(n, int) or n >= 2:
                        act.wait_ge(s_mm, n - 1)
                    act.copy(xT[:, b, :, :], grp(bX)).then_inc(xT_ok, 1)
                    act.wait_ge(xv_mm, n + 1)
                    if not isinstance(n, int) or n >= 2:
                        act.wait_ge(o_mm, n - 1)
                    act.copy(xv[:, b, :, :], grp(bV)).then_inc(xv_ok, 1)
                    act.wait_ge(top_ok, n + 1)
                    if not isinstance(n, int) or n >= 2:
                        act.wait_ge(pr_ok, n - 1)
                    for g in range(G):
                        act.activation(ex[:, b, g, :], sm[:, b, g, :], ACT.Exp, bias=top[:, b, g:g + 1],
                                       accum_out=den[:, b, g:g + 1]).then_inc(ex_ok, 1)

                def back(n, b):
                    act.wait_ge(prT_mm, n + 1)
                    act.copy(prT[:, b, :, :], grp(bP)).then_inc(prT_ok, 1)
                    act.wait_ge(cen_ok, n + 1)
                    for g in range(G):
                        if isinstance(n, int) and n == 0 and g == 0:
                            pass
                        else:
                            act.wait_ge(sq_ok, G * n + g)
                        act.activation(junk[:, :], cur[:, n * G + g, :], ACT.Square,
                                       accum_out=e.sqsum[:, bass.ds(n * G + g, 1)]).then_inc(sq_ok, 1)

                pipeline(act, front, back)

            @block.vector
            def _(v):
                def front(n, b):
                    v.wait_ge(x_in[b], 16 * (n - b) + 32)
                    q = Steps(v, seq_f, 6 * n)
                    v.wait_ge(t_mm, n + 1)
                    if not isinstance(n, int) or n >= 2:
                        v.wait_ge(s_mm, n - 1)
                    v.tensor_copy(tT[:, b, :, :], grp(bT)).then_inc(t_ok, 1)
                    q.add(v.tensor_scalar(drop[:, :, :], ain[:, b, :, :], 0.0, NEG, ALU.is_equal, ALU.mult))
                    v.wait_ge(s_mm, n + 1)
                    q.wait()
                    if not isinstance(n, int) or n >= 2:
                        v.wait_ge(ex_ok, G * (n - 1))
                    q.add(v.tensor_tensor(sm[:, b, :, :], grp(bS), drop[:, :, :], ALU.add))
                    q.wait()
                    v.tensor_reduce(top[:, b, :], sm[:, b, :, :], AX.X, ALU.max, negate=True).then_inc(top_ok, 1)
                    q.add(v.tensor_scalar(edge[:, :, :], ain[:, b, :, :], 0.0, None, ALU.not_equal))
                    q.wait()
                    q.add(v.tensor_tensor(odd[:, :, :], edge[:, :, :], ain[:, b, :, :], ALU.not_equal))
                    q.add(v.tensor_reduce(e.deg[:, 0, bass.ds(n * G, G)], edge[:, :, :], AX.X, ALU.add))
                    q.wait()
                    q.add(v.tensor_reduce(e.deg[:, 1, bass.ds(n * G, G)], odd[:, :, :], AX.X, ALU.add))

                def back(n, b):
                    q = Steps(v, seq_b, 3 * n)
                    v.wait_ge(ex_ok, G * (n + 1))
                    if not isinstance(n, int) or n >= 2:
                        v.wait_ge(prT_mm, n - 1)
                    q.add(v.reciprocal(rden[:, :], den[:, b, :]))
                    q.wait()
                    for g in range(G):
                        m = v.scalar_tensor_tensor(pr[:, b, g, :], ex[:, b, g, :], rden[:, g:g + 1], ain[:, b, g, :],
                                                   ALU.mult, ALU.add)
                    m.then_inc(pr_ok, 1)
                    v.wait_ge(o_mm, n + 1)
                    v.tensor_tensor(res[:, :, :], grp(bO), xin[:, b, :, :], ALU.add).then_inc(res_ok, 1)
                    v.wait_ge(res_ok, n + 1)
                    q.add(v.tensor_reduce(mean[:, :], res[:, :, :], AX.X, ALU.add))
                    q.wait()
                    q.add(v.tensor_scalar(mean[:, :], mean[:, :], 1.0 / P, None, ALU.mult))
                    q.wait()
                    v.tensor_tensor(cur[:, bass.ds(n * G, G), :], res[:, :, :],
                                    mean[:, :].unsqueeze(2).broadcast_to([P, G, P]), ALU.subtract).then_inc(cen_ok, 1)
                    v.wait_ge(cen_ok, n + 1)

                pipeline(v, front, back)


def prepare(nc, e):
    c = ExitStack()
    with c:
        def sem(name):
            return c.enter_context(nc.semaphore("p_" + name))

        below = c.enter_context(nc.sbuf_tensor("p_below", [P, P], F32))
        ones = c.enter_context(nc.sbuf_tensor("p_ones", [P, P], F32))
        worst = c.enter_context(nc.sbuf_tensor("p_worst", [P, 2], F32))
        mask_ok, sum_mm, seq = sem("mask_ok"), sem("sum_mm"), sem("seq")
        bank = e.banks[0]
        with nc.Block() as block:
            @block.gpsimd
            def _(pool):
                pool.memset(ones[:, :], 1.0).then_inc(mask_ok, 1)
                pool.memset(below[:, :], 1.0).then_inc(mask_ok, 1)
                pool.wait_ge(mask_ok, 2)
                pool.affine_select(out=below[:, :], in_=below[:, :], compare_op=ALU.is_gt, fill=0.0,
                                   base=0, pattern=[[1, P]], channel_multiplier=-1).then_inc(mask_ok, 1)

            @block.tensor
            def _(pe):
                pe.wait_ge(mask_ok, 3)
                pe.matmul(bank[:, 0:B], below[:, :], e.deg[:, 0, :], start=True, stop=True)
                pe.matmul(bank[:, P:P + 2 * B], ones[:, :], e.deg[:, :, :], start=True, stop=True).then_inc(sum_mm, 1)

            @block.vector
            def _(v):
                q = Steps(v, seq)
                v.wait_ge(sum_mm, 1)
                q.add(v.tensor_copy(e.first[:, :], bank[:, 0:B]))
                q.add(v.tensor_reduce(worst[:, 0:1], bank[:, P:P + B], AX.X, ALU.max))
                q.add(v.tensor_reduce(worst[:, 1:2], bank[:, P + B:P + 2 * B], AX.X, ALU.max))
                q.wait()
                q.add(v.tensor_tensor(e.end[:, :], e.first[:, :], e.deg[:, 0, :], ALU.add))
                q.add(v.tensor_scalar(worst[:, 0:1], worst[:, 0:1], float(ECAP), None, ALU.is_gt))
                q.add(v.tensor_scalar(worst[:, 1:2], worst[:, 1:2], 0.0, None, ALU.is_gt))
                q.wait()
                q.add(v.tensor_tensor(e.general[:, :], worst[:, 0:1], worst[:, 1:2], ALU.max))
                q.wait()


class Packed:
    pass


def packed_buffers(nc, c, tag, slots):
    s = Packed()

    def sb(name, shape, dt=F32):
        return c.enter_context(nc.sbuf_tensor(tag + name, shape, dt))

    def sem(name):
        return c.enter_context(nc.semaphore(tag + name))

    s.slots = slots
    s.ain = sb("ain", [P, 2, P])
    s.number = sb("number", [P, P])
    s.C = sb("C", [P, 2, P], F32R)
    s.after = sb("after", [P, ECAP])
    s.SI = sb("SI", [P, 2, ECAP], F32R)
    s.SJ = sb("SJ", [P, slots, ECAP], F32R)
    s.SIT = sb("SIT", [P, slots, TILES, P])
    s.xin = sb("xin", [P, 2, P])
    s.xT = sb("xT", [P, P])
    s.hi = sb("hi", [P, 2, 2 * P], F32R)
    s.lo = sb("lo", [P, 2, 2 * P], F32R)
    s.junk = sb("junk", [P, P])
    s.mean = sb("mean", [P, Q])
    s.res = sb("res", [P, Q, P])
    s.a_in = [sem(f"a_in{b}") for b in range(2)]
    s.x_ok = sem("x_ok")
    s.seq_p = sem("seq_p")
    s.c_ok = sem("c_ok")
    s.si_ok = sem("si_ok")
    s.c_mm = sem("c_mm")
    s.sj_ok = sem("sj_ok")
    s.s_mm = sem("s_mm")
    s.sit_ok = sem("sit_ok")
    s.xT_mm = sem("xT_mm")
    s.xT_ok = sem("xT_ok")
    s.p_mm = sem("p_mm")
    s.hi_ok = sem("hi_ok")
    s.lo_ok = sem("lo_ok")
    s.u_mm = sem("u_mm")
    s.cen_ok = sem("cen_ok")
    s.sq_ok = sem("sq_ok")
    return s


def chunk(k):
    return slice(CHUNK * k, min(CHUNK * (k + 1), ECAP))


def width(k):
    return chunk(k).stop - chunk(k).start


def tiles(k):
    return range(4 * k, min(4 * k + 4, TILES))


def every_step(eng, step, extra):
    for pos in range(8):
        step(0, pos, False)
    with eng.Fori(1, B // 8 - 1) as K:
        for pos in range(8):
            step(K, pos, True)
    for n in range(B - 8, B + extra):
        step(n // 8, n % 8, False)


def load_adjacency(sp, e, s):
    for n in range(2):
        sp.dma_start(s.ain[:, n, :], e.adj_v[:, n, :]).then_inc(s.a_in[n], 16)
    with sp.Fori(1, B // 2) as k:
        for b in range(2):
            sp.wait_ge(s.c_ok, 2 * k + b - 1)
            sp.dma_start(s.ain[:, b, :], e.adj_v[:, 2 * k + b, :]).then_inc(s.a_in[b], 16)


def normalise_x(act, e, s, K, pos, late):
    n = 8 * K + pos
    if late:
        act.wait_ge(s.xT_mm, n - 1)
    act.activation(s.xin[:, pos % 2, :], e.cur[:, bass.ds(n, 1), :].rearrange("p a f -> p (a f)"), ACT.Copy,
                   scale=e.rstd[:, bass.ds(n, 1)]).then_inc(s.x_ok, 1)


def prepare_edges(v, e, s, K, pos, late, si_users):
    n, b = 8 * K + pos, pos % 2
    q = Steps(v, s.seq_p, 2 * n)
    first, end = e.first[:, bass.ds(n, 1)], e.end[:, bass.ds(n, 1)]
    v.wait_ge(s.a_in[b], 16 * (4 * K + pos // 2) + 16)
    q.add(v.tensor_tensor_scan(s.number[:, :], e.ones[:, :], s.ain[:, b, :], first, ALU.mult, ALU.add))
    if late:
        v.wait_ge(s.c_mm, 3 * n - 3)
    q.wait()
    v.tensor_tensor(s.C[:, b, :], s.number[:, :], s.ain[:, b, :], ALU.mult).then_inc(s.c_ok, 1)
    q.add(v.tensor_scalar(s.after[:, :], e.number1[:, :], first, None, ALU.is_gt))
    if late:
        for sem in si_users:
            v.wait_ge(sem, 3 * n - 3)
    q.wait()
    v.scalar_tensor_tensor(s.SI[:, b, :], e.number1[:, :], end, s.after[:, :], ALU.is_le, ALU.mult).then_inc(s.si_ok, 1)


def split_low(v, s, ring, K, pos, late, hi_count):
    n = 8 * K + pos
    v.wait_ge(s.hi_ok, hi_count * n + hi_count)
    if late:
        v.wait_ge(s.u_mm, 3 * n - 3)
    v.tensor_tensor(s.lo[:, pos % 2, :], ring[1][:, 0:2 * P], s.hi[:, pos % 2, :].bitcast(F32),
                    ALU.subtract).then_inc(s.lo_ok, 1)


def number_edges(v, e, s, ring, K, pos):
    n = 8 * K + pos
    for k in range(CHUNKS):
        v.wait_ge(s.c_mm, 3 * n + k + 1)
        v.tensor_tensor(s.SJ[:, pos % s.slots, chunk(k)], ring[k][:, 0:width(k)], e.number1[:, chunk(k)],
                        ALU.is_equal).then_inc(s.sj_ok, 1)


def number_columns(pe, s, bank, pos, k):
    pe.matmul(bank[:, 0:width(k)], s.C[:, pos % 2, :], s.SI[:, pos % 2, chunk(k)], start=True, stop=True).then_inc(s.c_mm, 1)


def transpose_rows(pe, e, s, bank, pos, k):
    for j in tiles(k):
        m = pe.transpose(bank[:, P * (j - 4 * k):P * (j - 4 * k) + P], s.SI[:, pos % 2, P * j:P * j + P].bitcast(F32),
                         e.ident[:, :])
    m.then_inc(s.s_mm, 1)


def evacuate_rows(act, s, ring, K, pos):
    n = 8 * K + pos
    for k in range(CHUNKS):
        act.wait_ge(s.s_mm, 3 * n + k + 1)
        act.copy(s.SIT[:, pos % s.slots, tiles(k).start:tiles(k).stop, :],
                 ring[k][:, 0:width(k)].rearrange("p (j i) -> p j i", i=P)).then_inc(s.sit_ok, 1)


def gather_pairs(pe, s, bank, pos, k):
    w, cs, b = width(k), chunk(k), pos % 2
    pe.matmul(bank[:, 0:w], s.hi[:, b, 0:P], s.SJ[:, pos % s.slots, cs], start=True, stop=False)
    pe.matmul(bank[:, 0:w], s.lo[:, b, 0:P], s.SJ[:, pos % s.slots, cs], start=False, stop=False)
    pe.matmul(bank[:, 0:w], s.hi[:, b, P:2 * P], s.SI[:, b, cs], start=False, stop=False)
    pe.matmul(bank[:, 0:w], s.lo[:, b, P:2 * P], s.SI[:, b, cs], start=False, stop=True).then_inc(s.u_mm, 1)


def residual(v, e, s, z, i):
    part = e.cur[:, bass.ds(Q * i, Q), :]
    z.add(v.tensor_tensor(part, part, e.rstd[:, bass.ds(Q * i, Q)].unsqueeze(2).broadcast_to([P, Q, P]), ALU.mult))
    z.wait()
    z.add(v.tensor_tensor(s.res[:, :, :], s.res[:, :, :], part, ALU.add))
    z.wait()


def centre(v, e, s, z, i):
    z.add(v.tensor_reduce(s.mean[:, :], s.res[:, :, :], AX.X, ALU.add))
    z.wait()
    z.add(v.tensor_scalar(s.mean[:, :], s.mean[:, :], 1.0 / P, None, ALU.mult))
    z.wait()
    v.tensor_tensor(e.cur[:, bass.ds(Q * i, Q), :], s.res[:, :, :], s.mean[:, :].unsqueeze(2).broadcast_to([P, Q, P]),
                    ALU.subtract).then_inc(s.cen_ok, 1)


def squares(act, e, s, i):
    act.wait_ge(s.cen_ok, i + 1)
    for q in range(Q):
        act.wait_ge(s.sq_ok, Q * i + q + 1)
        act.activation(s.junk[:, :], e.cur[:, Q * i + q, :], ACT.Square,
                       accum_out=e.sqsum[:, bass.ds(Q * i + q, 1)]).then_inc(s.sq_ok, 1)


def layer1_packed(nc, e):
    c = ExitStack()
    with c:
        def sb(name, shape, dt=F32):
            return c.enter_context(nc.sbuf_tensor("b_" + name, shape, dt))

        def sem(name):
            return c.enter_context(nc.semaphore("b_" + name))

        LAG = 5
        W = P + HEADS
        H = Q * HEADS
        s = packed_buffers(nc, c, "b_", 8)
        grs = sb("grs", [P, 8, P])
        t = sb("t", [P, 2, CHUNK])
        vv = sb("vv", [P, 2, CHUNK])
        es = sb("es", [2 * H, ECAP])
        mark = sb("mark", [H, ECAP + 1])
        run = sb("run", [H, ECAP])
        top = sb("top", [H, ECAP])
        aT = sb("aT", [P, 2, TILES, H])
        wt = sb("wt", [P, 2, TILES, W])
        os = sb("os", [P, Q, W])
        rden = sb("rden", [P, Q, HEADS])
        t_ok = sem("t_ok")
        v_ok = sem("v_ok")
        e_mm = sem("e_mm")
        es_ok = sem("es_ok")
        pad_ok = sem("pad_ok")
        seq_z = sem("seq_z")
        z_ok = sem("z_ok")
        ex_ok = sem("ex_ok")
        at_mm = sem("at_mm")
        at_ok = sem("at_ok")
        g_mm = sem("g_mm")
        w_ok = sem("w_ok")
        wa_ok = sem("wa_ok")
        o_mm = sem("o_mm")
        os_ok = sem("os_ok")
        seq_c = sem("seq_c")
        ring = e.banks[0:3]
        bU = e.banks[3:5]
        bE = e.wide

        def scored(n, inner):
            return inner or n < B

        def prepared(n, inner):
            return inner or n + 1 < B

        def summed(n, inner):
            return inner or LAG <= n < B + LAG

        def softened(n, pos, inner):
            return pos % Q == 0 and (inner or Q <= n <= B)

        def finished(n, pos, inner):
            return pos % Q == 1 and (inner or n >= Q + LAG)

        def batches(K, pos):
            return 8 // Q * K + pos // Q

        def softmaxes(K, pos):
            return 8 // Q * K + (pos - LAG) // Q + 1

        def parity(pos):
            return ((pos - LAG) // Q) % 2

        with nc.Block() as block:
            @block.sync
            def _(sp):
                load_adjacency(sp, e, s)

            @block.gpsimd
            def _(pool):
                pool.memset(s.junk[:, :], 0.0).then_inc(s.sq_ok, 1)
                pool.memset(mark[:, 0:1], 0.0).then_inc(pad_ok, 1)
                pool.memset(mark[:, ECAP:ECAP + 1], 0.0).then_inc(pad_ok, 1)

            @block.tensor
            def _(pe):
                pe.wait_ge(s.x_ok, 1)
                pe.transpose(ring[0][:, 0:P], s.xin[:, 0, :], e.ident[:, :]).then_inc(s.xT_mm, 1)
                pe.wait_ge(s.xT_ok, 1)
                pe.matmul(ring[1][:, 0:2 * P], s.xT[:, :], e.WlrT[:, :, :], start=True, stop=True).then_inc(s.p_mm, 1)

                def step(K, pos, inner):
                    n = 8 * K + pos
                    m, ms = n - LAG, (pos - LAG) % 8
                    A, N, S = scored(n, inner), prepared(n, inner), summed(n, inner)
                    if A:
                        pe.wait_ge(s.c_ok, n + 1)
                        pe.wait_ge(s.si_ok, n + 1)
                        pe.wait_ge(s.xT_ok, n + 1)
                        if inner or n > LAG:
                            pe.wait_ge(w_ok, 3 * m)
                        number_columns(pe, s, ring[0], pos, 0)
                        pe.wait_ge(s.lo_ok, n + 1)
                        number_columns(pe, s, ring[1], pos, 1)
                        if inner or n > LAG:
                            pe.wait_ge(os_ok, m)
                        elif n > 0:
                            pe.wait_ge(s.sit_ok, 3 * n)
                        number_columns(pe, s, ring[2], pos, 2)
                        for k in range(CHUNKS):
                            pe.wait_ge(s.sj_ok, 3 * n + k + 1)
                            transpose_rows(pe, e, s, ring[k], pos, k)
                    if N:
                        pe.wait_ge(s.x_ok, n + 2)
                        pe.wait_ge(s.sit_ok, 3 * n + 1)
                        pe.transpose(ring[0][:, 0:P], s.xin[:, (pos + 1) % 2, :], e.ident[:, :]).then_inc(s.xT_mm, 1)
                    if S:
                        if A:
                            pe.wait_ge(s.sit_ok, 3 * n + 3)
                        if inner or n > LAG:
                            pe.wait_ge(w_ok, 3 * m)
                            pe.wait_ge(os_ok, m)
                        for k in range(CHUNKS):
                            if N and k == 2:
                                pe.wait_ge(s.xT_ok, n + 2)
                            for j in tiles(k):
                                d = pe.matmul(ring[(k + 1) % 3][:, P * (j - 4 * k):P * (j - 4 * k) + P],
                                              s.SJ[:, ms, P * j:P * j + P].bitcast(F32), grs[:, ms, :], start=True, stop=True)
                            d.then_inc(g_mm, 1)
                    if N:
                        pe.wait_ge(s.xT_ok, n + 2)
                        if S:
                            pe.wait_ge(w_ok, 3 * m + 1)
                        else:
                            pe.wait_ge(s.sit_ok, 3 * n + 2)
                        pe.matmul(ring[1][:, 0:2 * P], s.xT[:, :], e.WlrT[:, :, :], start=True, stop=True).then_inc(s.p_mm, 1)

                    def gather(k):
                        if inner or 3 * n + k >= 2:
                            pe.wait_ge(v_ok, 3 * n + k - 1)
                        gather_pairs(pe, s, bU[(pos + k) % 2], pos, k)

                    def score(k):
                        pe.wait_ge(v_ok, 3 * n + k + 1)
                        out = bE[0:2 * H, chunk(k)]
                        pe.matmul(out, e.put_w[:, pos % Q, :], vv[:, (pos + k) % 2, 0:width(k)], start=(pos % Q == 0), stop=False)
                        pe.matmul(out, e.put_m[:, pos % Q, :], s.SI[:, pos % 2, chunk(k)], start=False,
                                  stop=(pos % Q == Q - 1)).then_inc(e_mm, 1)

                    if A:
                        if pos % Q == 1 and (inner or n > Q):
                            pe.wait_ge(at_ok, batches(K, pos))
                        gather(0)
                        gather(1)
                    if S:
                        pe.wait_ge(w_ok, 3 * m + 3)
                        pe.wait_ge(wa_ok, m + 1)
                        for j in range(TILES):
                            d = pe.matmul(ring[2][:, 0:W], s.SIT[:, ms, j, :], wt[:, (pos - LAG) % 2, j, :],
                                          start=(j == 0), stop=(j == TILES - 1))
                        d.then_inc(o_mm, 1)
                    if A:
                        if pos % Q == 0 and (inner or n > 0):
                            pe.wait_ge(es_ok, batches(K, pos))
                        score(0)
                        gather(2)
                        score(1)
                        score(2)
                    if softened(n, pos, inner):
                        i = batches(K, pos)
                        pe.wait_ge(ex_ok, i)
                        if A:
                            pe.wait_ge(v_ok, 3 * n + 3)
                        for h in range(2):
                            for j in range(TILES // 2):
                                d = pe.matmul(bU[(pos + CHUNKS + h) % 2][:, H * j:H * j + H],
                                              top[:, P * (TILES // 2 * h + j):P * (TILES // 2 * h + j) + P],
                                              e.ident[0:H, 0:H], start=True, stop=True)
                            d.then_inc(at_mm, 1)

                every_step(pe, step, LAG + 2)

            @block.scalar
            def _(act):
                def project(K, pos, late, reuse):
                    n = 8 * K + pos
                    act.wait_ge(s.xT_mm, n + 1)
                    act.copy(s.xT[:, :], ring[0][:, 0:P]).then_inc(s.xT_ok, 1)
                    act.wait_ge(s.p_mm, n + 1)
                    if late:
                        act.wait_ge(s.u_mm, 3 * n - 3)
                    act.copy(s.hi[:, pos % 2, :], ring[1][:, 0:2 * P]).then_inc(s.hi_ok, 1)
                    if reuse:
                        act.wait_ge(g_mm, 3 * n - 21)
                    act.copy(grs[:, pos % 8, :], ring[1][:, P:2 * P]).then_inc(s.hi_ok, 1)

                normalise_x(act, e, s, 0, 0, False)
                project(0, 0, False, False)

                def step(K, pos, inner):
                    n = 8 * K + pos
                    m = n - LAG
                    i = batches(K, pos)
                    if softened(n, pos, inner):
                        act.wait_ge(e_mm, 3 * n)
                        if inner or n > Q:
                            act.wait_ge(z_ok, i - 1)
                        act.copy(es[:, :], bE[0:2 * H, 0:ECAP]).then_inc(es_ok, 1)
                    if prepared(n, inner):
                        normalise_x(act, e, s, K, pos + 1, inner or n + 1 >= 2)
                    if scored(n, inner):
                        if inner or n >= 8:
                            act.wait_ge(o_mm, n - 7)
                        evacuate_rows(act, s, ring, K, pos)
                    if prepared(n, inner):
                        project(K, pos + 1, inner or n + 1 >= 2, inner or n + 1 >= 8)
                    if summed(n, inner):
                        q = (pos - LAG) % Q
                        act.wait_ge(at_ok, softmaxes(K, pos))
                        if inner or m >= 2:
                            act.wait_ge(o_mm, m - 1)
                        act.copy(wt[:, (pos - LAG) % 2, :, P:W],
                                 aT[:, parity(pos), :, HEADS * q:HEADS * (q + 1)]).then_inc(wa_ok, 1)
                    if scored(n, inner):
                        for k in range(CHUNKS):
                            act.wait_ge(s.u_mm, 3 * n + k + 1)
                            if inner or 3 * n + k >= 2:
                                act.wait_ge(v_ok, 3 * n + k - 1)
                            b = (pos + k) % 2
                            act.mul(t[:, b, 0:width(k)], bU[b][:, 0:width(k)], SLOPE).then_inc(t_ok, 1)
                    if summed(n, inner):
                        act.wait_ge(o_mm, m + 1)
                        if (pos - LAG) % Q == 0 and (inner or m >= Q):
                            act.wait_ge(s.cen_ok, i - 1)
                        act.copy(os[:, (pos - LAG) % Q, :], ring[2][:, 0:W]).then_inc(os_ok, 1)
                    if softened(n, pos, inner):
                        act.wait_ge(z_ok, i)
                        act.activation(top[:, :], top[:, :], ACT.Exp).then_inc(ex_ok, 1)
                        for h in range(2):
                            act.wait_ge(at_mm, 2 * i - 1 + h)
                            d = act.copy(aT[:, (pos // Q + 1) % 2, TILES // 2 * h:TILES // 2 * (h + 1), :],
                                         bU[(pos + CHUNKS + h) % 2][:, 0:TILES // 2 * H].rearrange("p (j c) -> p j c", c=H))
                        d.then_inc(at_ok, 1)
                    if finished(n, pos, inner):
                        squares(act, e, s, i - 2)

                every_step(act, step, LAG + 2)

            @block.vector
            def _(v):
                prepare_edges(v, e, s, 0, 0, False, ())
                split_low(v, s, ring, 0, 0, False, 2)

                def step(K, pos, inner):
                    n = 8 * K + pos
                    m, q, b = n - LAG, (pos - LAG) % Q, (pos - LAG) % 2
                    i = batches(K, pos)
                    if scored(n, inner):
                        if inner or n >= 8:
                            v.wait_ge(g_mm, 3 * n - 21)
                        number_edges(v, e, s, ring, K, pos)
                    if prepared(n, inner):
                        prepare_edges(v, e, s, K, pos + 1, inner or n + 1 >= 2, (s.s_mm, e_mm))
                    if summed(n, inner):
                        v.wait_ge(at_ok, softmaxes(K, pos))
                        if inner or m >= 2:
                            v.wait_ge(o_mm, m - 1)
                        for k in range(CHUNKS):
                            r = len(tiles(k))
                            v.wait_ge(g_mm, 3 * m + k + 1)
                            att = aT[:, parity(pos), 4 * k:4 * k + r, HEADS * q:HEADS * (q + 1)]
                            v.tensor_tensor(wt[:, b, 4 * k:4 * k + r, 0:P].rearrange("p r (h f) -> p r h f", h=HEADS),
                                            ring[(k + 1) % 3][:, 0:P * r].rearrange("p (r h f) -> p r h f", r=r, h=HEADS),
                                            att.unsqueeze(3).broadcast_to([P, r, HEADS, HF]), ALU.mult).then_inc(w_ok, 1)
                    if finished(n, pos, inner):
                        z = Steps(v, seq_c, 7 * (i - 2))
                        v.wait_ge(os_ok, n - LAG)
                        z.add(v.reciprocal(rden[:, :, :], os[:, :, P:W]))
                        z.wait()
                        z.add(v.tensor_tensor(s.res[:, :, :].rearrange("p q (h f) -> p q h f", h=HEADS),
                                              os[:, :, 0:P].rearrange("p q (h f) -> p q h f", h=HEADS),
                                              rden[:, :, :].unsqueeze(3).broadcast_to([P, Q, HEADS, HF]), ALU.mult))
                        z.wait()
                        z.add(v.scalar_tensor_tensor(s.res[:, :, :], s.res[:, :, :], SLOPE, s.res[:, :, :], ALU.mult, ALU.max))
                        z.wait()
                        residual(v, e, s, z, i - 2)
                        centre(v, e, s, z, i - 2)
                    if prepared(n, inner):
                        split_low(v, s, ring, K, pos + 1, inner or n + 1 >= 2, 2)
                    if scored(n, inner):
                        for k in range(CHUNKS):
                            v.wait_ge(t_ok, 3 * n + k + 1)
                            if inner or 3 * n + k >= 2:
                                v.wait_ge(e_mm, 3 * n + k - 1)
                            w, b = width(k), (pos + k) % 2
                            v.tensor_tensor(vv[:, b, 0:w], bU[b][:, 0:w], t[:, b, 0:w], ALU.max).then_inc(v_ok, 1)
                    if softened(n, pos, inner):
                        z = Steps(v, seq_z, 3 * (i - 1))
                        v.wait_ge(es_ok, i)
                        v.wait_ge(pad_ok, 2)
                        z.add(v.tensor_tensor(mark[:, 1:ECAP], es[H:2 * H, 1:ECAP], es[H:2 * H, 0:ECAP - 1], ALU.subtract))
                        z.wait()
                        z.add(v.tensor_tensor_scan(run[:, :], mark[:, 0:ECAP], es[0:H, :], LOWEST, ALU.add, ALU.max))
                        z.wait()
                        if inner or n > Q:
                            v.wait_ge(at_mm, 2 * i - 2)
                        z.add(v.tensor_tensor_scan(top[:, ECAP - 1::-1], mark[:, ECAP:0:-1], run[:, ECAP - 1::-1],
                                                   LOWEST, ALU.add, ALU.max))
                        z.wait()
                        v.tensor_tensor(top[:, :], es[0:H, :], top[:, :], ALU.subtract).then_inc(z_ok, 1)

                every_step(v, step, LAG + 2)


def layer2_packed(nc, e):
    c = ExitStack()
    with c:
        def sb(name, shape, dt=F32):
            return c.enter_context(nc.sbuf_tensor("c_" + name, shape, dt))

        def sem(name):
            return c.enter_context(nc.semaphore("c_" + name))

        s = packed_buffers(nc, c, "c_", 2)
        h = sb("h", [P, 2, CHUNK])
        ysq = sb("ysq", [P, 2, CHUNK])
        var = sb("var", [P, 2, 4])
        z = sb("z", [P, 2, TILES, P])
        bb = sb("bb", [P, Q, P])
        h_ok = sem("h_ok")
        y_mm = sem("y_mm")
        ysq_ok = sem("ysq_ok")
        sum_ok = sem("sum_ok")
        root_ok = sem("root_ok")
        inv_ok = sem("inv_ok")
        z_ok = sem("z_ok")
        o_mm = sem("o_mm")
        o_read = sem("o_read")
        seq_c = sem("seq_c")
        ring = e.banks[0:3]
        bU = e.banks[3:5]
        bY = e.banks[5:7]
        bO = e.banks[7]

        def gathered(n, inner):
            return inner or n < B

        def prepared(n, inner):
            return inner or n + 1 < B

        def summed(n, inner):
            return inner or 1 <= n <= B

        def finished(n, pos, inner):
            return pos % Q == 1 and (inner or n > Q)

        def batches(K, pos):
            return 8 // Q * K + pos // Q

        with nc.Block() as block:
            @block.sync
            def _(sp):
                load_adjacency(sp, e, s)

            @block.gpsimd
            def _(pool):
                pool.memset(s.junk[:, :], 0.0).then_inc(s.sq_ok, 1)

            @block.tensor
            def _(pe):
                pe.wait_ge(s.x_ok, 1)
                pe.transpose(ring[0][:, 0:P], s.xin[:, 0, :], e.ident[:, :]).then_inc(s.xT_mm, 1)
                pe.wait_ge(s.xT_ok, 1)
                pe.matmul(ring[1][:, 0:2 * P], s.xT[:, :], e.W1s[:, :, :], start=True, stop=True).then_inc(s.p_mm, 1)

                def step(K, pos, inner):
                    n = 8 * K + pos
                    A, N, S = gathered(n, inner), prepared(n, inner), summed(n, inner)
                    if A:
                        pe.wait_ge(s.c_ok, n + 1)
                        pe.wait_ge(s.si_ok, n + 1)
                        pe.wait_ge(s.xT_ok, n + 1)
                        number_columns(pe, s, ring[0], pos, 0)
                        pe.wait_ge(s.lo_ok, n + 1)
                        number_columns(pe, s, ring[1], pos, 1)
                        if inner or n > 0:
                            pe.wait_ge(s.sit_ok, 3 * n)
                        number_columns(pe, s, ring[2], pos, 2)
                        for k in range(CHUNKS):
                            pe.wait_ge(s.sj_ok, 3 * n + k + 1)
                            transpose_rows(pe, e, s, ring[k], pos, k)
                    if N:
                        pe.wait_ge(s.x_ok, n + 2)
                        pe.wait_ge(s.sit_ok, 3 * n + 1)
                        pe.transpose(ring[0][:, 0:P], s.xin[:, (pos + 1) % 2, :], e.ident[:, :]).then_inc(s.xT_mm, 1)

                    def gather(k):
                        if inner or 3 * n + k >= 2:
                            pe.wait_ge(h_ok, 3 * n + k - 1)
                        gather_pairs(pe, s, bU[(pos + k) % 2], pos, k)

                    def mlp(k):
                        b = (pos + k) % 2
                        pe.wait_ge(h_ok, 3 * n + k + 1)
                        if inner or 3 * n + k >= 2:
                            pe.wait_ge(z_ok, 3 * n + k - 1)
                        for j in tiles(k):
                            a = P * (j - 4 * k)
                            pe.matmul(bY[b][:, a:a + P], e.ones3[:, :], e.b2x[:, :], start=True, stop=False)
                            d = pe.matmul(bY[b][:, a:a + P], h[:, b, a:a + P], e.W2c[:, :], start=False, stop=True)
                        d.then_inc(y_mm, 1)

                    if A:
                        gather(0)
                        gather(1)
                    if S:
                        m, ob = n - 1, (pos - 1) % 2
                        pe.wait_ge(z_ok, 3 * n)
                        if (pos - 1) % Q == 0 and (inner or m >= Q):
                            pe.wait_ge(o_read, batches(K, pos))
                        for j in range(TILES):
                            a = P * ((pos - 1) % Q)
                            d = pe.matmul(bO[:, a:a + P], s.SIT[:, ob, j, :], z[:, ob, j, :], start=(j == 0),
                                          stop=(j == TILES - 1), skip_group_check=True)
                        d.then_inc(o_mm, 1)
                    if N:
                        pe.wait_ge(s.xT_ok, n + 2)
                        pe.wait_ge(s.sit_ok, 3 * n + 2)
                        pe.matmul(ring[1][:, 0:2 * P], s.xT[:, :], e.W1s[:, :, :], start=True, stop=True).then_inc(s.p_mm, 1)
                    if A:
                        mlp(0)
                        gather(2)
                        mlp(1)
                        mlp(2)

                every_step(pe, step, 2)

            @block.scalar
            def _(act):
                def project(K, pos, late):
                    n = 8 * K + pos
                    act.wait_ge(s.xT_mm, n + 1)
                    act.copy(s.xT[:, :], ring[0][:, 0:P]).then_inc(s.xT_ok, 1)
                    act.wait_ge(s.p_mm, n + 1)
                    if late:
                        act.wait_ge(s.u_mm, 3 * n - 3)
                    act.copy(s.hi[:, pos % 2, :], ring[1][:, 0:2 * P]).then_inc(s.hi_ok, 1)

                normalise_x(act, e, s, 0, 0, False)
                project(0, 0, False)

                def step(K, pos, inner):
                    n = 8 * K + pos

                    def rectify(k):
                        b = (pos + k) % 2
                        act.wait_ge(s.u_mm, 3 * n + k + 1)
                        if inner or 3 * n + k >= 2:
                            act.wait_ge(y_mm, 3 * n + k - 1)
                        act.activation(h[:, b, 0:width(k)], bU[b][:, 0:width(k)], ACT.Relu,
                                       bias=e.b1c[:, 0:1]).then_inc(h_ok, 1)

                    def square(k):
                        b = (pos + k) % 2
                        act.wait_ge(y_mm, 3 * n + k + 1)
                        if inner or 3 * n + k >= 2:
                            act.wait_ge(sum_ok, 3 * n + k - 1)
                        act.activation(ysq[:, b, 0:width(k)], bY[b][:, 0:width(k)], ACT.Square).then_inc(ysq_ok, 1)

                    def root(k):
                        r = len(tiles(k))
                        act.wait_ge(sum_ok, 3 * n + k + 1)
                        sd = var[:, (pos + k) % 2, 0:r]
                        act.activation(sd, sd, ACT.Sqrt, bias=e.eps[:, 0:1], scale=1.0 / P).then_inc(root_ok, 1)

                    if prepared(n, inner):
                        normalise_x(act, e, s, K, pos + 1, inner or n + 1 >= 2)
                    if gathered(n, inner):
                        if inner or n >= 2:
                            act.wait_ge(o_mm, n - 1)
                        evacuate_rows(act, s, ring, K, pos)
                        rectify(0)
                        rectify(1)
                    if prepared(n, inner):
                        project(K, pos + 1, inner or n + 1 >= 2)
                    if gathered(n, inner):
                        square(0)
                        rectify(2)
                        square(1)
                        root(0)
                        square(2)
                        root(1)
                        root(2)
                    if finished(n, pos, inner):
                        squares(act, e, s, batches(K, pos) - 1)

                every_step(act, step, 2)

            @block.vector
            def _(v):
                prepare_edges(v, e, s, 0, 0, False, ())
                split_low(v, s, ring, 0, 0, False, 1)

                def step(K, pos, inner):
                    n = 8 * K + pos

                    def total(k):
                        r, b = len(tiles(k)), (pos + k) % 2
                        v.wait_ge(ysq_ok, 3 * n + k + 1)
                        if inner or 3 * n + k >= 2:
                            v.wait_ge(z_ok, 3 * n + k - 1)
                        v.tensor_reduce(var[:, b, 0:r], ysq[:, b, 0:width(k)].rearrange("p (j f) -> p j f", f=P),
                                        AX.X, ALU.add).then_inc(sum_ok, 1)

                    def scale(k):
                        r, b = len(tiles(k)), (pos + k) % 2
                        v.wait_ge(root_ok, 3 * n + k + 1)
                        v.reciprocal(var[:, b, 0:r], var[:, b, 0:r]).then_inc(inv_ok, 1)
                        v.wait_ge(inv_ok, 3 * n + k + 1)
                        v.tensor_tensor(z[:, pos % 2, 4 * k:4 * k + r, :], bY[b][:, 0:width(k)].rearrange("p (j f) -> p j f", f=P),
                                        var[:, b, 0:r].unsqueeze(2).broadcast_to([P, r, P]), ALU.mult).then_inc(z_ok, 1)

                    if gathered(n, inner):
                        if inner or n >= 2:
                            v.wait_ge(s.u_mm, 3 * n - 3)
                        number_edges(v, e, s, ring, K, pos)
                    if prepared(n, inner):
                        prepare_edges(v, e, s, K, pos + 1, inner or n + 1 >= 2, (s.s_mm, s.u_mm))
                    if finished(n, pos, inner):
                        i = batches(K, pos) - 1
                        q = Steps(v, seq_c, 6 * i)
                        v.wait_ge(o_mm, n - 1)
                        v.tensor_tensor(s.res[:, :, :], bO[:, :].rearrange("p (q f) -> p q f", f=P),
                                        e.gam[:, :].unsqueeze(1).broadcast_to([P, Q, P]), ALU.mult).then_inc(o_read, 1)
                        q.add(v.tensor_tensor(bb[:, :, :], e.bet[:, :].unsqueeze(1).broadcast_to([P, Q, P]),
                                              e.deg[:, 0, bass.ds(Q * i, Q)].unsqueeze(2).broadcast_to([P, Q, P]), ALU.mult))
                        q.wait()
                        v.wait_ge(o_read, i + 1)
                        q.add(v.tensor_tensor(s.res[:, :, :], s.res[:, :, :], bb[:, :, :], ALU.add))
                        q.wait()
                        residual(v, e, s, q, i)
                        centre(v, e, s, q, i)
                    if prepared(n, inner):
                        split_low(v, s, ring, K, pos + 1, inner or n + 1 >= 2, 1)
                    if gathered(n, inner):
                        if inner or n >= 2:
                            v.wait_ge(o_mm, n - 1)
                        total(0)
                        total(1)
                        scale(0)
                        total(2)
                        scale(1)
                        scale(2)

                every_step(v, step, 2)


class Masks:
    pass


def dense_masks(nc, c, e):
    m = Masks()

    def sb(name, shape):
        return c.enter_context(nc.sbuf_tensor("m_" + name, shape, F32))

    m.Wpad = sb("Wpad", [P, 2 * P - HEADS])
    m.Rep = sb("Rep", [P, P, HEADS])
    m.RepT = sb("RepT", [P, NRT, P])
    m.diag = sb("diag", [P, P])
    hselT = sb("hselT", [HEADS, P])
    rep8 = sb("rep8", [HEADS, P])
    masks, made, heads_mm, diag_mm, diag_ok = (c.enter_context(nc.semaphore("m_" + k)) for k in (
        "masks", "made", "heads_mm", "diag_mm", "diag_ok"))
    banks = e.banks
    with nc.Block() as block:
        @block.gpsimd
        def _(pool):
            pool.memset(m.Wpad[:, :], 0.0).then_inc(masks, 1)
            pool.memset(m.Rep[:, :, :], 0.0).then_inc(masks, 1)
            pool.memset(m.RepT[:, :, :], 1.0).then_inc(masks, 1)
            pool.wait_ge(masks, 3)
            pool.affine_select(out=m.Rep[:, :, :], in_=m.Rep[:, :, :], compare_op=ALU.not_equal, fill=1.0,
                               base=0, pattern=[[-1, P], [0, HEADS]], channel_multiplier=1).then_inc(masks, 1)
            pool.affine_select(out=m.RepT[:, :, :], in_=m.RepT[:, :, :], compare_op=ALU.is_ge, fill=0.0,
                               base=0, pattern=[[P, NRT], [-HEADS, P]], channel_multiplier=1).then_inc(masks, 1)
            pool.wait_ge(masks, 5)
            pool.affine_select(out=m.RepT[:, :, :], in_=m.RepT[:, :, :], compare_op=ALU.is_ge, fill=0.0,
                               base=HEADS - 1, pattern=[[-P, NRT], [HEADS, P]], channel_multiplier=-1).then_inc(masks, 1)

        @block.tensor
        def _(pe):
            pe.transpose(banks[1][0:HEADS, 0:P], e.hsel[:, :], e.ident[:, :]).then_inc(heads_mm, 1)
            pe.wait_ge(made, 2)
            pe.matmul(banks[2][:, 0:P], rep8[:, :], hselT[:, :], start=True, stop=True).then_inc(diag_mm, 1)

        @block.vector
        def _(v):
            v.wait_ge(masks, 3)
            v.tensor_scalar(m.Wpad[:, P - HEADS:P], e.hsel[:, :], e.wcol[:, 0:1], None, ALU.mult)
            v.tensor_copy(rep8[:, :].rearrange("k (r h) -> k r h", h=HEADS),
                          e.ident[0:HEADS, 0:HEADS].unsqueeze(1).broadcast_to([HEADS, RT, HEADS])).then_inc(made, 1)
            v.wait_ge(heads_mm, 1)
            v.tensor_copy(hselT[:, :], banks[1][0:HEADS, 0:P]).then_inc(made, 1)
            v.wait_ge(diag_mm, 1)
            v.tensor_copy(m.diag[:, :], banks[2][:, 0:P]).then_inc(diag_ok, 1)
            v.wait_ge(diag_ok, 1)
    return m


def layer1_dense(nc, e):
    c = ExitStack()
    with c:
        def sb(name, shape, dt=F32):
            return c.enter_context(nc.sbuf_tensor("gb_" + name, shape, dt))

        def sem(name):
            return c.enter_context(nc.semaphore("gb_" + name))

        cur, ident = e.cur, e.ident
        ain = sb("ain", [P, P])
        xin = sb("xin", [P, P])
        xT = sb("xT", [P, P])
        gT = sb("gT", [P, 2, P])
        gr = sb("gr", [P, P])
        u = sb("u", [P, 2, RS, P])
        lk = sb("lk", [P, 2, RS, P])
        arep = sb("arep", [P, P])
        drop = sb("drop", [P, P])
        sc = sb("sc", [P, P])
        top = sb("top", [P, 1])
        ex = sb("ex", [P, P])
        den = sb("den", [P, 1])
        aT = sb("aT", [P, P])
        od = sb("od", [P, P])
        res = sb("res", [P, P])
        mean = sb("mean", [P, 1])
        junk = sb("junk", [P, P])
        (a_in, x_ok, xT_mm, xT_ok, g_mm, gT_ok, lk_ok, lk_used, e_mm, rep_mm, arep_ok, top_ok, ex_ok, a_ok, aT_mm, aT_ok,
         o_mm, od_ok, out_mm, cen_ok, sq_ok, seq_g, seq_s, seq_t) = (sem(k) for k in (
             "a_in", "x_ok", "xT_mm", "xT_ok", "g_mm", "gT_ok", "lk_ok", "lk_used", "e_mm", "rep_mm", "arep_ok", "top_ok",
             "ex_ok", "a_ok", "aT_mm", "aT_ok", "o_mm", "od_ok", "out_mm", "cen_ok", "sq_ok", "seq_g", "seq_s", "seq_t"))
        seq_x = sem("seq_x")
        bX, bG, bE, bR, bT, bO, bZ = e.banks[:7]
        masks = dense_masks(nc, c, e)
        NS = P // RS

        with nc.Block() as block:
            @block.sync
            def _(sp):
                sp.dma_start(ain[:, :], e.adj_v[:, 0, :]).then_inc(a_in, 16)
                with sp.Fori(1, B) as n:
                    sp.wait_ge(rep_mm, NRT * n)
                    sp.dma_start(ain[:, :], e.adj_v[:, n, :]).then_inc(a_in, 16)

            @block.tensor
            def _(pe):
                with pe.Fori(0, B) as n:
                    pe.wait_ge(x_ok, n + 1)
                    pe.transpose(bX[:, 0:P], xin[:, :], ident[:, :]).then_inc(xT_mm, 1)
                    pe.wait_ge(xT_ok, n + 1)
                    pe.matmul(bG[:, 0:P], e.WlrT[:, 0, :], xT[:, :], start=True, stop=True)
                    pe.matmul(bG[:, P:2 * P], e.WlrT[:, 1, :], xT[:, :], start=True, stop=True)
                    pe.matmul(bG[:, 2 * P:3 * P], xT[:, :], e.WlrT[:, 1, :], start=True, stop=True).then_inc(g_mm, 1)
                    pe.wait_ge(a_in, 16 * n + 16)
                    pe.wait_ge(gT_ok, n + 1)
                    for t in range(NRT):
                        m = NRT * n + t
                        pe.matmul(bR[:, 0:P], masks.Rep[:, :, :].rearrange("i r h -> i (r h)")[:, P * t:P * t + P],
                                  ain[:, :], start=True, stop=True).then_inc(rep_mm, 1)
                        for k in range(RT // RS):
                            s = NS * n + (RT // RS) * t + k
                            pe.wait_ge(lk_ok, s + 1)
                            for r in range(RS):
                                row = RS * k + r
                                w = masks.Wpad[:, P - HEADS - HEADS * row:2 * P - HEADS - HEADS * row]
                                q = pe.matmul(bE[:, 0:P], w, lk[:, k % 2, r, :], start=(row == 0), stop=(row == RT - 1))
                            q.then_inc(lk_used, 1)
                        pe.wait_ge(a_ok, m + 1)
                        pe.transpose(bT[:, 0:P], ex[:, :], ident[:, :]).then_inc(aT_mm, 1)
                        pe.wait_ge(aT_ok, m + 1)
                        pe.matmul(bO[:, 0:P], aT[:, :], gr[:, :], start=True, stop=True).then_inc(o_mm, 1)
                        pe.wait_ge(od_ok, m + 1)
                        pe.matmul(bZ[:, 0:P], masks.RepT[:, t, :], od[:, :], start=(t == 0), stop=(t == NRT - 1)).then_inc(out_mm, 1)

            @block.scalar
            def _(act):
                with act.Fori(0, B) as n:
                    act.wait_ge(xT_mm, n + 1)
                    act.copy(xT[:, :], bX[:, 0:P]).then_inc(xT_ok, 1)
                    act.wait_ge(g_mm, n + 1)
                    act.copy(gT[:, :, :], bG[:, 0:2 * P].rearrange("p (a f) -> p a f", a=2)).then_inc(gT_ok, 1)
                    act.copy(gr[:, :], bG[:, 2 * P:3 * P]).then_inc(seq_g, 1)
                    act.wait_ge(seq_g, n + 1)
                    for t in range(NRT):
                        m = NRT * n + t
                        act.wait_ge(top_ok, m + 1)
                        act.activation(ex[:, :], sc[:, :], ACT.Exp, bias=top[:, 0:1], accum_out=den[:, 0:1]).then_inc(ex_ok, 1)
                        act.wait_ge(aT_mm, m + 1)
                        act.copy(aT[:, :], bT[:, 0:P]).then_inc(aT_ok, 1)
                    act.wait_ge(cen_ok, n + 1)
                    act.activation(junk[:, :], cur[:, n, :], ACT.Square, accum_out=e.sqsum[:, bass.ds(n, 1)]).then_inc(sq_ok, 1)
                    act.wait_ge(sq_ok, n + 1)

            @block.vector
            def _(v):
                with v.Fori(0, B) as n:
                    v.tensor_copy(xin[:, :], cur[:, n, :]).then_inc(x_ok, 1)
                    v.wait_ge(gT_ok, n + 1)
                    v.wait_ge(seq_g, n + 1)
                    for t in range(NRT):
                        m = NRT * n + t
                        for k in range(RT // RS):
                            s = NS * n + (RT // RS) * t + k
                            q = Steps(v, seq_s, s)
                            b = k % 2
                            for r in range(RS):
                                i = RT * t + RS * k + r
                                d = v.tensor_scalar(u[:, b, r, :], gT[:, 0, :], gT[:, 1, i:i + 1], None, ALU.add)
                            q.add(d)
                            q.wait()
                            if t == 0 and k < 2:
                                v.wait_ge(out_mm, NRT * n)
                            else:
                                v.wait_ge(lk_used, s - 1)
                            v.scalar_tensor_tensor(lk[:, b, :, :], u[:, b, :, :], SLOPE, u[:, b, :, :],
                                                   ALU.mult, ALU.max).then_inc(lk_ok, 1)
                        q = Steps(v, seq_t, 5 * m)
                        v.wait_ge(rep_mm, m + 1)
                        q.add(v.tensor_copy(arep[:, :], bR[:, 0:P]))
                        q.wait()
                        q.add(v.tensor_scalar(drop[:, :], arep[:, :], 0.0, NEG, ALU.is_equal, ALU.mult))
                        v.wait_ge(lk_used, NS * n + (RT // RS) * (t + 1))
                        q.add(v.tensor_tensor(sc[:, :], bE[:, 0:P], arep[:, :], ALU.mult))
                        q.wait()
                        q.add(v.tensor_tensor(sc[:, :], sc[:, :], drop[:, :], ALU.add))
                        q.wait()
                        v.tensor_reduce(top[:, :], sc[:, :], AX.X, ALU.max, negate=True).then_inc(top_ok, 1)
                        v.wait_ge(ex_ok, m + 1)
                        q.add(v.reciprocal(den[:, :], den[:, :]))
                        q.wait()
                        v.tensor_scalar(ex[:, :], ex[:, :], den[:, 0:1], None, ALU.mult).then_inc(a_ok, 1)
                        v.wait_ge(o_mm, m + 1)
                        v.tensor_tensor(od[:, :], bO[:, 0:P], masks.diag[:, :], ALU.mult).then_inc(od_ok, 1)
                    v.wait_ge(out_mm, NRT * (n + 1))
                    q = Steps(v, seq_x, 5 * n)
                    q.add(v.tensor_copy(res[:, :], bZ[:, 0:P]))
                    q.wait()
                    q.add(v.scalar_tensor_tensor(res[:, :], res[:, :], SLOPE, res[:, :], ALU.mult, ALU.max))
                    q.wait()
                    q.add(v.tensor_tensor(res[:, :], res[:, :], xin[:, :], ALU.add))
                    q.wait()
                    q.add(v.tensor_reduce(mean[:, :], res[:, :], AX.X, ALU.add))
                    q.wait()
                    q.add(v.tensor_scalar(mean[:, :], mean[:, :], 1.0 / P, None, ALU.mult))
                    q.wait()
                    v.tensor_scalar(cur[:, n, :], res[:, :], mean[:, 0:1], None, ALU.subtract).then_inc(cen_ok, 1)
                    v.wait_ge(cen_ok, n + 1)


def layer2_dense(nc, e):
    c = ExitStack()
    with c:
        def sb(name, shape, dt=F32):
            return c.enter_context(nc.sbuf_tensor("gc_" + name, shape, dt))

        def sem(name):
            return c.enter_context(nc.semaphore("gc_" + name))

        cur, ident = e.cur, e.ident
        ain = sb("ain", [P, P])
        aT = sb("aT", [P, P])
        xin = sb("xin", [P, P])
        xT = sb("xT", [P, P])
        hT = sb("hT", [P, 2, P])
        h = sb("h", [P, 2, RS, P])
        y = sb("y", [P, P, P])
        ysq = sb("ysq", [P, 2, RS, P])
        cf = sb("cf", [P, P])
        zT = sb("zT", [P, P])
        asum = sb("asum", [P, 1])
        bb = sb("bb", [P, P])
        res = sb("res", [P, P])
        mean = sb("mean", [P, 1])
        junk = sb("junk", [P, P])
        (a_in, x_ok, xT_mm, xT_ok, g_mm, h1_ok, h_ok, y_mm, y_ok, ysq_ok, var_ok, cf_root, cf_ok, aT_ok, z_mm, zT_ok,
         zt_mm, cen_ok, sq_ok, seq_c, seq_x) = (sem(k) for k in (
             "a_in", "x_ok", "xT_mm", "xT_ok", "g_mm", "h1_ok", "h_ok", "y_mm", "y_ok", "ysq_ok", "var_ok", "cf_root",
             "cf_ok", "aT_ok", "z_mm", "zT_ok", "zt_mm", "cen_ok", "sq_ok", "seq_c", "seq_x"))
        bX, bG, bY0, bY1, bZ, bZT = e.banks[:6]
        bY = (bY0, bY1)
        NS = P // RS

        with nc.Block() as block:
            @block.sync
            def _(sp):
                sp.dma_start(ain[:, :], e.adj_v[:, 0, :]).then_inc(a_in, 16)
                with sp.Fori(1, B) as n:
                    sp.wait_ge(cen_ok, n)
                    sp.dma_start(ain[:, :], e.adj_v[:, n, :]).then_inc(a_in, 16)

            @block.tensor
            def _(pe):
                with pe.Fori(0, B) as n:
                    pe.wait_ge(x_ok, n + 1)
                    pe.wait_ge(a_in, 16 * n + 16)
                    pe.transpose(bX[:, 0:P], xin[:, :], ident[:, :])
                    pe.transpose(bX[:, P:2 * P], ain[:, :], ident[:, :]).then_inc(xT_mm, 1)
                    pe.wait_ge(xT_ok, n + 1)
                    pe.matmul(bG[:, 0:P], e.W1s[:, 1, :], xT[:, :], start=True, stop=True)
                    pe.matmul(bG[:, P:2 * P], e.W1s[:, 0, :], xT[:, :], start=True, stop=True).then_inc(g_mm, 1)
                    for k in range(NS):
                        s = NS * n + k
                        pe.wait_ge(h_ok, s + 1)
                        if k >= 2:
                            pe.wait_ge(y_ok, s - 1)
                        for r in range(RS):
                            q = pe.matmul(bY[k % 2][:, P * r:P * r + P], h[:, k % 2, r, :], e.W2c[:, :], start=True, stop=True)
                        q.then_inc(y_mm, 1)
                    pe.wait_ge(cf_ok, n + 1)
                    for i in range(P):
                        q = pe.matmul(bZ[:, i:i + 1], y[:, i, :], cf[:, i:i + 1], start=True, stop=True)
                    q.then_inc(z_mm, 1)
                    pe.wait_ge(zT_ok, n + 1)
                    pe.transpose(bZT[:, 0:P], zT[:, :], ident[:, :]).then_inc(zt_mm, 1)

            @block.scalar
            def _(act):
                with act.Fori(0, B) as n:
                    act.wait_ge(xT_mm, n + 1)
                    act.copy(aT[:, :], bX[:, P:2 * P]).then_inc(aT_ok, 1)
                    act.copy(xT[:, :], bX[:, 0:P]).then_inc(xT_ok, 1)
                    for k in range(NS):
                        s = NS * n + k
                        act.wait_ge(y_ok, s + 1)
                        if k >= 2:
                            act.wait_ge(var_ok, s - 1)
                        act.activation(ysq[:, k % 2, :, :], y[:, RS * k:RS * k + RS, :], ACT.Square).then_inc(ysq_ok, 1)
                    act.wait_ge(var_ok, NS * (n + 1))
                    act.activation(cf[:, :], cf[:, :], ACT.Sqrt, bias=e.eps[:, 0:1], scale=1.0 / P).then_inc(cf_root, 1)
                    act.wait_ge(z_mm, n + 1)
                    act.copy(zT[:, :], bZ[:, 0:P]).then_inc(zT_ok, 1)
                    act.wait_ge(cen_ok, n + 1)
                    act.activation(junk[:, :], cur[:, n, :], ACT.Square, accum_out=e.sqsum[:, bass.ds(n, 1)]).then_inc(sq_ok, 1)
                    act.wait_ge(sq_ok, n + 1)

            @block.vector
            def _(v):
                with v.Fori(0, B) as n:
                    v.tensor_copy(xin[:, :], cur[:, n, :]).then_inc(x_ok, 1)
                    v.wait_ge(g_mm, n + 1)
                    v.tensor_copy(hT[:, 0, :], bG[:, 0:P]).then_inc(h1_ok, 1)
                    v.tensor_scalar(hT[:, 1, :], bG[:, P:2 * P], e.b1c[:, 0:1], None, ALU.add).then_inc(h1_ok, 1)
                    v.wait_ge(h1_ok, 2 * n + 2)

                    def variance(k):
                        v.wait_ge(ysq_ok, NS * n + k + 1)
                        v.tensor_reduce(cf[:, RS * k:RS * k + RS], ysq[:, k % 2, :, :], AX.X, ALU.add).then_inc(var_ok, 1)

                    def evacuate(k):
                        v.wait_ge(y_mm, NS * n + k + 1)
                        v.tensor_tensor(y[:, RS * k:RS * k + RS, :], bY[k % 2][:, :].rearrange("p (r f) -> p r f", r=RS),
                                        e.b2c[:, :].unsqueeze(1).broadcast_to([P, RS, P]), ALU.add).then_inc(y_ok, 1)

                    for k in range(NS):
                        if k >= 2:
                            v.wait_ge(y_mm, NS * n + k - 1)
                        for r in range(RS):
                            i = RS * k + r
                            d = v.tensor_scalar(h[:, k % 2, r, :], hT[:, 1, :], hT[:, 0, i:i + 1], 0.0, ALU.add, ALU.max)
                        d.then_inc(h_ok, 1)
                        if k >= 1:
                            evacuate(k - 1)
                        if k >= 2:
                            variance(k - 2)
                    evacuate(NS - 1)
                    variance(NS - 2)
                    variance(NS - 1)
                    q = Steps(v, seq_c, n)
                    v.wait_ge(cf_root, n + 1)
                    q.add(v.reciprocal(cf[:, :], cf[:, :]))
                    q.wait()
                    v.wait_ge(aT_ok, n + 1)
                    v.tensor_tensor(cf[:, :], cf[:, :], aT[:, :], ALU.mult).then_inc(cf_ok, 1)
                    q = Steps(v, seq_x, 6 * n)
                    q.add(v.tensor_reduce(asum[:, :], ain[:, :], AX.X, ALU.add))
                    q.wait()
                    q.add(v.scalar_tensor_tensor(bb[:, :], e.bet[:, :], asum[:, 0:1], xin[:, :], ALU.mult, ALU.add))
                    v.wait_ge(zt_mm, n + 1)
                    q.add(v.tensor_tensor(res[:, :], bZT[:, 0:P], e.gam[:, :], ALU.mult))
                    q.wait()
                    q.add(v.tensor_tensor(res[:, :], res[:, :], bb[:, :], ALU.add))
                    q.wait()
                    q.add(v.tensor_reduce(mean[:, :], res[:, :], AX.X, ALU.add))
                    q.wait()
                    q.add(v.tensor_scalar(mean[:, :], mean[:, :], 1.0 / P, None, ALU.mult))
                    q.wait()
                    v.tensor_scalar(cur[:, n, :], res[:, :], mean[:, 0:1], None, ALU.subtract).then_inc(cen_ok, 1)
                    v.wait_ge(cen_ok, n + 1)


def layer3(nc, e):
    c = ExitStack()
    with c:
        def sb(name, shape, dt=F32):
            return c.enter_context(nc.sbuf_tensor("d_" + name, shape, dt))

        def sem(name):
            return c.enter_context(nc.semaphore("d_" + name))

        cur, ident = e.cur, e.ident
        ain = sb("ain", [P, 2, G, P])
        dg = sb("dg", [P, 2, G])
        nz = sb("nz", [P, 2, G])
        xd = sb("xd", [P, 2, G, P])
        aT = sb("aT", [P, 2, G, P])
        gT = sb("gT", [P, 2, G, P])
        res = sb("res", [P, G, P])
        mean = sb("mean", [P, G])
        junk = sb("junk", [P, P])
        a_in = [sem(f"a_in{b}") for b in range(2)]
        self_ok, sum_ok, root_ok, xd_ok, aT_mm, aT_ok, g_mm, g_ok, o_mm, res_ok, cen_ok, sq_ok, seq_f, seq_b = (
            sem(k) for k in ("self_ok", "sum_ok", "root_ok", "xd_ok", "aT_mm", "aT_ok", "g_mm", "g_ok", "o_mm",
                             "res_ok", "cen_ok", "sq_ok", "seq_f", "seq_b"))
        bA, bG, bO = e.banks[:3]

        def grp(t):
            return t[:, :].rearrange("p (g f) -> p g f", g=G)

        def pipeline(eng, front, back):
            front(0, 0)
            front(1, 1)
            back(0, 0)
            with eng.Fori(0, NG // 2 - 1) as k:
                front(2 * k + 2, 0)
                back(2 * k + 1, 1)
                front(2 * k + 3, 1)
                back(2 * k + 2, 0)
            back(NG - 1, 1)

        with nc.Block() as block:
            @block.sync
            def _(sp):
                def load(n, b):
                    sp.dma_start(ain[:, b, :, :], e.adj_v[:, bass.ds(n * G, G), :]).then_inc(a_in[b], 16)
                load(0, 0)
                load(1, 1)
                with sp.Fori(0, NG // 2 - 1) as k:
                    for b in range(2):
                        sp.wait_ge(aT_mm, 2 * k + b + 1)
                        sp.wait_ge(seq_f, 5 * (2 * k + b) + 1)
                        load(2 * k + 2 + b, b)

            @block.tensor
            def _(pe):
                def front(n, b):
                    pe.wait_ge(self_ok, n + 1)
                    if not (isinstance(n, int) and n == 0):
                        pe.wait_ge(aT_ok, n)
                    for g in range(G):
                        m = pe.transpose(bA[:, P * g:P * g + P], ain[:, b, g, :], ident[:, :])
                    m.then_inc(aT_mm, 1)
                    pe.wait_ge(aT_ok, n + 1)
                    pe.wait_ge(xd_ok, n + 1)
                    if not (isinstance(n, int) and n == 0):
                        pe.wait_ge(g_ok, n)
                    for g in range(G):
                        m = pe.matmul(bG[:, P * g:P * g + P], xd[:, b, g, :], aT[:, b, g, :], start=True, stop=True)
                    m.then_inc(g_mm, 1)

                def back(n, b):
                    pe.wait_ge(g_ok, n + 1)
                    if not (isinstance(n, int) and n == 0):
                        pe.wait_ge(res_ok, n)
                    for g in range(G):
                        m = pe.matmul(bO[:, P * g:P * g + P], gT[:, b, g, :], e.W3[:, :], start=True, stop=True)
                    m.then_inc(o_mm, 1)

                pipeline(pe, front, back)

            @block.scalar
            def _(act):
                def front(n, b):
                    act.wait_ge(sum_ok, n + 1)
                    act.activation(dg[:, b, :], dg[:, b, :], ACT.Sqrt).then_inc(root_ok, 1)
                    act.wait_ge(aT_mm, n + 1)
                    if not isinstance(n, int) or n >= 2:
                        act.wait_ge(g_mm, n - 1)
                    act.copy(aT[:, b, :, :], grp(bA)).then_inc(aT_ok, 1)
                    act.wait_ge(g_mm, n + 1)
                    if not isinstance(n, int) or n >= 2:
                        act.wait_ge(o_mm, n - 1)
                    act.copy(gT[:, b, :, :], grp(bG)).then_inc(g_ok, 1)

                def back(n, b):
                    act.wait_ge(cen_ok, n + 1)
                    for g in range(G):
                        if not (isinstance(n, int) and n == 0 and g == 0):
                            act.wait_ge(sq_ok, G * n + g)
                        act.activation(junk[:, :], cur[:, n * G + g, :], ACT.Square,
                                       accum_out=e.sqsum[:, bass.ds(n * G + g, 1)]).then_inc(sq_ok, 1)

                pipeline(act, front, back)

            @block.vector
            def _(v):
                def front(n, b):
                    q = Steps(v, seq_f, 5 * n)
                    v.wait_ge(a_in[b], 8 * (n - b) + 16)
                    v.tensor_tensor(ain[:, b, :, :], ain[:, b, :, :],
                                    ident[:, :].unsqueeze(1).broadcast_to([P, G, P]), ALU.add).then_inc(self_ok, 1)
                    v.wait_ge(self_ok, n + 1)
                    q.add(v.tensor_reduce(dg[:, b, :], ain[:, b, :, :], AX.X, ALU.add))
                    q.wait()
                    q.add(v.tensor_scalar(nz[:, b, :], dg[:, b, :], 0.0, None, ALU.is_equal))
                    q.wait()
                    v.tensor_tensor(dg[:, b, :], dg[:, b, :], nz[:, b, :], ALU.add).then_inc(sum_ok, 1)
                    v.wait_ge(root_ok, n + 1)
                    q.add(v.tensor_scalar(nz[:, b, :], nz[:, b, :], -1.0, 1.0, ALU.mult, ALU.add))
                    q.add(v.reciprocal(dg[:, b, :], dg[:, b, :]))
                    q.wait()
                    q.add(v.tensor_tensor(dg[:, b, :], dg[:, b, :], nz[:, b, :], ALU.mult))
                    q.wait()
                    if not isinstance(n, int) or n >= 2:
                        v.wait_ge(g_mm, n - 1)
                    v.tensor_tensor(xd[:, b, :, :], cur[:, bass.ds(n * G, G), :],
                                    dg[:, b, :].unsqueeze(2).broadcast_to([P, G, P]), ALU.mult).then_inc(xd_ok, 1)

                def back(n, b):
                    q = Steps(v, seq_b, 4 * n)
                    v.wait_ge(o_mm, n + 1)
                    q.add(v.tensor_tensor(res[:, :, :], grp(bO), dg[:, b, :].unsqueeze(2).broadcast_to([P, G, P]),
                                          ALU.mult))
                    q.wait()
                    v.tensor_tensor(res[:, :, :], res[:, :, :], cur[:, bass.ds(n * G, G), :], ALU.add).then_inc(res_ok, 1)
                    v.wait_ge(res_ok, n + 1)
                    q.add(v.tensor_tensor(res[:, :, :], res[:, :, :],
                                          e.bia[:, :].unsqueeze(1).broadcast_to([P, G, P]), ALU.add))
                    q.wait()
                    q.add(v.tensor_reduce(mean[:, :], res[:, :, :], AX.X, ALU.add))
                    q.wait()
                    q.add(v.tensor_scalar(mean[:, :], mean[:, :], 1.0 / P, None, ALU.mult))
                    q.wait()
                    v.tensor_tensor(cur[:, bass.ds(n * G, G), :], res[:, :, :],
                                    mean[:, :].unsqueeze(2).broadcast_to([P, G, P]), ALU.subtract).then_inc(cen_ok, 1)
                    v.wait_ge(cen_ok, n + 1)

                pipeline(v, front, back)


def roots(nc, e, tag):
    c = ExitStack()
    with c:
        root_ok, rstd_ok = (c.enter_context(nc.semaphore(tag + k)) for k in ("root_ok", "rstd_ok"))
        with nc.Block() as block:
            @block.scalar
            def _(act):
                act.activation(e.rstd[:, :], e.sqsum[:, :], ACT.Sqrt, bias=e.eps[:, 0:1],
                               scale=1.0 / P).then_inc(root_ok, 1)

            @block.vector
            def _(v):
                v.wait_ge(root_ok, 1)
                v.reciprocal(e.rstd[:, :], e.rstd[:, :]).then_inc(rstd_ok, 1)
                v.wait_ge(rstd_ok, 1)

            @block.tensor
            def _(pe):
                pe.wait_ge(rstd_ok, 1)

            @block.gpsimd
            def _(pool):
                pool.wait_ge(rstd_ok, 1)

            @block.sync
            def _(sp):
                sp.wait_ge(rstd_ok, 1)


def normalise(nc, e, tag, last=False):
    c = ExitStack()
    with c:
        root_ok, rstd_ok, scaled, stored = (c.enter_context(nc.semaphore(tag + k)) for k in (
            "root_ok", "rstd_ok", "scaled", "stored"))
        with nc.Block() as block:
            @block.scalar
            def _(act):
                act.activation(e.rstd[:, :], e.sqsum[:, :], ACT.Sqrt, bias=e.eps[:, 0:1],
                               scale=1.0 / P).then_inc(root_ok, 1)

            @block.vector
            def _(v):
                v.wait_ge(root_ok, 1)
                v.reciprocal(e.rstd[:, :], e.rstd[:, :]).then_inc(rstd_ok, 1)
                v.wait_ge(rstd_ok, 1)
                with v.Fori(0, NG) as n:
                    part = e.cur[:, bass.ds(n * G, G), :]
                    v.tensor_tensor(part, part, e.rstd[:, bass.ds(n * G, G)].unsqueeze(2).broadcast_to([P, G, P]),
                                    ALU.mult).then_inc(scaled, 1)

            @block.tensor
            def _(pe):
                pe.wait_ge(rstd_ok, 1)

            @block.gpsimd
            def _(pool):
                pool.wait_ge(rstd_ok, 1)

            @block.sync
            def _(sp):
                sp.wait_ge(rstd_ok, 1)
                if last:
                    with sp.Fori(0, NG) as n:
                        sp.wait_ge(scaled, n + 1)
                        sp.dma_start(e.out_v[:, bass.ds(n * G, G), :], e.cur[:, bass.ds(n * G, G), :]).then_inc(stored, 16)
                    sp.wait_ge(stored, 16 * NG)


def adjacency_stack(nc, x, adj, Wq, Wk, Wv, W_l, W_r, w_attn, W1, b1, W2, b2, gamma, beta,
                    weight, bias, out):
    ctx = ExitStack()
    with ctx:
        def sb(name, shape, dt=F32):
            return ctx.enter_context(nc.sbuf_tensor(name, shape, dt))

        def pb(name, shape, dt=F32):
            return ctx.enter_context(nc.psum_tensor(name, shape, dt))

        def sem(name):
            return ctx.enter_context(nc.semaphore(name))

        x_v = x.rearrange("b n f -> n b f")
        adj_v = adj.rearrange("b n m -> n b m")
        out_v = out.rearrange("b n f -> n b f")

        cur = sb("cur", [P, B, P])
        sqsum = sb("sqsum", [P, B])
        rstd = sb("rstd", [P, B])
        eps = sb("eps", [P, 1])
        ident = sb("ident", [P, P])
        M = sb("M", [P, P])
        WvT = sb("WvT", [P, P])
        W1s = sb("W1s", [P, 2, P])
        W2c = sb("W2c", [P, P])
        b2c = sb("b2c", [P, P])
        b1c = sb("b1c", [P, 1])
        gam = sb("gam", [P, P])
        bet = sb("bet", [P, P])
        W3 = sb("W3", [P, P])
        bia = sb("bia", [P, P])
        hsel = sb("hsel", [P, HEADS])
        wcol = sb("wcol", [P, 1])
        WlrT = sb("WlrT", [P, 2, P])
        put_w = sb("put_w", [P, Q, 2 * Q * HEADS])
        put_m = sb("put_m", [P, Q, 2 * Q * HEADS], F32R)
        ones = sb("ones", [P, P])
        ones3 = sb("ones3", [3, P], BF16)
        b2x = sb("b2x", [3, P], BF16)
        number1 = sb("number1", [P, ECAP])
        deg = sb("deg", [P, 2, B])
        first = sb("first", [P, B])
        end = sb("end", [P, B])
        general = sb("general", [P, 1], I32)

        banks = [pb(f"bank{i}", [P, 512]) for i in range(5)]
        wide = pb("wide", [P, 3 * 512])
        banks += [wide[:, 512 * i:512 * (i + 1)] for i in range(3)]

        with ExitStack() as c0:
            raw = c0.enter_context(nc.sbuf_tensor("raw", [P, 5, P], F32))
            b2r = c0.enter_context(nc.sbuf_tensor("b2r", [P, P], F32))
            rmean = c0.enter_context(nc.sbuf_tensor("rmean", [P, 2], F32))
            weights_in = sem("weights_in")
            masks = sem("masks")
            w_ready = sem("w_ready")
            w_seq = sem("w_seq")
            tri = c0.enter_context(nc.sbuf_tensor("tri", [P, P], F32))
            mk = c0.enter_context(nc.sbuf_tensor("mk", [P, 1], F32))
            zero = c0.enter_context(nc.sbuf_tensor("zero", [P, Q * 2 * Q * HEADS], F32))
            bp = c0.enter_context(nc.sbuf_tensor("bp", [P, 3, P], F32))
            bh = c0.enter_context(nc.sbuf_tensor("bh", [P, 3, P], BF16))
            pick = c0.enter_context(nc.sbuf_tensor("pick", [3, 3, P], F32))
            with nc.Block() as block:
                @block.sync
                def _(sp):
                    for k, w in enumerate((Wq, Wk, Wv, W_l, W_r)):
                        sp.dma_start(raw[:, k, :], w).then_inc(weights_in, 16)
                    sp.dma_start(W1s[:, 0, :], W1[P:2 * P, :]).then_inc(weights_in, 16)
                    sp.dma_start(W1s[:, 1, :], W1[0:P, :]).then_inc(weights_in, 16)
                    sp.dma_start(W2c[:, :], W2).then_inc(weights_in, 16)
                    sp.dma_start(W3[:, :], weight).then_inc(weights_in, 16)
                    for dst, v in ((b2r, b2), (gam, gamma), (bet, beta), (bia, bias)):
                        sp.dma_start(dst[:, :], v.partition_broadcast(P)).then_inc(weights_in, 16)
                    sp.dma_start(b1c[:, :], b1.rearrange("(k a) -> k a", a=1)).then_inc(weights_in, 16)
                    for h in range(HEADS):
                        sp.dma_start(wcol[HF * h:HF * (h + 1), :],
                                     w_attn.rearrange("(f a) -> f a", a=1)).then_inc(weights_in, 16)

                NW = 16 * (14 + HEADS)

                @block.gpsimd
                def _(pool):
                    for t, v in ((ident, 0.0), (eps, EPS)):
                        pool.memset(t[:, :], v).then_inc(masks, 1)
                    pool.memset(hsel[:, :], 1.0).then_inc(masks, 1)
                    pool.memset(tri[:, :], 1.0).then_inc(masks, 1)
                    pool.memset(ones[:, :], 1.0).then_inc(masks, 1)
                    pool.memset(ones3[:, :], 1.0).then_inc(masks, 1)
                    pool.memset(zero[:, :], 0.0).then_inc(masks, 1)
                    pool.memset(number1[:, :], 1.0).then_inc(masks, 1)
                    pool.wait_ge(masks, 8)
                    pool.affine_select(out=tri[:, :], in_=tri[:, :], compare_op=ALU.is_ge, fill=0.0,
                                       base=0, pattern=[[1, P]], channel_multiplier=-1).then_inc(masks, 1)
                    pool.affine_select(out=ident[:, :], in_=ident[:, :], compare_op=ALU.not_equal, fill=1.0,
                                       base=0, pattern=[[-1, P]], channel_multiplier=1).then_inc(masks, 1)
                    pool.affine_select(out=hsel[:, :], in_=hsel[:, :], compare_op=ALU.is_ge, fill=0.0,
                                       base=0, pattern=[[-HF, HEADS]], channel_multiplier=1).then_inc(masks, 1)
                    pool.wait_ge(masks, 11)
                    pool.affine_select(out=hsel[:, :], in_=hsel[:, :], compare_op=ALU.is_ge, fill=0.0,
                                       base=HF - 1, pattern=[[HF, HEADS]], channel_multiplier=-1).then_inc(masks, 1)

                @block.tensor
                def _(pe):
                    pe.wait_ge(weights_in, NW)
                    pe.wait_ge(masks, 12)
                    pe.matmul(banks[0][:, 0:P], raw[:, 0, :], raw[:, 1, :], start=True, stop=True)
                    pe.transpose(banks[0][:, P:2 * P], raw[:, 2, :], ident[:, :])
                    pe.transpose(banks[0][:, 2 * P:3 * P], raw[:, 3, :], ident[:, :])
                    pe.transpose(banks[0][:, 3 * P:4 * P], raw[:, 4, :], ident[:, :]).then_inc(w_ready, 1)

                @block.vector
                def _(v):
                    q = Steps(v, w_seq)
                    v.wait_ge(masks, 12)
                    v.wait_ge(weights_in, NW)
                    v.wait_ge(w_ready, 1)
                    v.tensor_scalar(M[:, :], banks[0][:, 0:P], float(P) ** -0.5, None, ALU.mult)
                    v.tensor_copy(WvT[:, :], banks[0][:, P:2 * P])
                    v.tensor_copy(WlrT[:, :, :], banks[0][:, 2 * P:4 * P].rearrange("p (a f) -> p a f", a=2))
                    q.add(v.tensor_tensor_scan(number1[:, :], number1[:, :], number1[:, :], 0.0, ALU.mult, ALU.add))
                    q.add(v.tensor_copy(put_w[:, :, :].rearrange("p q c -> p (q c)"), zero[:, :]))
                    q.add(v.tensor_copy(put_m[:, :, :].rearrange("p q c -> p (q c)"), zero[:, :]))
                    q.add(v.tensor_reduce(mk[:, :], tri[:, :], AX.X, ALU.add))
                    q.wait()
                    q.add(v.tensor_scalar(mk[:, :], mk[:, :], MARK, None, ALU.mult))
                    q.wait()
                    H = Q * HEADS
                    for k in range(Q):
                        q.add(v.tensor_scalar(put_w[:, k, HEADS * k:HEADS * (k + 1)], hsel[:, :], wcol[:, 0:1], None, ALU.mult))
                        q.add(v.tensor_copy(put_m[:, k, H + HEADS * k:H + HEADS * (k + 1)], mk[:, :].broadcast_to([P, HEADS])))
                    q.add(v.tensor_reduce(rmean[:, 0:1], W2c[:, :], AX.X, ALU.add))
                    q.add(v.tensor_reduce(rmean[:, 1:2], b2r[:, :], AX.X, ALU.add))
                    q.wait()
                    q.add(v.tensor_scalar(rmean[:, :], rmean[:, :], -1.0 / P, None, ALU.mult))
                    q.wait()
                    q.add(v.tensor_scalar(W2c[:, :], W2c[:, :], rmean[:, 0:1], None, ALU.add))
                    q.add(v.tensor_scalar(b2c[:, :], b2r[:, :], rmean[:, 1:2], None, ALU.add))
                    q.wait()
                    q.add(v.tensor_copy(bh[:, 0, :], b2c[:, :]))
                    q.wait()
                    q.add(v.tensor_tensor(bp[:, 0, :], b2c[:, :], bh[:, 0, :], ALU.subtract))
                    q.wait()
                    q.add(v.tensor_copy(bh[:, 1, :], bp[:, 0, :]))
                    q.wait()
                    q.add(v.tensor_tensor(bp[:, 1, :], bp[:, 0, :], bh[:, 1, :], ALU.subtract))
                    q.wait()
                    q.add(v.tensor_copy(bh[:, 2, :], bp[:, 1, :]))
                    q.wait()
                    q.add(v.tensor_scalar(pick[:, 0, :], bh[0:3, 0, :], ident[0:3, 0:1], None, ALU.mult))
                    q.wait()
                    for k in (1, 2):
                        q.add(v.scalar_tensor_tensor(pick[:, k, :], bh[0:3, k, :], ident[0:3, k:k + 1], pick[:, k - 1, :],
                                                     ALU.mult, ALU.add))
                        q.wait()
                    q.add(v.tensor_copy(b2x[:, :], pick[:, 2, :]))
                    q.wait()

        e = Shared()
        e.cur = cur
        e.sqsum = sqsum
        e.rstd = rstd
        e.eps = eps
        e.ident = ident
        e.M = M
        e.WvT = WvT
        e.W1s = W1s
        e.W2c = W2c
        e.b2c = b2c
        e.b1c = b1c
        e.gam = gam
        e.bet = bet
        e.W3 = W3
        e.bia = bia
        e.hsel = hsel
        e.wcol = wcol
        e.WlrT = WlrT
        e.put_w = put_w
        e.put_m = put_m
        e.ones = ones
        e.ones3 = ones3
        e.b2x = b2x
        e.number1 = number1
        e.deg = deg
        e.first = first
        e.end = end
        e.general = general
        e.wide = wide
        e.banks = banks
        e.x_v = x_v
        e.adj_v = adj_v
        e.out_v = out_v
        layer0(nc, e)
        prepare(nc, e)
        flag = nc.values_load(general[0:1, 0:1], min_val=0, max_val=1)
        before = nc.snapshot_sems()
        with nc.If(flag > 0):
            middle_general(nc, e)
        nc.restore_sems(before)
        with nc.Else():
            middle_packed(nc, e)
        nc.end_ifs()
        layer3(nc, e)
        normalise(nc, e, "d_", last=True)


def middle_general(nc, e):
    normalise(nc, e, "na_")
    layer1_dense(nc, e)
    normalise(nc, e, "nb_")
    layer2_dense(nc, e)
    normalise(nc, e, "nc_")


def middle_packed(nc, e):
    roots(nc, e, "ra_")
    layer1_packed(nc, e)
    roots(nc, e, "rb_")
    layer2_packed(nc, e)
    normalise(nc, e, "nd_")



_INS = ['x', 'adj', 'L0_gnn_Wq', 'L0_gnn_Wk', 'L0_gnn_Wv', 'L1_gnn_W_l', 'L1_gnn_W_r', 'L1_gnn_w_attn',
        'L2_gnn_W1', 'L2_gnn_b1', 'L2_gnn_W2', 'L2_gnn_b2', 'L2_gnn_gamma', 'L2_gnn_beta',
        'L3_gnn_weight', 'L3_gnn_bias']
_OUTS = [((B, P, P), 'float32')]


def kernel(**inputs):
    import numpy as _np
    import concourse.bacc as _bacc
    from concourse import mybir as _mybir
    from concourse.bass_utils import run_bass_kernel_spmd as _run

    nc = _bacc.Bacc("TRN2", target_bir_lowering=False, num_devices=1)
    arrays, args = {}, []
    for name in _INS:
        a = _np.ascontiguousarray(inputs[name])
        arrays[f"in_{name}_dram"] = a
        args.append(nc.dram_tensor(f"in_{name}_dram", a.shape, _mybir.dt.from_np(a.dtype), kind="ExternalInput").ap())
    for i, (shape, dtype) in enumerate(_OUTS):
        dt = _mybir.dt.from_np(_np.dtype(dtype))
        args.append(nc.dram_tensor(f"out_{i}_dram", shape, dt, kind="ExternalOutput").ap())
    adjacency_stack(nc, *args)
    r = _run(nc, [arrays], core_ids=[0])
    got = tuple(r.results[0][f"out_{i}_dram"] for i in range(len(_OUTS)))
    return got[0]
```

```python
from contextlib import ExitStack

import concourse.bass as bass
from concourse import mybir

F32 = mybir.dt.float32
ALU = mybir.AluOpType
ACT = mybir.ActivationFunctionType
AX = mybir.AxisListType

P = 128
B = 64
HEADS = 8
HF = P // HEADS
SLOPE = 0.2
EPS = 1e-5
NEG = -1e30
G = 4
NG = B // G
RT = P // HEADS
NRT = P // RT
RS = 4
TILES = 10
ECAP = TILES * P
CHUNK = 512
CHUNKS = -(-ECAP // CHUNK)
Q = 4
MARK = 2.0 ** 100
LOWEST = -1e35
F32R = mybir.dt.float32r
BF16 = mybir.dt.bfloat16
I32 = mybir.dt.int32


class Shared:
    pass


class Steps:

    def __init__(self, eng, sem, base=0):
        self.eng, self.sem, self.base, self.n = eng, sem, base, 0

    def add(self, instruction):
        instruction.then_inc(self.sem, 1)
        self.n += 1

    def wait(self):
        self.eng.wait_ge(self.sem, self.base + self.n)


def group(n, inner):
    return inner or 0 <= n < NG


def every_group(eng, step, extra):
    step(0, -2, False)
    step(0, -1, False)
    for pos in range(4):
        step(0, pos, False)
    with eng.Fori(1, NG // 4 - 1) as K:
        for pos in range(4):
            step(K, pos, True)
    for n in range(NG - 4, NG + extra):
        step(n // 4, n % 4, False)


def grp(bank):
    return bank[:, :].rearrange("p (g f) -> p g f", g=G)


def load_group(sp, e, n, b):
    sp.dma_start(e.xin[:, b, :, :], e.x_v[:, bass.ds(n * G, G), :]).then_inc(e.x_in[b], 16)
    sp.dma_start(e.ain[:, b, :, :], e.adj_v[:, bass.ds(n * G, G), :]).then_inc(e.x_in[b], 16)


def layer0(nc, e):
    c = ExitStack()
    with c:
        def sb(name, shape, dt=F32):
            return c.enter_context(nc.sbuf_tensor("a_" + name, shape, dt))

        def sem(name):
            return c.enter_context(nc.semaphore("a_" + name))

        cur, ident = e.cur, e.ident
        xin, ain, x_in = e.xin, e.ain, e.x_in
        xT = sb("xT", [P, 2, G, P])
        tT = sb("tT", [P, 2, G, P])
        xv = sb("xv", [P, 4, G, P])
        drop = sb("drop", [P, G, P])
        odd = sb("odd", [P, G, P])
        sm = sb("sm", [P, 2, G, P])
        top = sb("top", [P, 2, G])
        ex = sb("ex", [P, 2, G, P])
        den = sb("den", [P, 2, G])
        rden = sb("rden", [P, G])
        pr = sb("pr", [P, 2, G, P])
        prT = sb("prT", [P, 2, G, P])
        res = sb("res", [P, G, P])
        mean = sb("mean", [P, G])
        junk = sb("junk", [P, 2, P])
        xT_mm, xT_ok, t_mm, t_ok, xv_mm, xv_ok, s_mm = (sem(k) for k in (
            "xT_mm", "xT_ok", "t_mm", "t_ok", "xv_mm", "xv_ok", "s_mm"))
        top_ok, ex_ok, pr_ok, prT_mm, prT_ok, o_mm, cen_ok, sq_ok = (sem(k) for k in (
            "top_ok", "ex_ok", "pr_ok", "prT_mm", "prT_ok", "o_mm", "cen_ok", "sq_ok"))
        res_ok, seq_f, seq_b = sem("res_ok"), sem("seq_f"), sem("seq_b")
        bX, bT, bV, bS, bP, bO = e.banks[:6]

        with nc.Block() as block:
            @block.sync
            def _(sp):
                with sp.Fori(1, NG // 4) as k:
                    for b in range(4):
                        sp.wait_ge(res_ok, 4 * k + b - 3)
                        load_group(sp, e, 4 * k + b, b)

            @block.tensor
            def _(pe):
                def step(K, pos, inner):
                    n = 4 * K + pos
                    if group(n + 1, inner):
                        h, b = n + 1, (pos + 1) % 2
                        pe.wait_ge(t_ok, h + 1)
                        if inner or h > 0:
                            pe.wait_ge(top_ok, h)
                        for g in range(G):
                            m = pe.matmul(bS[:, P * g:P * g + P], tT[:, b, g, :], xT[:, b, g, :], start=True, stop=True)
                        m.then_inc(s_mm, 1)
                    if group(n + 2, inner):
                        f, b = n + 2, (pos + 2) % 4
                        pe.wait_ge(x_in[b], 32 * (K + (pos + 2) // 4) + 32)
                        if inner or f > 0:
                            pe.wait_ge(xT_ok, f)
                        for g in range(G):
                            m = pe.transpose(bX[:, P * g:P * g + P], xin[:, b, g, :], ident[:, :])
                        m.then_inc(xT_mm, 1)
                    if group(n, inner):
                        pe.wait_ge(pr_ok, n + 1)
                        if inner or n > 0:
                            pe.wait_ge(prT_ok, n)
                        for g in range(G):
                            m = pe.transpose(bP[:, P * g:P * g + P], pr[:, pos % 2, g, :], ident[:, :])
                        m.then_inc(prT_mm, 1)
                    if group(n + 2, inner):
                        pe.wait_ge(xT_ok, f + 1)
                        if inner or f > 0:
                            pe.wait_ge(t_ok, f)
                            pe.wait_ge(xv_ok, f)
                        pe.matmul(bT[:, :], e.M[:, :], xT[:, pos % 2, :, :], start=True, stop=True).then_inc(t_mm, 1)
                        for g in range(G):
                            m = pe.matmul(bV[:, P * g:P * g + P], xT[:, pos % 2, g, :], e.WvT[:, :], start=True, stop=True)
                        m.then_inc(xv_mm, 1)
                    if group(n, inner):
                        pe.wait_ge(prT_ok, n + 1)
                        if inner or n > 0:
                            pe.wait_ge(res_ok, n)
                        for g in range(G):
                            m = pe.matmul(bO[:, P * g:P * g + P], prT[:, pos % 2, g, :], xv[:, pos % 4, g, :], start=True, stop=True)
                        m.then_inc(o_mm, 1)

                every_group(pe, step, 1)

            @block.scalar
            def _(act):
                def step(K, pos, inner):
                    n = 4 * K + pos
                    f, h = n + 2, n + 1
                    if group(f, inner):
                        act.wait_ge(xT_mm, f + 1)
                        if inner or f >= 2:
                            act.wait_ge(s_mm, f - 1)
                        act.copy(xT[:, pos % 2, :, :], grp(bX)).then_inc(xT_ok, 1)
                    if group(n, inner):
                        act.wait_ge(prT_mm, n + 1)
                        act.copy(prT[:, pos % 2, :, :], grp(bP)).then_inc(prT_ok, 1)
                    if group(h, inner):
                        b = (pos + 1) % 2
                        act.wait_ge(top_ok, h + 1)
                        if inner or h >= 2:
                            act.wait_ge(pr_ok, h - 1)
                        for g in range(G):
                            act.activation(ex[:, b, g, :], sm[:, b, g, :], ACT.Exp, bias=top[:, b, g:g + 1],
                                           accum_out=den[:, b, g:g + 1]).then_inc(ex_ok, 1)
                    if group(f, inner):
                        act.wait_ge(t_mm, f + 1)
                        act.copy(tT[:, pos % 2, :, :], grp(bT)).then_inc(t_ok, 1)
                        act.wait_ge(xv_mm, f + 1)
                        if inner or f >= 4:
                            act.wait_ge(o_mm, f - 3)
                        act.copy(xv[:, (pos + 2) % 4, :, :], grp(bV)).then_inc(xv_ok, 1)
                    if group(n - 1, inner):
                        act.wait_ge(cen_ok, n)
                        for g in range(G):
                            if inner or G * (n - 1) + g >= 2:
                                act.wait_ge(sq_ok, G * (n - 1) + g - 1)
                            act.activation(junk[:, g % 2, :], cur[:, (n - 1) * G + g, :], ACT.Square,
                                           accum_out=e.sqsum[:, bass.ds((n - 1) * G + g, 1)]).then_inc(sq_ok, 1)

                every_group(act, step, 1)

            @block.vector
            def _(v):
                def step(K, pos, inner):
                    n = 4 * K + pos
                    h, hb, ha = n + 1, (pos + 1) % 2, (pos + 1) % 4
                    b = pos % 2
                    r = Steps(v, seq_b, 3 * n)
                    q = Steps(v, seq_f, 5 * h)
                    if group(h, inner):
                        v.wait_ge(x_in[ha], 32 * (K + (pos + 1) // 4) + 32)
                        q.add(v.tensor_scalar(drop[:, :, :], ain[:, ha, :, :], 0.0, NEG, ALU.is_equal, ALU.mult))
                    if group(n, inner):
                        v.wait_ge(ex_ok, G * (n + 1))
                        if inner or n >= 2:
                            v.wait_ge(prT_mm, n - 1)
                        r.add(v.reciprocal(rden[:, :], den[:, b, :]))
                        r.wait()
                        for g in range(G):
                            m = v.scalar_tensor_tensor(pr[:, b, g, :], ex[:, b, g, :], rden[:, g:g + 1], ain[:, pos % 4, g, :],
                                                       ALU.mult, ALU.add)
                        m.then_inc(pr_ok, 1)
                    if group(h, inner):
                        v.wait_ge(s_mm, h + 1)
                        q.wait()
                        if inner or h >= 2:
                            v.wait_ge(ex_ok, G * (h - 1))
                        q.add(v.tensor_tensor(sm[:, hb, :, :], grp(bS), drop[:, :, :], ALU.add))
                        q.wait()
                        v.tensor_reduce(top[:, hb, :], sm[:, hb, :, :], AX.X, ALU.max, negate=True).then_inc(top_ok, 1)
                        q.add(v.scalar_tensor_tensor(odd[:, :, :], ain[:, ha, :, :], 0.0, ain[:, ha, :, :],
                                                     ALU.not_equal, ALU.not_equal))
                        q.add(v.tensor_reduce(e.deg[:, 0, bass.ds(h * G, G)], ain[:, ha, :, :], AX.X, ALU.add))
                        q.wait()
                        q.add(v.tensor_reduce(e.deg[:, 1, bass.ds(h * G, G)], odd[:, :, :], AX.X, ALU.add))
                    if group(n, inner):
                        v.wait_ge(o_mm, n + 1)
                        if inner or n > 0:
                            v.wait_ge(cen_ok, n)
                        v.tensor_tensor(res[:, :, :], grp(bO), xin[:, pos % 4, :, :], ALU.add).then_inc(res_ok, 1)
                        v.wait_ge(res_ok, n + 1)
                        r.add(v.tensor_reduce(mean[:, :], res[:, :, :], AX.X, ALU.add))
                        r.wait()
                        r.add(v.tensor_scalar(mean[:, :], mean[:, :], 1.0 / P, None, ALU.mult))
                        r.wait()
                        v.tensor_tensor(cur[:, bass.ds(n * G, G), :], res[:, :, :],
                                        mean[:, :].unsqueeze(2).broadcast_to([P, G, P]), ALU.subtract).then_inc(cen_ok, 1)

                every_group(v, step, 1)


def prepare(nc, e):
    c = ExitStack()
    with c:
        def sem(name):
            return c.enter_context(nc.semaphore("p_" + name))

        below = c.enter_context(nc.sbuf_tensor("p_below", [P, P], F32))
        ones = c.enter_context(nc.sbuf_tensor("p_ones", [P, P], F32))
        worst = c.enter_context(nc.sbuf_tensor("p_worst", [P, 2], F32))
        mask_ok, sum_mm, seq = sem("mask_ok"), sem("sum_mm"), sem("seq")
        bank = e.banks[0]
        with nc.Block() as block:
            @block.gpsimd
            def _(pool):
                pool.memset(ones[:, :], 1.0).then_inc(mask_ok, 1)
                pool.memset(below[:, :], 1.0).then_inc(mask_ok, 1)
                pool.wait_ge(mask_ok, 2)
                pool.affine_select(out=below[:, :], in_=below[:, :], compare_op=ALU.is_gt, fill=0.0,
                                   base=0, pattern=[[1, P]], channel_multiplier=-1).then_inc(mask_ok, 1)

            @block.tensor
            def _(pe):
                pe.wait_ge(mask_ok, 3)
                pe.matmul(bank[:, 0:B], below[:, :], e.deg[:, 0, :], start=True, stop=True)
                pe.matmul(bank[:, P:P + 2 * B], ones[:, :], e.deg[:, :, :], start=True, stop=True).then_inc(sum_mm, 1)

            @block.vector
            def _(v):
                q = Steps(v, seq)
                v.wait_ge(sum_mm, 1)
                q.add(v.tensor_copy(e.first[:, :], bank[:, 0:B]))
                q.add(v.tensor_scalar(e.unfirst[:, :], bank[:, 0:B], -1.0, None, ALU.mult))
                q.add(v.tensor_reduce(worst[:, 0:1], bank[:, P:P + B], AX.X, ALU.max))
                q.add(v.tensor_reduce(worst[:, 1:2], bank[:, P + B:P + 2 * B], AX.X, ALU.max))
                q.wait()
                q.add(v.tensor_tensor(e.end[:, :], e.first[:, :], e.deg[:, 0, :], ALU.add))
                q.add(v.tensor_scalar(worst[:, 0:1], worst[:, 0:1], float(ECAP), None, ALU.is_gt))
                q.add(v.tensor_scalar(worst[:, 1:2], worst[:, 1:2], 0.0, None, ALU.is_gt))
                q.wait()
                q.add(v.tensor_tensor(e.general[:, :], worst[:, 0:1], worst[:, 1:2], ALU.max))
                q.wait()


class Packed:
    pass


def packed_buffers(nc, c, tag, slots, row_slots):
    s = Packed()

    def sb(name, shape, dt=F32):
        return c.enter_context(nc.sbuf_tensor(tag + name, shape, dt))

    def sem(name):
        return c.enter_context(nc.semaphore(tag + name))

    s.slots, s.row_slots = slots, row_slots
    s.ain = sb("ain", [P, 2, P])
    s.number = sb("number", [P, P])
    s.C = sb("C", [P, 2, P], F32R)
    s.after = sb("after", [P, ECAP], BF16)
    s.SI = sb("SI", [P, 4, ECAP], F32R)
    s.SIb = sb("SIb", [P, ECAP], BF16)
    s.SJ = sb("SJ", [P, slots, ECAP], F32R)
    s.SIT = sb("SIT", [P, row_slots, TILES, P])
    s.xin = sb("xin", [P, 2, P])
    s.xT = sb("xT", [P, P])
    s.hi = sb("hi", [P, 2 * P], F32R)
    s.lo = sb("lo", [P, 2 * P], F32R)
    s.junk = sb("junk", [P, P])
    s.mean = sb("mean", [P, Q])
    s.res = sb("res", [P, Q, P])
    s.a_in = [sem(f"a_in{b}") for b in range(2)]
    s.x_ok = sem("x_ok")
    s.seq_p = sem("seq_p")
    s.after_ok = sem("after_ok")
    s.sib_ok = sem("sib_ok")
    s.c_ok = sem("c_ok")
    s.si_ok = sem("si_ok")
    s.c_mm = sem("c_mm")
    s.sj_ok = sem("sj_ok")
    s.s_mm = sem("s_mm")
    s.sit_ok = sem("sit_ok")
    s.xT_mm = sem("xT_mm")
    s.xT_ok = sem("xT_ok")
    s.p_mm = sem("p_mm")
    s.hi_ok = sem("hi_ok")
    s.lo_ok = sem("lo_ok")
    s.u_mm = sem("u_mm")
    s.cen_ok = sem("cen_ok")
    s.sq_ok = sem("sq_ok")
    return s


def chunk(k):
    return slice(CHUNK * k, min(CHUNK * (k + 1), ECAP))


def width(k):
    return chunk(k).stop - chunk(k).start


def tiles(k):
    return range(4 * k, min(4 * k + 4, TILES))


def every_step(eng, step, extra):
    step(0, -1, False)
    for pos in range(8):
        step(0, pos, False)
    with eng.Fori(1, B // 8 - 1) as K:
        for pos in range(8):
            step(K, pos, True)
    for n in range(B - 8, B + extra):
        step(n // 8, n % 8, False)


def load_adjacency(sp, e, s):
    for n in range(2):
        sp.dma_start(s.ain[:, n, :], e.adj_v[:, n, :]).then_inc(s.a_in[n], 16)
    with sp.Fori(1, B // 2) as k:
        for b in range(2):
            sp.wait_ge(s.c_ok, 2 * k + b - 1)
            sp.dma_start(s.ain[:, b, :], e.adj_v[:, 2 * k + b, :]).then_inc(s.a_in[b], 16)


def normalise_x(act, e, s, K, pos, late):
    n = 8 * K + pos
    if late:
        act.wait_ge(s.xT_mm, n - 1)
    act.activation(s.xin[:, pos % 2, :], e.cur[:, bass.ds(n, 1), :].rearrange("p a f -> p (a f)"), ACT.Copy,
                   scale=e.rstd[:, bass.ds(n, 1)]).then_inc(s.x_ok, 1)


def number_rows(v, e, s, K, pos, late):
    n, b = 8 * K + pos, pos % 2
    q = Steps(v, s.seq_p, n)
    v.wait_ge(s.a_in[b], 16 * (4 * K + pos // 2) + 16)
    if late or pos > 0:
        v.wait_ge(s.c_ok, n)
    q.add(v.tensor_tensor_scan(s.number[:, :], e.ones[:, :], s.ain[:, b, :], e.first[:, bass.ds(n, 1)], ALU.mult, ALU.add))
    if late:
        v.wait_ge(s.c_mm, 3 * n - 3)
    q.wait()
    v.tensor_tensor(s.C[:, b, :], s.number[:, :], s.ain[:, b, :], ALU.mult).then_inc(s.c_ok, 1)


def start_rows(act, e, s, K, pos, late):
    n = 8 * K + pos
    if late:
        act.wait_ge(s.si_ok, n)
    act.activation(s.after[:, :], e.number1[:, :], ACT.Relu, bias=e.unfirst[:, bass.ds(n, 1)]).then_inc(s.after_ok, 1)


def select_rows(v, e, s, K, pos, late):
    n = 8 * K + pos
    v.wait_ge(s.after_ok, n + 1)
    if late:
        v.wait_ge(s.u_mm, 3 * n - 9)
    v.scalar_tensor_tensor(s.SI[:, pos % 4, :], e.number1[:, :], e.end[:, bass.ds(n, 1)], s.after[:, :],
                           ALU.is_le, ALU.min).then_inc(s.si_ok, 1)


def shorten_rows(act, s, K, pos, late):
    n = 8 * K + pos
    act.wait_ge(s.si_ok, n + 1)
    if late:
        act.wait_ge(s.s_mm, 3 * n)
    act.copy(s.SIb[:, :], s.SI[:, pos % 4, :].bitcast(F32)).then_inc(s.sib_ok, 1)


def split_low(v, s, bank, K, pos, late, hi_count):
    n = 8 * K + pos
    v.wait_ge(s.hi_ok, hi_count * n + hi_count)
    if late:
        v.wait_ge(s.u_mm, 3 * n)
    v.tensor_tensor(s.lo[:, :], bank[:, 0:2 * P], s.hi[:, :].bitcast(F32),
                    ALU.subtract).then_inc(s.lo_ok, 1)


def number_edges(v, e, s, ring, K, pos):
    n = 8 * K + pos
    for k in range(CHUNKS):
        v.wait_ge(s.c_mm, 3 * n + k + 1)
        v.tensor_tensor(s.SJ[:, pos % s.slots, chunk(k)], ring[k][:, 0:width(k)], e.number1[:, chunk(k)],
                        ALU.is_equal).then_inc(s.sj_ok, 1)


def number_columns(pe, s, bank, pos, k):
    pe.matmul(bank[:, 0:width(k)], s.C[:, pos % 2, :], s.SI[:, pos % 4, chunk(k)], start=True, stop=True).then_inc(s.c_mm, 1)


def transpose_rows(pe, e, s, bank, k):
    for j in tiles(k):
        m = pe.matmul(bank[:, P * (j - 4 * k):P * (j - 4 * k) + P], s.SIb[:, P * j:P * j + P], e.identb[:, :],
                      start=True, stop=True)
    m.then_inc(s.s_mm, 1)


def evacuate_rows(act, s, bank, K, pos, k):
    n = 8 * K + pos
    act.wait_ge(s.s_mm, 3 * n + k + 1)
    act.copy(s.SIT[:, pos % s.row_slots, tiles(k).start:tiles(k).stop, :],
             bank[:, 0:width(k)].rearrange("p (j i) -> p j i", i=P)).then_inc(s.sit_ok, 1)


def gather_pairs(pe, s, bank, pos, k):
    w, cs, r = width(k), chunk(k), pos % 4
    pe.matmul(bank[:, 0:w], s.hi[:, 0:P], s.SJ[:, pos % s.slots, cs], start=True, stop=False)
    pe.matmul(bank[:, 0:w], s.lo[:, 0:P], s.SJ[:, pos % s.slots, cs], start=False, stop=False)
    pe.matmul(bank[:, 0:w], s.hi[:, P:2 * P], s.SI[:, r, cs], start=False, stop=False)
    pe.matmul(bank[:, 0:w], s.lo[:, P:2 * P], s.SI[:, r, cs], start=False, stop=True).then_inc(s.u_mm, 1)


def residual(v, e, s, z, i):
    part = e.cur[:, bass.ds(Q * i, Q), :]
    z.add(v.tensor_tensor(part, part, e.rstd[:, bass.ds(Q * i, Q)].unsqueeze(2).broadcast_to([P, Q, P]), ALU.mult))
    z.wait()
    z.add(v.tensor_tensor(s.res[:, :, :], s.res[:, :, :], part, ALU.add))
    z.wait()


def centre(v, e, s, z, i):
    z.add(v.tensor_reduce(s.mean[:, :], s.res[:, :, :], AX.X, ALU.add))
    z.wait()
    z.add(v.tensor_scalar(s.mean[:, :], s.mean[:, :], 1.0 / P, None, ALU.mult))
    z.wait()
    v.tensor_tensor(e.cur[:, bass.ds(Q * i, Q), :], s.res[:, :, :], s.mean[:, :].unsqueeze(2).broadcast_to([P, Q, P]),
                    ALU.subtract).then_inc(s.cen_ok, 1)


def squares(act, e, s, i, graphs):
    act.wait_ge(s.cen_ok, i + 1)
    for q in graphs:
        act.wait_ge(s.sq_ok, Q * i + q + 1)
        act.activation(s.junk[:, :], e.cur[:, Q * i + q, :], ACT.Square,
                       accum_out=e.sqsum[:, bass.ds(Q * i + q, 1)]).then_inc(s.sq_ok, 1)


def layer1_packed(nc, e):
    c = ExitStack()
    with c:
        def sb(name, shape, dt=F32):
            return c.enter_context(nc.sbuf_tensor("b_" + name, shape, dt))

        def sem(name):
            return c.enter_context(nc.semaphore("b_" + name))

        LAG = 6
        W = P + HEADS
        H = Q * HEADS
        s = packed_buffers(nc, c, "b_", 8, 8)
        grs = sb("grs", [P, 8, P])
        t = sb("t", [P, 2, CHUNK])
        vv = sb("vv", [P, 2, CHUNK])
        es = sb("es", [2 * H, ECAP])
        mark = sb("mark", [H, ECAP + 1])
        top = sb("top", [H, ECAP])
        aT = sb("aT", [P, 2, TILES, H])
        wt = sb("wt", [P, 2, TILES, W])
        os = sb("os", [P, 2, Q, W])
        rden = sb("rden", [P, Q, HEADS])
        t_ok = sem("t_ok")
        v_ok = sem("v_ok")
        e_mm = sem("e_mm")
        es_ok = sem("es_ok")
        pad_ok = sem("pad_ok")
        seq_z = sem("seq_z")
        z_ok = sem("z_ok")
        ex_ok = sem("ex_ok")
        at_mm = sem("at_mm")
        at_ok = sem("at_ok")
        g_mm = sem("g_mm")
        w_ok = sem("w_ok")
        wa_ok = sem("wa_ok")
        o_mm = sem("o_mm")
        os_ok = sem("os_ok")
        seq_c = sem("seq_c")
        ring = e.banks[0:3]
        bU = e.banks[3:5]
        bE = e.wide

        def scored(n, inner):
            return inner or 0 <= n < B

        def summed(n, inner):
            return inner or LAG <= n < B + LAG

        def maximised(n, pos, inner):
            return pos % Q == 0 and (inner or Q <= n <= B)

        def softened(n, pos, inner):
            return pos % Q == 1 and (inner or Q < n <= B + 1)

        def transposed(n, pos, inner):
            return pos % Q == 2 and (inner or Q < n <= B + 2)

        def finished(n, pos, inner):
            return pos % Q == 2 and (inner or n >= Q + LAG)

        def centred(n, pos, inner):
            return pos % Q == 3 and (inner or n >= Q + LAG)

        def batches(K, pos):
            return 8 // Q * K + pos // Q

        def softmaxes(K, pos):
            return 8 // Q * K + (pos - LAG) // Q + 1

        def parity(pos):
            return ((pos - LAG) // Q) % 2

        def pair_bank(pos, k):
            return bU[(pos + k) % 2]

        with nc.Block() as block:
            @block.sync
            def _(sp):
                load_adjacency(sp, e, s)

            @block.gpsimd
            def _(pool):
                pool.memset(s.junk[:, :], 0.0).then_inc(s.sq_ok, 1)
                pool.memset(mark[:, 0:1], 0.0).then_inc(pad_ok, 1)
                pool.memset(mark[:, ECAP:ECAP + 1], 0.0).then_inc(pad_ok, 1)

            @block.tensor
            def _(pe):
                def transpose_exponentials(half):
                    for j in range(TILES // 2 * half, TILES // 2 * (half + 1)):
                        o = pe.matmul(ring[2][:, H * j:H * j + H], top[:, P * j:P * j + P], e.ident[0:H, 0:H],
                                      start=True, stop=True)
                    return o

                def step(K, pos, inner):
                    n = 8 * K + pos
                    g = n + 1
                    m, ms = n - LAG, (pos - LAG) % 8
                    A, N, S = scored(n, inner), scored(n + 1, inner), summed(n, inner)

                    def gather(k):
                        if inner or 3 * n + k >= 2:
                            pe.wait_ge(v_ok, 3 * n + k - 1)
                        gather_pairs(pe, s, pair_bank(pos, k), pos, k)

                    def score(k):
                        pe.wait_ge(v_ok, 3 * n + k + 1)
                        out = bE[0:2 * H, chunk(k)]
                        pe.matmul(out, e.put_w[:, pos % Q, :], vv[:, (pos + k) % 2, 0:width(k)], start=(pos % Q == 0), stop=False)
                        pe.matmul(out, e.put_m[:, pos % Q, :], s.SI[:, pos % 4, chunk(k)], start=False,
                                  stop=(pos % Q == Q - 1)).then_inc(e_mm, 1)

                    if A:
                        pe.wait_ge(s.lo_ok, n + 1)
                        pe.wait_ge(s.sj_ok, 3 * n + 3)
                        gather(0)
                    if transposed(n, pos, inner):
                        pe.wait_ge(ex_ok, batches(K, pos))
                        if A:
                            pe.wait_ge(s.sit_ok, 3 * n + 2)
                        if inner or m > 0:
                            pe.wait_ge(w_ok, 3 * m)
                        transpose_exponentials(0)
                    if A:
                        gather(1)
                    if transposed(n, pos, inner):
                        transpose_exponentials(1).then_inc(at_mm, 1)
                    if inner or 0 <= n < B:
                        pe.wait_ge(s.sit_ok, 3 * n + 3)
                    if S:
                        if inner or m > 0:
                            pe.wait_ge(w_ok, 3 * m)
                            pe.wait_ge(os_ok, m)
                        for k in range(CHUNKS):
                            if k == 2 and transposed(n, pos, inner):
                                pe.wait_ge(at_ok, batches(K, pos))
                            for j in tiles(k):
                                d = pe.matmul(ring[k][:, P * (j - 4 * k):P * (j - 4 * k) + P],
                                              s.SJ[:, ms, P * j:P * j + P].bitcast(F32), grs[:, ms, :], start=True, stop=True)
                            d.then_inc(g_mm, 1)
                    if A:
                        if pos % Q == 0 and (inner or n > 0):
                            pe.wait_ge(es_ok, batches(K, pos))
                        score(0)
                    if N:
                        pe.wait_ge(s.x_ok, g + 1)
                        if A:
                            pe.wait_ge(v_ok, 3 * n + 2)
                        pe.transpose(pair_bank(pos, 1)[:, 0:P], s.xin[:, (pos + 1) % 2, :], e.ident[:, :]).then_inc(s.xT_mm, 1)
                    if A:
                        gather(2)
                    if N:
                        pe.wait_ge(s.c_ok, g + 1)
                        pe.wait_ge(s.si_ok, g + 1)
                        for k in range(CHUNKS):
                            if S:
                                pe.wait_ge(w_ok, 3 * m + k + 1)
                            elif k == 2 and transposed(n, pos, inner):
                                pe.wait_ge(at_ok, batches(K, pos))
                            number_columns(pe, s, ring[k], pos + 1, k)
                    if A:
                        score(1)
                    if N:
                        pe.wait_ge(s.xT_ok, g + 1)
                        pe.matmul(pair_bank(pos, 1)[:, 0:2 * P], s.xT[:, :], e.WlrT[:, :, :], start=True, stop=True).then_inc(s.p_mm, 1)
                    if A:
                        score(2)
                    if S:
                        pe.wait_ge(w_ok, 3 * m + 3)
                        pe.wait_ge(wa_ok, m + 1)
                        if N:
                            pe.wait_ge(s.sj_ok, 3 * g + 1)
                        for j in range(TILES):
                            d = pe.matmul(ring[0][:, 0:W], s.SIT[:, ms, j, :], wt[:, (pos - LAG) % 2, j, :],
                                          start=(j == 0), stop=(j == TILES - 1))
                        d.then_inc(o_mm, 1)
                    if N:
                        pe.wait_ge(s.sib_ok, g + 1)
                        pe.wait_ge(s.sj_ok, 3 * g + 2)
                        transpose_rows(pe, e, s, ring[1], 0)
                        pe.wait_ge(s.sj_ok, 3 * g + 3)
                        transpose_rows(pe, e, s, ring[2], 1)
                        if S:
                            pe.wait_ge(os_ok, m + 1)
                        transpose_rows(pe, e, s, ring[0], 2)

                every_step(pe, step, LAG + 3)

            @block.scalar
            def _(act):
                normalise_x(act, e, s, 0, 0, False)
                start_rows(act, e, s, 0, 0, False)

                def step(K, pos, inner):
                    n = 8 * K + pos
                    g = n + 1
                    m = n - LAG
                    i = batches(K, pos)
                    A, N, N2, S = scored(n, inner), scored(n + 1, inner), scored(n + 2, inner), summed(n, inner)

                    def slope(k):
                        act.wait_ge(s.u_mm, 3 * n + k + 1)
                        if inner or 3 * n + k >= 2:
                            act.wait_ge(v_ok, 3 * n + k - 1)
                        act.mul(t[:, (pos + k) % 2, 0:width(k)], pair_bank(pos, k)[:, 0:width(k)], SLOPE).then_inc(t_ok, 1)

                    if A:
                        slope(0)
                    if transposed(n, pos, inner):
                        act.wait_ge(at_mm, i)
                        act.copy(aT[:, (pos // Q + 1) % 2, :, :],
                                 ring[2][:, 0:TILES * H].rearrange("p (j c) -> p j c", c=H)).then_inc(at_ok, 1)
                    if A:
                        slope(1)
                    if maximised(n, pos, inner):
                        act.wait_ge(e_mm, 3 * n)
                        if inner or n > Q:
                            act.wait_ge(z_ok, i - 1)
                        act.copy(es[:, :], bE[0:2 * H, 0:ECAP]).then_inc(es_ok, 1)
                    if S:
                        q = (pos - LAG) % Q
                        act.wait_ge(at_ok, softmaxes(K, pos))
                        if inner or m >= 2:
                            act.wait_ge(o_mm, m - 1)
                        act.copy(wt[:, (pos - LAG) % 2, :, P:W],
                                 aT[:, parity(pos), :, HEADS * q:HEADS * (q + 1)]).then_inc(wa_ok, 1)
                    if N:
                        shorten_rows(act, s, K, pos + 1, inner or g >= 1)
                        act.wait_ge(s.xT_mm, g + 1)
                        act.copy(s.xT[:, :], pair_bank(pos, 1)[:, 0:P]).then_inc(s.xT_ok, 1)
                    if A:
                        slope(2)
                    if N2:
                        start_rows(act, e, s, K, pos + 2, True)
                    if N:
                        act.wait_ge(s.p_mm, g + 1)
                        if inner or g >= 1:
                            act.wait_ge(s.u_mm, 3 * g)
                        act.copy(s.hi[:, :], pair_bank(pos, 1)[:, 0:2 * P]).then_inc(s.hi_ok, 1)
                        if inner or g >= 8:
                            act.wait_ge(g_mm, 3 * g - 21)
                        act.copy(grs[:, (pos + 1) % 8, :], pair_bank(pos, 1)[:, P:2 * P]).then_inc(s.hi_ok, 1)
                    if N2:
                        normalise_x(act, e, s, K, pos + 2, inner or n >= 0)
                    if softened(n, pos, inner):
                        act.wait_ge(z_ok, i)
                        act.activation(top[:, :], top[:, :], ACT.Exp).then_inc(ex_ok, 1)
                    if centred(n, pos, inner):
                        squares(act, e, s, i - 2, range(Q))
                    if S:
                        act.wait_ge(o_mm, m + 1)
                        if (pos - LAG) % Q == 0 and (inner or m >= 2 * Q):
                            act.wait_ge(s.cen_ok, i - 2)
                        act.copy(os[:, parity(pos), (pos - LAG) % Q, :], ring[0][:, 0:W]).then_inc(os_ok, 1)
                    if N:
                        if inner or g >= 8:
                            act.wait_ge(o_mm, g - 7)
                        for k in range(CHUNKS):
                            evacuate_rows(act, s, ring[(k + 1) % 3], K, pos + 1, k)

                every_step(act, step, LAG + 3)

            @block.vector
            def _(v):
                number_rows(v, e, s, 0, 0, False)
                select_rows(v, e, s, 0, 0, False)

                def step(K, pos, inner):
                    n = 8 * K + pos
                    g = n + 1
                    m, q, b = n - LAG, (pos - LAG) % Q, (pos - LAG) % 2
                    i = batches(K, pos)
                    A, N, N2, S = scored(n, inner), scored(n + 1, inner), scored(n + 2, inner), summed(n, inner)

                    def bend(k):
                        v.wait_ge(t_ok, 3 * n + k + 1)
                        if inner or 3 * n + k >= 2:
                            v.wait_ge(e_mm, 3 * n + k - 1)
                        w, b = width(k), (pos + k) % 2
                        v.tensor_tensor(vv[:, b, 0:w], bU[b][:, 0:w], t[:, b, 0:w], ALU.max).then_inc(v_ok, 1)

                    z = Steps(v, seq_z, 3 * (i - 1))
                    if softened(n, pos, inner):
                        z.n = 3
                    if N2:
                        number_rows(v, e, s, K, pos + 2, inner or n >= 0)
                    if A:
                        bend(0)
                        bend(1)
                    if S:
                        v.wait_ge(at_ok, softmaxes(K, pos))
                        if inner or m >= 2:
                            v.wait_ge(o_mm, m - 1)
                        for k in range(CHUNKS):
                            r = len(tiles(k))
                            v.wait_ge(g_mm, 3 * m + k + 1)
                            att = aT[:, parity(pos), 4 * k:4 * k + r, HEADS * q:HEADS * (q + 1)]
                            v.tensor_tensor(wt[:, b, 4 * k:4 * k + r, 0:P].rearrange("p r (h f) -> p r h f", h=HEADS),
                                            ring[k][:, 0:P * r].rearrange("p (r h f) -> p r h f", r=r, h=HEADS),
                                            att.unsqueeze(3).broadcast_to([P, r, HEADS, HF]), ALU.mult).then_inc(w_ok, 1)
                    if finished(n, pos, inner):
                        part = os[:, (pos // Q) % 2, :, :]
                        f = Steps(v, seq_c, 7 * (i - 2))
                        v.wait_ge(os_ok, n - LAG)
                        f.add(v.reciprocal(rden[:, :, :], part[:, :, P:W]))
                        f.wait()
                        f.add(v.tensor_tensor(s.res[:, :, :].rearrange("p q (h f) -> p q h f", h=HEADS),
                                              part[:, :, 0:P].rearrange("p q (h f) -> p q h f", h=HEADS),
                                              rden[:, :, :].unsqueeze(3).broadcast_to([P, Q, HEADS, HF]), ALU.mult))
                        f.wait()
                        f.add(v.scalar_tensor_tensor(s.res[:, :, :], s.res[:, :, :], SLOPE, s.res[:, :, :], ALU.mult, ALU.max))
                    if centred(n, pos, inner):
                        f = Steps(v, seq_c, 7 * (i - 2))
                        f.n = 3
                        f.wait()
                        residual(v, e, s, f, i - 2)
                        centre(v, e, s, f, i - 2)
                    if softened(n, pos, inner):
                        z.wait()
                        v.tensor_tensor(top[:, :], es[0:H, :], top[:, :], ALU.subtract).then_inc(z_ok, 1)
                    if maximised(n, pos, inner):
                        v.wait_ge(es_ok, i)
                        v.wait_ge(pad_ok, 2)
                        z.add(v.tensor_tensor(mark[:, 1:ECAP], es[H:2 * H, 1:ECAP], es[H:2 * H, 0:ECAP - 1], ALU.subtract))
                    if A:
                        bend(2)
                    if maximised(n, pos, inner):
                        z.wait()
                        if inner or n > Q:
                            v.wait_ge(at_mm, i - 1)
                        z.add(v.tensor_tensor_scan(top[:, :], mark[:, 0:ECAP], es[0:H, :], LOWEST, ALU.add, ALU.max))
                    if N:
                        if inner or g >= 8:
                            v.wait_ge(g_mm, 3 * g - 21)
                        number_edges(v, e, s, ring, K, pos + 1)
                        split_low(v, s, pair_bank(pos, 1), K, pos + 1, inner or g >= 1, 2)
                    if N2:
                        select_rows(v, e, s, K, pos + 2, inner or n + 2 >= 4)
                    if maximised(n, pos, inner):
                        z.wait()
                        z.add(v.tensor_tensor_scan(top[:, ECAP - 1::-1], mark[:, ECAP:0:-1], top[:, ECAP - 1::-1],
                                                   LOWEST, ALU.add, ALU.max))

                every_step(v, step, LAG + 3)


def layer2_packed(nc, e):
    c = ExitStack()
    with c:
        def sb(name, shape, dt=F32):
            return c.enter_context(nc.sbuf_tensor("c_" + name, shape, dt))

        def sem(name):
            return c.enter_context(nc.semaphore("c_" + name))

        s = packed_buffers(nc, c, "c_", 2, 4)
        h = sb("h", [P, 2, CHUNK])
        ysq = sb("ysq", [P, 2, CHUNK])
        var = sb("var", [P, 2, 4])
        z = sb("z", [P, 2, TILES, P])
        bb = sb("bb", [P, Q, P])
        h_ok = sem("h_ok")
        y_mm = sem("y_mm")
        ysq_ok = sem("ysq_ok")
        sum_ok = sem("sum_ok")
        root_ok = sem("root_ok")
        inv_ok = sem("inv_ok")
        z_ok = sem("z_ok")
        o_mm = sem("o_mm")
        o_read = sem("o_read")
        seq_c = sem("seq_c")
        ring = e.banks[0:3]
        bU = e.banks[3:5]
        bY = e.banks[5:7]
        bO = e.banks[7]

        def gathered(n, inner):
            return inner or 0 <= n < B

        def summed(n, inner):
            return inner or 1 <= n <= B

        def part(n, pos, inner, k):
            return pos % Q == k % Q and (inner or Q + k <= n <= B + k)

        def batches(K, pos):
            return 8 // Q * K + pos // Q

        def pair_bank(pos, k):
            return bU[(pos + k) % 2]

        with nc.Block() as block:
            @block.sync
            def _(sp):
                load_adjacency(sp, e, s)

            @block.gpsimd
            def _(pool):
                pool.memset(s.junk[:, :], 0.0).then_inc(s.sq_ok, 1)

            @block.tensor
            def _(pe):
                def step(K, pos, inner):
                    n = 8 * K + pos
                    g = n + 1
                    A, N, S = gathered(n, inner), gathered(n + 1, inner), summed(n, inner)

                    def gather(k):
                        if inner or 3 * n + k >= 2:
                            pe.wait_ge(h_ok, 3 * n + k - 1)
                        gather_pairs(pe, s, pair_bank(pos, k), pos, k)

                    def mlp(k):
                        b = (pos + k) % 2
                        pe.wait_ge(h_ok, 3 * n + k + 1)
                        if inner or 3 * n + k >= 2:
                            pe.wait_ge(z_ok, 3 * n + k - 1)
                        for j in tiles(k):
                            a = P * (j - 4 * k)
                            pe.matmul(bY[b][:, a:a + P], e.ones3[:, :], e.b2x[:, :], start=True, stop=False)
                            d = pe.matmul(bY[b][:, a:a + P], h[:, b, a:a + P], e.W2c[:, :], start=False, stop=True)
                        d.then_inc(y_mm, 1)

                    if A:
                        pe.wait_ge(s.lo_ok, n + 1)
                        gather(0)
                        gather(1)
                    if N:
                        pe.wait_ge(s.c_ok, g + 1)
                        pe.wait_ge(s.si_ok, g + 1)
                        if A:
                            pe.wait_ge(s.sit_ok, 3 * g)
                        for k in range(CHUNKS):
                            number_columns(pe, s, ring[k], pos + 1, k)
                    if A:
                        mlp(0)
                    if N:
                        pe.wait_ge(s.x_ok, g + 1)
                        if A:
                            pe.wait_ge(h_ok, 3 * n + 2)
                        pe.transpose(pair_bank(pos, 1)[:, 0:P], s.xin[:, (pos + 1) % 2, :], e.ident[:, :]).then_inc(s.xT_mm, 1)
                    if A:
                        gather(2)
                        mlp(1)
                    if N:
                        pe.wait_ge(s.xT_ok, g + 1)
                        pe.matmul(pair_bank(pos, 1)[:, 0:2 * P], s.xT[:, :], e.W1s[:, :, :], start=True, stop=True).then_inc(s.p_mm, 1)
                    if S:
                        m, a = n - 1, P * ((pos - 1) % Q)
                        pe.wait_ge(z_ok, 3 * n)
                        if (pos - 1) % Q == 0 and (inner or m >= Q):
                            pe.wait_ge(o_read, batches(K, pos))
                        for j in range(TILES):
                            d = pe.matmul(bO[:, a:a + P], s.SIT[:, (pos - 1) % 4, j, :], z[:, (pos - 1) % 2, j, :],
                                          start=(j == 0), stop=(j == TILES - 1))
                        d.then_inc(o_mm, 1)
                    if N:
                        pe.wait_ge(s.sib_ok, g + 1)
                        for k in range(CHUNKS):
                            pe.wait_ge(s.sj_ok, 3 * g + k + 1)
                            transpose_rows(pe, e, s, ring[k], k)
                    if A:
                        mlp(2)

                every_step(pe, step, 7)

            @block.scalar
            def _(act):
                normalise_x(act, e, s, 0, 0, False)
                start_rows(act, e, s, 0, 0, False)

                def step(K, pos, inner):
                    n = 8 * K + pos
                    g = n + 1
                    A, N, N2 = gathered(n, inner), gathered(n + 1, inner), gathered(n + 2, inner)

                    def rectify(k):
                        b = (pos + k) % 2
                        act.wait_ge(s.u_mm, 3 * n + k + 1)
                        if inner or 3 * n + k >= 2:
                            act.wait_ge(y_mm, 3 * n + k - 1)
                        act.activation(h[:, b, 0:width(k)], bU[b][:, 0:width(k)], ACT.Relu,
                                       bias=e.b1c[:, 0:1]).then_inc(h_ok, 1)

                    def square(k):
                        b = (pos + k) % 2
                        act.wait_ge(y_mm, 3 * n + k + 1)
                        if inner or 3 * n + k >= 2:
                            act.wait_ge(sum_ok, 3 * n + k - 1)
                        act.activation(ysq[:, b, 0:width(k)], bY[b][:, 0:width(k)], ACT.Square).then_inc(ysq_ok, 1)

                    def root(k):
                        r = len(tiles(k))
                        act.wait_ge(sum_ok, 3 * n + k + 1)
                        sd = var[:, (pos + k) % 2, 0:r]
                        act.activation(sd, sd, ACT.Sqrt, bias=e.eps[:, 0:1], scale=1.0 / P).then_inc(root_ok, 1)

                    if A:
                        rectify(0)
                        rectify(1)
                    if N:
                        shorten_rows(act, s, K, pos + 1, inner or g >= 1)
                    if A:
                        square(0)
                    if N:
                        act.wait_ge(s.xT_mm, g + 1)
                        act.copy(s.xT[:, :], pair_bank(pos, 1)[:, 0:P]).then_inc(s.xT_ok, 1)
                    if A:
                        rectify(2)
                        root(0)
                        square(1)
                    if N:
                        act.wait_ge(s.p_mm, g + 1)
                        if inner or g >= 1:
                            act.wait_ge(s.u_mm, 3 * g)
                        act.copy(s.hi[:, :], pair_bank(pos, 1)[:, 0:2 * P]).then_inc(s.hi_ok, 1)
                    if A:
                        root(1)
                    if part(n, pos, inner, 5):
                        squares(act, e, s, batches(K, pos) - 2, range(0, Q // 2))
                    if part(n, pos, inner, 6):
                        squares(act, e, s, batches(K, pos) - 2, range(Q // 2, Q))
                    if N2:
                        start_rows(act, e, s, K, pos + 2, True)
                        normalise_x(act, e, s, K, pos + 2, inner or n >= 0)
                    if N:
                        if inner or g >= 4:
                            act.wait_ge(o_mm, g - 3)
                        for k in range(CHUNKS):
                            evacuate_rows(act, s, ring[k], K, pos + 1, k)
                    if A:
                        square(2)
                        root(2)

                every_step(act, step, 7)

            @block.vector
            def _(v):
                number_rows(v, e, s, 0, 0, False)
                select_rows(v, e, s, 0, 0, False)

                def step(K, pos, inner):
                    n = 8 * K + pos
                    g = n + 1
                    A, N, N2 = gathered(n, inner), gathered(n + 1, inner), gathered(n + 2, inner)

                    def total(k):
                        r, b = len(tiles(k)), (pos + k) % 2
                        v.wait_ge(ysq_ok, 3 * n + k + 1)
                        if inner or 3 * n + k >= 2:
                            v.wait_ge(z_ok, 3 * n + k - 1)
                        v.tensor_reduce(var[:, b, 0:r], ysq[:, b, 0:width(k)].rearrange("p (j f) -> p j f", f=P),
                                        AX.X, ALU.add).then_inc(sum_ok, 1)

                    def scale(k):
                        r, b = len(tiles(k)), (pos + k) % 2
                        v.wait_ge(root_ok, 3 * n + k + 1)
                        v.reciprocal(var[:, b, 0:r], var[:, b, 0:r]).then_inc(inv_ok, 1)
                        v.wait_ge(inv_ok, 3 * n + k + 1)
                        v.tensor_tensor(z[:, pos % 2, 4 * k:4 * k + r, :], bY[b][:, 0:width(k)].rearrange("p (j f) -> p j f", f=P),
                                        var[:, b, 0:r].unsqueeze(2).broadcast_to([P, r, P]), ALU.mult).then_inc(z_ok, 1)

                    i = batches(K, pos) - (2 if pos % Q == 0 else 1)
                    q = Steps(v, seq_c, 6 * i)

                    def own():
                        return e.cur[:, bass.ds(Q * i, Q), :]

                    if part(n, pos, inner, 1):
                        v.wait_ge(o_mm, n - 1)
                        if inner or n > Q + 1:
                            v.wait_ge(s.cen_ok, i)
                        v.tensor_tensor(s.res[:, :, :], bO[:, :].rearrange("p (q f) -> p q f", f=P),
                                        e.gam[:, :].unsqueeze(1).broadcast_to([P, Q, P]), ALU.mult).then_inc(o_read, 1)
                    if N:
                        if inner or g >= 2:
                            v.wait_ge(s.u_mm, 3 * g - 3)
                        number_edges(v, e, s, ring, K, pos + 1)
                    if part(n, pos, inner, 2):
                        q.n = 1
                        q.wait()
                        v.wait_ge(o_read, i + 1)
                        q.add(v.tensor_tensor(s.res[:, :, :], s.res[:, :, :], bb[:, :, :], ALU.add))
                    if part(n, pos, inner, 3):
                        q.n = 3
                        q.wait()
                        q.add(v.tensor_tensor(s.res[:, :, :], s.res[:, :, :], own(), ALU.add))
                    if part(n, pos, inner, 4):
                        q.n = 5
                        q.wait()
                        q.add(v.tensor_scalar(s.mean[:, :], s.mean[:, :], 1.0 / P, None, ALU.mult))
                    if A:
                        if inner or n >= 2:
                            v.wait_ge(o_mm, n - 1)
                        total(0)
                    if N2:
                        number_rows(v, e, s, K, pos + 2, inner or n >= 0)
                    if A:
                        total(1)
                        scale(0)
                    if N:
                        split_low(v, s, pair_bank(pos, 1), K, pos + 1, inner or g >= 1, 1)
                    if A:
                        scale(1)
                    if N2:
                        select_rows(v, e, s, K, pos + 2, inner or n + 2 >= 4)
                    if A:
                        total(2)
                    if part(n, pos, inner, 1):
                        q.add(v.tensor_tensor(bb[:, :, :], e.bet[:, :].unsqueeze(1).broadcast_to([P, Q, P]),
                                              e.deg[:, 0, bass.ds(Q * i, Q)].unsqueeze(2).broadcast_to([P, Q, P]), ALU.mult))
                    if part(n, pos, inner, 2):
                        q.add(v.tensor_tensor(own(), own(), e.rstd[:, bass.ds(Q * i, Q)].unsqueeze(2).broadcast_to([P, Q, P]),
                                              ALU.mult))
                    if part(n, pos, inner, 3):
                        q.wait()
                        q.add(v.tensor_reduce(s.mean[:, :], s.res[:, :, :], AX.X, ALU.add))
                    if part(n, pos, inner, 4):
                        q.wait()
                        v.tensor_tensor(own(), s.res[:, :, :], s.mean[:, :].unsqueeze(2).broadcast_to([P, Q, P]),
                                        ALU.subtract).then_inc(s.cen_ok, 1)
                    if A:
                        scale(2)

                every_step(v, step, 7)


class Masks:
    pass


def dense_masks(nc, c, e):
    m = Masks()

    def sb(name, shape):
        return c.enter_context(nc.sbuf_tensor("m_" + name, shape, F32))

    m.Wpad = sb("Wpad", [P, 2 * P - HEADS])
    m.Rep = sb("Rep", [P, P, HEADS])
    m.RepT = sb("RepT", [P, NRT, P])
    m.diag = sb("diag", [P, P])
    hselT = sb("hselT", [HEADS, P])
    rep8 = sb("rep8", [HEADS, P])
    masks, made, heads_mm, diag_mm, diag_ok = (c.enter_context(nc.semaphore("m_" + k)) for k in (
        "masks", "made", "heads_mm", "diag_mm", "diag_ok"))
    banks = e.banks
    with nc.Block() as block:
        @block.gpsimd
        def _(pool):
            pool.memset(m.Wpad[:, :], 0.0).then_inc(masks, 1)
            pool.memset(m.Rep[:, :, :], 0.0).then_inc(masks, 1)
            pool.memset(m.RepT[:, :, :], 1.0).then_inc(masks, 1)
            pool.wait_ge(masks, 3)
            pool.affine_select(out=m.Rep[:, :, :], in_=m.Rep[:, :, :], compare_op=ALU.not_equal, fill=1.0,
                               base=0, pattern=[[-1, P], [0, HEADS]], channel_multiplier=1).then_inc(masks, 1)
            pool.affine_select(out=m.RepT[:, :, :], in_=m.RepT[:, :, :], compare_op=ALU.is_ge, fill=0.0,
                               base=0, pattern=[[P, NRT], [-HEADS, P]], channel_multiplier=1).then_inc(masks, 1)
            pool.wait_ge(masks, 5)
            pool.affine_select(out=m.RepT[:, :, :], in_=m.RepT[:, :, :], compare_op=ALU.is_ge, fill=0.0,
                               base=HEADS - 1, pattern=[[-P, NRT], [HEADS, P]], channel_multiplier=-1).then_inc(masks, 1)

        @block.tensor
        def _(pe):
            pe.transpose(banks[1][0:HEADS, 0:P], e.hsel[:, :], e.ident[:, :]).then_inc(heads_mm, 1)
            pe.wait_ge(made, 2)
            pe.matmul(banks[2][:, 0:P], rep8[:, :], hselT[:, :], start=True, stop=True).then_inc(diag_mm, 1)

        @block.vector
        def _(v):
            v.wait_ge(masks, 3)
            v.tensor_scalar(m.Wpad[:, P - HEADS:P], e.hsel[:, :], e.wcol[:, 0:1], None, ALU.mult)
            v.tensor_copy(rep8[:, :].rearrange("k (r h) -> k r h", h=HEADS),
                          e.ident[0:HEADS, 0:HEADS].unsqueeze(1).broadcast_to([HEADS, RT, HEADS])).then_inc(made, 1)
            v.wait_ge(heads_mm, 1)
            v.tensor_copy(hselT[:, :], banks[1][0:HEADS, 0:P]).then_inc(made, 1)
            v.wait_ge(diag_mm, 1)
            v.tensor_copy(m.diag[:, :], banks[2][:, 0:P]).then_inc(diag_ok, 1)
            v.wait_ge(diag_ok, 1)
    return m


def layer1_dense(nc, e):
    c = ExitStack()
    with c:
        def sb(name, shape, dt=F32):
            return c.enter_context(nc.sbuf_tensor("gb_" + name, shape, dt))

        def sem(name):
            return c.enter_context(nc.semaphore("gb_" + name))

        cur, ident = e.cur, e.ident
        ain = sb("ain", [P, P])
        xin = sb("xin", [P, P])
        xT = sb("xT", [P, P])
        gT = sb("gT", [P, 2, P])
        gr = sb("gr", [P, P])
        u = sb("u", [P, 2, RS, P])
        lk = sb("lk", [P, 2, RS, P])
        arep = sb("arep", [P, P])
        drop = sb("drop", [P, P])
        sc = sb("sc", [P, P])
        top = sb("top", [P, 1])
        ex = sb("ex", [P, P])
        den = sb("den", [P, 1])
        aT = sb("aT", [P, P])
        od = sb("od", [P, P])
        res = sb("res", [P, P])
        mean = sb("mean", [P, 1])
        junk = sb("junk", [P, P])
        (a_in, x_ok, xT_mm, xT_ok, g_mm, gT_ok, lk_ok, lk_used, e_mm, rep_mm, arep_ok, top_ok, ex_ok, a_ok, aT_mm, aT_ok,
         o_mm, od_ok, out_mm, cen_ok, sq_ok, seq_g, seq_s, seq_t) = (sem(k) for k in (
             "a_in", "x_ok", "xT_mm", "xT_ok", "g_mm", "gT_ok", "lk_ok", "lk_used", "e_mm", "rep_mm", "arep_ok", "top_ok",
             "ex_ok", "a_ok", "aT_mm", "aT_ok", "o_mm", "od_ok", "out_mm", "cen_ok", "sq_ok", "seq_g", "seq_s", "seq_t"))
        seq_x = sem("seq_x")
        bX, bG, bE, bR, bT, bO, bZ = e.banks[:7]
        masks = dense_masks(nc, c, e)
        NS = P // RS

        with nc.Block() as block:
            @block.sync
            def _(sp):
                sp.dma_start(ain[:, :], e.adj_v[:, 0, :]).then_inc(a_in, 16)
                with sp.Fori(1, B) as n:
                    sp.wait_ge(rep_mm, NRT * n)
                    sp.dma_start(ain[:, :], e.adj_v[:, n, :]).then_inc(a_in, 16)

            @block.tensor
            def _(pe):
                with pe.Fori(0, B) as n:
                    pe.wait_ge(x_ok, n + 1)
                    pe.transpose(bX[:, 0:P], xin[:, :], ident[:, :]).then_inc(xT_mm, 1)
                    pe.wait_ge(xT_ok, n + 1)
                    pe.matmul(bG[:, 0:P], e.WlrT[:, 0, :], xT[:, :], start=True, stop=True)
                    pe.matmul(bG[:, P:2 * P], e.WlrT[:, 1, :], xT[:, :], start=True, stop=True)
                    pe.matmul(bG[:, 2 * P:3 * P], xT[:, :], e.WlrT[:, 1, :], start=True, stop=True).then_inc(g_mm, 1)
                    pe.wait_ge(a_in, 16 * n + 16)
                    pe.wait_ge(gT_ok, n + 1)
                    for t in range(NRT):
                        m = NRT * n + t
                        pe.matmul(bR[:, 0:P], masks.Rep[:, :, :].rearrange("i r h -> i (r h)")[:, P * t:P * t + P],
                                  ain[:, :], start=True, stop=True).then_inc(rep_mm, 1)
                        for k in range(RT // RS):
                            s = NS * n + (RT // RS) * t + k
                            pe.wait_ge(lk_ok, s + 1)
                            for r in range(RS):
                                row = RS * k + r
                                w = masks.Wpad[:, P - HEADS - HEADS * row:2 * P - HEADS - HEADS * row]
                                q = pe.matmul(bE[:, 0:P], w, lk[:, k % 2, r, :], start=(row == 0), stop=(row == RT - 1))
                            q.then_inc(lk_used, 1)
                        pe.wait_ge(a_ok, m + 1)
                        pe.transpose(bT[:, 0:P], ex[:, :], ident[:, :]).then_inc(aT_mm, 1)
                        pe.wait_ge(aT_ok, m + 1)
                        pe.matmul(bO[:, 0:P], aT[:, :], gr[:, :], start=True, stop=True).then_inc(o_mm, 1)
                        pe.wait_ge(od_ok, m + 1)
                        pe.matmul(bZ[:, 0:P], masks.RepT[:, t, :], od[:, :], start=(t == 0), stop=(t == NRT - 1)).then_inc(out_mm, 1)

            @block.scalar
            def _(act):
                with act.Fori(0, B) as n:
                    act.wait_ge(xT_mm, n + 1)
                    act.copy(xT[:, :], bX[:, 0:P]).then_inc(xT_ok, 1)
                    act.wait_ge(g_mm, n + 1)
                    act.copy(gT[:, :, :], bG[:, 0:2 * P].rearrange("p (a f) -> p a f", a=2)).then_inc(gT_ok, 1)
                    act.copy(gr[:, :], bG[:, 2 * P:3 * P]).then_inc(seq_g, 1)
                    act.wait_ge(seq_g, n + 1)
                    for t in range(NRT):
                        m = NRT * n + t
                        act.wait_ge(top_ok, m + 1)
                        act.activation(ex[:, :], sc[:, :], ACT.Exp, bias=top[:, 0:1], accum_out=den[:, 0:1]).then_inc(ex_ok, 1)
                        act.wait_ge(aT_mm, m + 1)
                        act.copy(aT[:, :], bT[:, 0:P]).then_inc(aT_ok, 1)
                    act.wait_ge(cen_ok, n + 1)
                    act.activation(junk[:, :], cur[:, n, :], ACT.Square, accum_out=e.sqsum[:, bass.ds(n, 1)]).then_inc(sq_ok, 1)
                    act.wait_ge(sq_ok, n + 1)

            @block.vector
            def _(v):
                with v.Fori(0, B) as n:
                    v.tensor_copy(xin[:, :], cur[:, n, :]).then_inc(x_ok, 1)
                    v.wait_ge(gT_ok, n + 1)
                    v.wait_ge(seq_g, n + 1)
                    for t in range(NRT):
                        m = NRT * n + t
                        for k in range(RT // RS):
                            s = NS * n + (RT // RS) * t + k
                            q = Steps(v, seq_s, s)
                            b = k % 2
                            for r in range(RS):
                                i = RT * t + RS * k + r
                                d = v.tensor_scalar(u[:, b, r, :], gT[:, 0, :], gT[:, 1, i:i + 1], None, ALU.add)
                            q.add(d)
                            q.wait()
                            if t == 0 and k < 2:
                                v.wait_ge(out_mm, NRT * n)
                            else:
                                v.wait_ge(lk_used, s - 1)
                            v.scalar_tensor_tensor(lk[:, b, :, :], u[:, b, :, :], SLOPE, u[:, b, :, :],
                                                   ALU.mult, ALU.max).then_inc(lk_ok, 1)
                        q = Steps(v, seq_t, 5 * m)
                        v.wait_ge(rep_mm, m + 1)
                        q.add(v.tensor_copy(arep[:, :], bR[:, 0:P]))
                        q.wait()
                        q.add(v.tensor_scalar(drop[:, :], arep[:, :], 0.0, NEG, ALU.is_equal, ALU.mult))
                        v.wait_ge(lk_used, NS * n + (RT // RS) * (t + 1))
                        q.add(v.tensor_tensor(sc[:, :], bE[:, 0:P], arep[:, :], ALU.mult))
                        q.wait()
                        q.add(v.tensor_tensor(sc[:, :], sc[:, :], drop[:, :], ALU.add))
                        q.wait()
                        v.tensor_reduce(top[:, :], sc[:, :], AX.X, ALU.max, negate=True).then_inc(top_ok, 1)
                        v.wait_ge(ex_ok, m + 1)
                        q.add(v.reciprocal(den[:, :], den[:, :]))
                        q.wait()
                        v.tensor_scalar(ex[:, :], ex[:, :], den[:, 0:1], None, ALU.mult).then_inc(a_ok, 1)
                        v.wait_ge(o_mm, m + 1)
                        v.tensor_tensor(od[:, :], bO[:, 0:P], masks.diag[:, :], ALU.mult).then_inc(od_ok, 1)
                    v.wait_ge(out_mm, NRT * (n + 1))
                    q = Steps(v, seq_x, 5 * n)
                    q.add(v.tensor_copy(res[:, :], bZ[:, 0:P]))
                    q.wait()
                    q.add(v.scalar_tensor_tensor(res[:, :], res[:, :], SLOPE, res[:, :], ALU.mult, ALU.max))
                    q.wait()
                    q.add(v.tensor_tensor(res[:, :], res[:, :], xin[:, :], ALU.add))
                    q.wait()
                    q.add(v.tensor_reduce(mean[:, :], res[:, :], AX.X, ALU.add))
                    q.wait()
                    q.add(v.tensor_scalar(mean[:, :], mean[:, :], 1.0 / P, None, ALU.mult))
                    q.wait()
                    v.tensor_scalar(cur[:, n, :], res[:, :], mean[:, 0:1], None, ALU.subtract).then_inc(cen_ok, 1)
                    v.wait_ge(cen_ok, n + 1)


def layer2_dense(nc, e):
    c = ExitStack()
    with c:
        def sb(name, shape, dt=F32):
            return c.enter_context(nc.sbuf_tensor("gc_" + name, shape, dt))

        def sem(name):
            return c.enter_context(nc.semaphore("gc_" + name))

        cur, ident = e.cur, e.ident
        ain = sb("ain", [P, P])
        aT = sb("aT", [P, P])
        xin = sb("xin", [P, P])
        xT = sb("xT", [P, P])
        hT = sb("hT", [P, 2, P])
        h = sb("h", [P, 2, RS, P])
        y = sb("y", [P, P, P])
        ysq = sb("ysq", [P, 2, RS, P])
        cf = sb("cf", [P, P])
        zT = sb("zT", [P, P])
        asum = sb("asum", [P, 1])
        bb = sb("bb", [P, P])
        res = sb("res", [P, P])
        mean = sb("mean", [P, 1])
        junk = sb("junk", [P, P])
        (a_in, x_ok, xT_mm, xT_ok, g_mm, h1_ok, h_ok, y_mm, y_ok, ysq_ok, var_ok, cf_root, cf_ok, aT_ok, z_mm, zT_ok,
         zt_mm, cen_ok, sq_ok, seq_c, seq_x) = (sem(k) for k in (
             "a_in", "x_ok", "xT_mm", "xT_ok", "g_mm", "h1_ok", "h_ok", "y_mm", "y_ok", "ysq_ok", "var_ok", "cf_root",
             "cf_ok", "aT_ok", "z_mm", "zT_ok", "zt_mm", "cen_ok", "sq_ok", "seq_c", "seq_x"))
        bX, bG, bY0, bY1, bZ, bZT = e.banks[:6]
        bY = (bY0, bY1)
        NS = P // RS

        with nc.Block() as block:
            @block.sync
            def _(sp):
                sp.dma_start(ain[:, :], e.adj_v[:, 0, :]).then_inc(a_in, 16)
                with sp.Fori(1, B) as n:
                    sp.wait_ge(cen_ok, n)
                    sp.dma_start(ain[:, :], e.adj_v[:, n, :]).then_inc(a_in, 16)

            @block.tensor
            def _(pe):
                with pe.Fori(0, B) as n:
                    pe.wait_ge(x_ok, n + 1)
                    pe.wait_ge(a_in, 16 * n + 16)
                    pe.transpose(bX[:, 0:P], xin[:, :], ident[:, :])
                    pe.transpose(bX[:, P:2 * P], ain[:, :], ident[:, :]).then_inc(xT_mm, 1)
                    pe.wait_ge(xT_ok, n + 1)
                    pe.matmul(bG[:, 0:P], e.W1s[:, 1, :], xT[:, :], start=True, stop=True)
                    pe.matmul(bG[:, P:2 * P], e.W1s[:, 0, :], xT[:, :], start=True, stop=True).then_inc(g_mm, 1)
                    for k in range(NS):
                        s = NS * n + k
                        pe.wait_ge(h_ok, s + 1)
                        if k >= 2:
                            pe.wait_ge(y_ok, s - 1)
                        for r in range(RS):
                            q = pe.matmul(bY[k % 2][:, P * r:P * r + P], h[:, k % 2, r, :], e.W2c[:, :], start=True, stop=True)
                        q.then_inc(y_mm, 1)
                    pe.wait_ge(cf_ok, n + 1)
                    for i in range(P):
                        q = pe.matmul(bZ[:, i:i + 1], y[:, i, :], cf[:, i:i + 1], start=True, stop=True)
                    q.then_inc(z_mm, 1)
                    pe.wait_ge(zT_ok, n + 1)
                    pe.transpose(bZT[:, 0:P], zT[:, :], ident[:, :]).then_inc(zt_mm, 1)

            @block.scalar
            def _(act):
                with act.Fori(0, B) as n:
                    act.wait_ge(xT_mm, n + 1)
                    act.copy(aT[:, :], bX[:, P:2 * P]).then_inc(aT_ok, 1)
                    act.copy(xT[:, :], bX[:, 0:P]).then_inc(xT_ok, 1)
                    for k in range(NS):
                        s = NS * n + k
                        act.wait_ge(y_ok, s + 1)
                        if k >= 2:
                            act.wait_ge(var_ok, s - 1)
                        act.activation(ysq[:, k % 2, :, :], y[:, RS * k:RS * k + RS, :], ACT.Square).then_inc(ysq_ok, 1)
                    act.wait_ge(var_ok, NS * (n + 1))
                    act.activation(cf[:, :], cf[:, :], ACT.Sqrt, bias=e.eps[:, 0:1], scale=1.0 / P).then_inc(cf_root, 1)
                    act.wait_ge(z_mm, n + 1)
                    act.copy(zT[:, :], bZ[:, 0:P]).then_inc(zT_ok, 1)
                    act.wait_ge(cen_ok, n + 1)
                    act.activation(junk[:, :], cur[:, n, :], ACT.Square, accum_out=e.sqsum[:, bass.ds(n, 1)]).then_inc(sq_ok, 1)
                    act.wait_ge(sq_ok, n + 1)

            @block.vector
            def _(v):
                with v.Fori(0, B) as n:
                    v.tensor_copy(xin[:, :], cur[:, n, :]).then_inc(x_ok, 1)
                    v.wait_ge(g_mm, n + 1)
                    v.tensor_copy(hT[:, 0, :], bG[:, 0:P]).then_inc(h1_ok, 1)
                    v.tensor_scalar(hT[:, 1, :], bG[:, P:2 * P], e.b1c[:, 0:1], None, ALU.add).then_inc(h1_ok, 1)
                    v.wait_ge(h1_ok, 2 * n + 2)

                    def variance(k):
                        v.wait_ge(ysq_ok, NS * n + k + 1)
                        v.tensor_reduce(cf[:, RS * k:RS * k + RS], ysq[:, k % 2, :, :], AX.X, ALU.add).then_inc(var_ok, 1)

                    def evacuate(k):
                        v.wait_ge(y_mm, NS * n + k + 1)
                        v.tensor_tensor(y[:, RS * k:RS * k + RS, :], bY[k % 2][:, :].rearrange("p (r f) -> p r f", r=RS),
                                        e.b2c[:, :].unsqueeze(1).broadcast_to([P, RS, P]), ALU.add).then_inc(y_ok, 1)

                    for k in range(NS):
                        if k >= 2:
                            v.wait_ge(y_mm, NS * n + k - 1)
                        for r in range(RS):
                            i = RS * k + r
                            d = v.tensor_scalar(h[:, k % 2, r, :], hT[:, 1, :], hT[:, 0, i:i + 1], 0.0, ALU.add, ALU.max)
                        d.then_inc(h_ok, 1)
                        if k >= 1:
                            evacuate(k - 1)
                        if k >= 2:
                            variance(k - 2)
                    evacuate(NS - 1)
                    variance(NS - 2)
                    variance(NS - 1)
                    q = Steps(v, seq_c, n)
                    v.wait_ge(cf_root, n + 1)
                    q.add(v.reciprocal(cf[:, :], cf[:, :]))
                    q.wait()
                    v.wait_ge(aT_ok, n + 1)
                    v.tensor_tensor(cf[:, :], cf[:, :], aT[:, :], ALU.mult).then_inc(cf_ok, 1)
                    q = Steps(v, seq_x, 6 * n)
                    q.add(v.tensor_reduce(asum[:, :], ain[:, :], AX.X, ALU.add))
                    q.wait()
                    q.add(v.scalar_tensor_tensor(bb[:, :], e.bet[:, :], asum[:, 0:1], xin[:, :], ALU.mult, ALU.add))
                    v.wait_ge(zt_mm, n + 1)
                    q.add(v.tensor_tensor(res[:, :], bZT[:, 0:P], e.gam[:, :], ALU.mult))
                    q.wait()
                    q.add(v.tensor_tensor(res[:, :], res[:, :], bb[:, :], ALU.add))
                    q.wait()
                    q.add(v.tensor_reduce(mean[:, :], res[:, :], AX.X, ALU.add))
                    q.wait()
                    q.add(v.tensor_scalar(mean[:, :], mean[:, :], 1.0 / P, None, ALU.mult))
                    q.wait()
                    v.tensor_scalar(cur[:, n, :], res[:, :], mean[:, 0:1], None, ALU.subtract).then_inc(cen_ok, 1)
                    v.wait_ge(cen_ok, n + 1)


def layer3(nc, e):
    c = ExitStack()
    with c:
        def sb(name, shape, dt=F32):
            return c.enter_context(nc.sbuf_tensor("d_" + name, shape, dt))

        def sem(name):
            return c.enter_context(nc.semaphore("d_" + name))

        cur, ident = e.cur, e.ident
        ain = sb("ain", [P, 4, G, P])
        dg = sb("dg", [P, 4, G])
        nz = sb("nz", [P, 4, G])
        xd = sb("xd", [P, 2, G, P])
        aT = sb("aT", [P, 2, G, P])
        gT = sb("gT", [P, 2, G, P])
        res = sb("res", [P, G, P])
        mean = sb("mean", [P, G])
        sums = sb("sums", [P, 2, G])
        scale = sb("scale", [P, 2, G])
        junk = sb("junk", [P, G, P])
        a_in = [sem(f"a_in{b}") for b in range(4)]
        norm_ok, sum_ok, root_ok, xd_ok, aT_mm, aT_ok, g_mm, g_ok, o_mm, cen_ok, sq_ok = (
            sem(k) for k in ("norm_ok", "sum_ok", "root_ok", "xd_ok", "aT_mm", "aT_ok", "g_mm",
                             "g_ok", "o_mm", "cen_ok", "sq_ok"))
        out_read, last_root, last_inv, scaled, stored, seq_f, seq_b = (
            sem(k) for k in ("out_read", "last_root", "last_inv", "scaled", "stored", "seq_f", "seq_b"))
        bA, bG, bO = e.banks[:3]

        with nc.Block() as block:
            @block.sync
            def _(sp):
                def load(n, b):
                    sp.dma_start(ain[:, b, :, :], e.adj_v[:, bass.ds(n * G, G), :]).then_inc(a_in[b], 16)

                def store(n):
                    sp.wait_ge(scaled, n + 1)
                    sp.dma_start(e.out_v[:, bass.ds(n * G, G), :], cur[:, bass.ds(n * G, G), :]).then_inc(stored, 16)

                for b in range(4):
                    load(b, b)
                with sp.Fori(1, NG // 4) as k:
                    for b in range(4):
                        sp.wait_ge(aT_mm, 4 * k + b - 3)
                        sp.wait_ge(sum_ok, 4 * k + b - 3)
                        load(4 * k + b, b)
                        store(4 * k + b - 4)
                for n in range(NG - 4, NG):
                    store(n)
                sp.wait_ge(stored, 16 * NG)

            @block.tensor
            def _(pe):
                def step(K, pos, inner):
                    n = 4 * K + pos
                    f, h = n + 2, n + 1
                    if group(n, inner):
                        pe.wait_ge(g_ok, n + 1)
                        if inner or n > 0:
                            pe.wait_ge(out_read, n)
                        for g in range(G):
                            m = pe.matmul(bO[:, P * g:P * g + P], gT[:, pos % 2, g, :], e.W3[:, :], start=True, stop=True)
                        m.then_inc(o_mm, 1)
                    if group(h, inner):
                        b = (pos + 1) % 2
                        pe.wait_ge(aT_ok, h + 1)
                        pe.wait_ge(xd_ok, h + 1)
                        if inner or h > 0:
                            pe.wait_ge(g_ok, h)
                        for g in range(G):
                            pe.matmul(bG[:, P * g:P * g + P], xd[:, b, g, :], aT[:, b, g, :], start=True, stop=False)
                            m = pe.matmul(bG[:, P * g:P * g + P], xd[:, b, g, :], ident[:, :], start=False, stop=True)
                        m.then_inc(g_mm, 1)
                    if group(f, inner):
                        pe.wait_ge(a_in[(pos + 2) % 4], 16 * (K + (pos + 2) // 4) + 16)
                        if inner or f > 0:
                            pe.wait_ge(aT_ok, f)
                        for g in range(G):
                            m = pe.transpose(bA[:, P * g:P * g + P], ain[:, (pos + 2) % 4, g, :], ident[:, :])
                        m.then_inc(aT_mm, 1)

                every_group(pe, step, 1)

            @block.scalar
            def _(act):
                def step(K, pos, inner):
                    n = 4 * K + pos
                    f, h, fb = n + 2, n + 1, (pos + 2) % 4
                    if group(f, inner):
                        for g in range(G):
                            act.activation(cur[:, f * G + g, :], cur[:, f * G + g, :], ACT.Copy,
                                           scale=e.rstd[:, bass.ds(f * G + g, 1)]).then_inc(norm_ok, 1)
                    if group(h, inner):
                        act.wait_ge(g_mm, h + 1)
                        if inner or h >= 2:
                            act.wait_ge(o_mm, h - 1)
                        act.copy(gT[:, (pos + 1) % 2, :, :], grp(bG)).then_inc(g_ok, 1)
                    if group(f, inner):
                        act.wait_ge(sum_ok, f + 1)
                        act.activation(dg[:, fb, :], dg[:, fb, :], ACT.Sqrt).then_inc(root_ok, 1)
                    if group(n - 1, inner):
                        act.wait_ge(cen_ok, n)
                        if inner or n - 1 > 0:
                            act.wait_ge(sq_ok, G * (n - 1))
                    if group(f, inner):
                        act.wait_ge(aT_mm, f + 1)
                        if inner or f >= 2:
                            act.wait_ge(g_mm, f - 1)
                        act.copy(aT[:, pos % 2, :, :], grp(bA)).then_inc(aT_ok, 1)
                    if group(n - 1, inner):
                        for g in range(G):
                            act.activation(junk[:, g, :], cur[:, (n - 1) * G + g, :], ACT.Square,
                                           accum_out=sums[:, (pos - 1) % 2, g:g + 1]).then_inc(sq_ok, 1)
                    if group(n - 1, inner):
                        act.wait_ge(sq_ok, G * n)
                        if inner or n - 1 >= 2:
                            act.wait_ge(scaled, n - 2)
                        act.activation(scale[:, (pos - 1) % 2, :], sums[:, (pos - 1) % 2, :], ACT.Sqrt,
                                       bias=e.eps[:, 0:1], scale=1.0 / P).then_inc(last_root, 1)

                every_group(act, step, 1)

            @block.vector
            def _(v):
                def step(K, pos, inner):
                    n = 4 * K + pos
                    f, fb = n + 2, (pos + 2) % 4
                    q = Steps(v, seq_f, 6 * f)
                    r = Steps(v, seq_b, 4 * n)
                    if group(f, inner):
                        v.wait_ge(a_in[fb], 16 * (K + (pos + 2) // 4) + 16)
                        q.add(v.tensor_reduce(dg[:, fb, :], ain[:, fb, :, :], AX.X, ALU.add))
                        q.wait()
                        q.add(v.tensor_scalar(dg[:, fb, :], dg[:, fb, :], 1.0, None, ALU.add))
                        q.wait()
                        q.add(v.tensor_scalar(nz[:, fb, :], dg[:, fb, :], 0.0, None, ALU.is_equal))
                        q.wait()
                        v.tensor_tensor(dg[:, fb, :], dg[:, fb, :], nz[:, fb, :], ALU.add).then_inc(sum_ok, 1)
                    if group(n, inner):
                        v.wait_ge(o_mm, n + 1)
                        if inner or n > 0:
                            v.wait_ge(cen_ok, n)
                        v.tensor_tensor(res[:, :, :], grp(bO), dg[:, pos % 4, :].unsqueeze(2).broadcast_to([P, G, P]),
                                        ALU.mult).then_inc(out_read, 1)
                        v.wait_ge(out_read, n + 1)
                        r.add(v.tensor_tensor(res[:, :, :], res[:, :, :], cur[:, bass.ds(n * G, G), :], ALU.add))
                        r.wait()
                    if group(f, inner):
                        v.wait_ge(root_ok, f + 1)
                        q.add(v.tensor_scalar(nz[:, fb, :], nz[:, fb, :], -1.0, 1.0, ALU.mult, ALU.add))
                        q.add(v.reciprocal(dg[:, fb, :], dg[:, fb, :]))
                        q.wait()
                        q.add(v.tensor_tensor(dg[:, fb, :], dg[:, fb, :], nz[:, fb, :], ALU.mult))
                        q.wait()
                        v.wait_ge(norm_ok, G * (f + 1))
                        if inner or f >= 2:
                            v.wait_ge(g_mm, f - 1)
                        v.tensor_tensor(xd[:, pos % 2, :, :], cur[:, bass.ds(f * G, G), :],
                                        dg[:, fb, :].unsqueeze(2).broadcast_to([P, G, P]), ALU.mult).then_inc(xd_ok, 1)
                    if group(n, inner):
                        r.add(v.tensor_tensor(res[:, :, :], res[:, :, :],
                                              e.bia[:, :].unsqueeze(1).broadcast_to([P, G, P]), ALU.add))
                        r.wait()
                        r.add(v.tensor_reduce(mean[:, :], res[:, :, :], AX.X, ALU.add))
                        r.wait()
                        r.add(v.tensor_scalar(mean[:, :], mean[:, :], 1.0 / P, None, ALU.mult))
                        r.wait()
                        v.tensor_tensor(cur[:, bass.ds(n * G, G), :], res[:, :, :],
                                        mean[:, :].unsqueeze(2).broadcast_to([P, G, P]), ALU.subtract).then_inc(cen_ok, 1)
                    if group(n - 1, inner):
                        inverse = scale[:, (pos - 1) % 2, :]
                        part = cur[:, bass.ds((n - 1) * G, G), :]
                        v.wait_ge(last_root, n)
                        v.reciprocal(inverse, inverse).then_inc(last_inv, 1)
                        v.wait_ge(last_inv, n)
                        v.tensor_tensor(part, part, inverse.unsqueeze(2).broadcast_to([P, G, P]), ALU.mult).then_inc(scaled, 1)

                every_group(v, step, 1)


def roots(nc, e, tag):
    c = ExitStack()
    with c:
        root_ok, rstd_ok = (c.enter_context(nc.semaphore(tag + k)) for k in ("root_ok", "rstd_ok"))
        with nc.Block() as block:
            @block.scalar
            def _(act):
                act.activation(e.rstd[:, :], e.sqsum[:, :], ACT.Sqrt, bias=e.eps[:, 0:1],
                               scale=1.0 / P).then_inc(root_ok, 1)

            @block.vector
            def _(v):
                v.wait_ge(root_ok, 1)
                v.reciprocal(e.rstd[:, :], e.rstd[:, :]).then_inc(rstd_ok, 1)
                v.wait_ge(rstd_ok, 1)

            @block.tensor
            def _(pe):
                pe.wait_ge(rstd_ok, 1)

            @block.gpsimd
            def _(pool):
                pool.wait_ge(rstd_ok, 1)

            @block.sync
            def _(sp):
                sp.wait_ge(rstd_ok, 1)


def normalise(nc, e, tag):
    c = ExitStack()
    with c:
        root_ok, rstd_ok, scaled = (c.enter_context(nc.semaphore(tag + k)) for k in ("root_ok", "rstd_ok", "scaled"))
        with nc.Block() as block:
            @block.scalar
            def _(act):
                act.activation(e.rstd[:, :], e.sqsum[:, :], ACT.Sqrt, bias=e.eps[:, 0:1],
                               scale=1.0 / P).then_inc(root_ok, 1)

            @block.vector
            def _(v):
                v.wait_ge(root_ok, 1)
                v.reciprocal(e.rstd[:, :], e.rstd[:, :]).then_inc(rstd_ok, 1)
                v.wait_ge(rstd_ok, 1)
                with v.Fori(0, NG) as n:
                    part = e.cur[:, bass.ds(n * G, G), :]
                    v.tensor_tensor(part, part, e.rstd[:, bass.ds(n * G, G)].unsqueeze(2).broadcast_to([P, G, P]),
                                    ALU.mult).then_inc(scaled, 1)

            @block.tensor
            def _(pe):
                pe.wait_ge(rstd_ok, 1)

            @block.gpsimd
            def _(pool):
                pool.wait_ge(rstd_ok, 1)

            @block.sync
            def _(sp):
                sp.wait_ge(rstd_ok, 1)


def adjacency_stack(nc, x, adj, Wq, Wk, Wv, W_l, W_r, w_attn, W1, b1, W2, b2, gamma, beta,
                    weight, bias, out):
    ctx = ExitStack()
    with ctx:
        def sb(name, shape, dt=F32):
            return ctx.enter_context(nc.sbuf_tensor(name, shape, dt))

        def pb(name, shape, dt=F32):
            return ctx.enter_context(nc.psum_tensor(name, shape, dt))

        def sem(name):
            return ctx.enter_context(nc.semaphore(name))

        x_v = x.rearrange("b n f -> n b f")
        adj_v = adj.rearrange("b n m -> n b m")
        out_v = out.rearrange("b n f -> n b f")

        cur = sb("cur", [P, B, P])
        sqsum = sb("sqsum", [P, B])
        rstd = sb("rstd", [P, B])
        eps = sb("eps", [P, 1])
        ident = sb("ident", [P, P])
        identb = sb("identb", [P, P], BF16)
        M = sb("M", [P, P])
        WvT = sb("WvT", [P, P])
        W1s = sb("W1s", [P, 2, P])
        W2c = sb("W2c", [P, P])
        b2c = sb("b2c", [P, P])
        b1c = sb("b1c", [P, 1])
        gam = sb("gam", [P, P])
        bet = sb("bet", [P, P])
        W3 = sb("W3", [P, P])
        bia = sb("bia", [P, P])
        hsel = sb("hsel", [P, HEADS])
        wcol = sb("wcol", [P, 1])
        WlrT = sb("WlrT", [P, 2, P])
        put_w = sb("put_w", [P, Q, 2 * Q * HEADS])
        put_m = sb("put_m", [P, Q, 2 * Q * HEADS], F32R)
        ones = sb("ones", [P, P])
        ones3 = sb("ones3", [3, P], BF16)
        b2x = sb("b2x", [3, P], BF16)
        number1 = sb("number1", [P, ECAP])
        deg = sb("deg", [P, 2, B])
        first = sb("first", [P, B])
        unfirst = sb("unfirst", [P, B])
        end = sb("end", [P, B])
        general = sb("general", [P, 1], I32)

        banks = [pb(f"bank{i}", [P, 512]) for i in range(5)]
        wide = pb("wide", [P, 3 * 512])
        banks += [wide[:, 512 * i:512 * (i + 1)] for i in range(3)]

        e = Shared()
        e.x_v = x_v
        e.adj_v = adj_v
        e.out_v = out_v
        staged = ctx.enter_context(ExitStack())
        e.xin = staged.enter_context(nc.sbuf_tensor("xin", [P, 4, G, P], F32))
        e.ain = staged.enter_context(nc.sbuf_tensor("ain", [P, 4, G, P], F32))
        e.x_in = [sem(f"x_in{b}") for b in range(4)]

        with ExitStack() as c0:
            raw = c0.enter_context(nc.sbuf_tensor("raw", [P, 5, P], F32))
            b2r = c0.enter_context(nc.sbuf_tensor("b2r", [P, P], F32))
            rmean = c0.enter_context(nc.sbuf_tensor("rmean", [P, 2], F32))
            weights_in = sem("weights_in")
            masks = sem("masks")
            w_ready = sem("w_ready")
            w_seq = sem("w_seq")
            tri = c0.enter_context(nc.sbuf_tensor("tri", [P, P], F32))
            mk = c0.enter_context(nc.sbuf_tensor("mk", [P, 1], F32))
            zero = c0.enter_context(nc.sbuf_tensor("zero", [P, Q * 2 * Q * HEADS], F32))
            bp = c0.enter_context(nc.sbuf_tensor("bp", [P, 3, P], F32))
            bh = c0.enter_context(nc.sbuf_tensor("bh", [P, 3, P], BF16))
            pick = c0.enter_context(nc.sbuf_tensor("pick", [3, 3, P], F32))
            with nc.Block() as block:
                @block.sync
                def _(sp):
                    for k, w in enumerate((Wq, Wk, Wv, W_l, W_r)):
                        sp.dma_start(raw[:, k, :], w).then_inc(weights_in, 16)
                    sp.dma_start(W1s[:, 0, :], W1[P:2 * P, :]).then_inc(weights_in, 16)
                    sp.dma_start(W1s[:, 1, :], W1[0:P, :]).then_inc(weights_in, 16)
                    sp.dma_start(W2c[:, :], W2).then_inc(weights_in, 16)
                    sp.dma_start(W3[:, :], weight).then_inc(weights_in, 16)
                    for dst, v in ((b2r, b2), (gam, gamma), (bet, beta), (bia, bias)):
                        sp.dma_start(dst[:, :], v.partition_broadcast(P)).then_inc(weights_in, 16)
                    for b in range(4):
                        load_group(sp, e, b, b)

                @block.scalar
                def _(act):
                    act.dma_start(b1c[:, :], b1.rearrange("(k a) -> k a", a=1)).then_inc(weights_in, 16)
                    for h in range(HEADS):
                        act.dma_start(wcol[HF * h:HF * (h + 1), :],
                                      w_attn.rearrange("(f a) -> f a", a=1)).then_inc(weights_in, 16)

                NW = 16 * (14 + HEADS)

                @block.gpsimd
                def _(pool):
                    for t, v in ((ident, 0.0), (eps, EPS)):
                        pool.memset(t[:, :], v).then_inc(masks, 1)
                    pool.memset(hsel[:, :], 1.0).then_inc(masks, 1)
                    pool.memset(tri[:, :], 1.0).then_inc(masks, 1)
                    pool.memset(ones[:, :], 1.0).then_inc(masks, 1)
                    pool.memset(ones3[:, :], 1.0).then_inc(masks, 1)
                    pool.memset(zero[:, :], 0.0).then_inc(masks, 1)
                    pool.memset(number1[:, :], 1.0).then_inc(masks, 1)
                    pool.wait_ge(masks, 8)
                    pool.affine_select(out=tri[:, :], in_=tri[:, :], compare_op=ALU.is_ge, fill=0.0,
                                       base=0, pattern=[[1, P]], channel_multiplier=-1).then_inc(masks, 1)
                    pool.affine_select(out=ident[:, :], in_=ident[:, :], compare_op=ALU.not_equal, fill=1.0,
                                       base=0, pattern=[[-1, P]], channel_multiplier=1).then_inc(masks, 1)
                    pool.affine_select(out=hsel[:, :], in_=hsel[:, :], compare_op=ALU.is_ge, fill=0.0,
                                       base=0, pattern=[[-HF, HEADS]], channel_multiplier=1).then_inc(masks, 1)
                    pool.wait_ge(masks, 11)
                    pool.affine_select(out=hsel[:, :], in_=hsel[:, :], compare_op=ALU.is_ge, fill=0.0,
                                       base=HF - 1, pattern=[[HF, HEADS]], channel_multiplier=-1).then_inc(masks, 1)

                @block.tensor
                def _(pe):
                    pe.wait_ge(weights_in, NW)
                    pe.wait_ge(masks, 12)
                    pe.matmul(banks[0][:, 0:P], raw[:, 0, :], raw[:, 1, :], start=True, stop=True)
                    pe.transpose(banks[0][:, P:2 * P], raw[:, 2, :], ident[:, :])
                    pe.transpose(banks[0][:, 2 * P:3 * P], raw[:, 3, :], ident[:, :])
                    pe.transpose(banks[0][:, 3 * P:4 * P], raw[:, 4, :], ident[:, :]).then_inc(w_ready, 1)

                @block.vector
                def _(v):
                    q = Steps(v, w_seq)
                    v.wait_ge(masks, 12)
                    v.wait_ge(weights_in, NW)
                    v.wait_ge(w_ready, 1)
                    v.tensor_scalar(M[:, :], banks[0][:, 0:P], float(P) ** -0.5, None, ALU.mult)
                    v.tensor_copy(WvT[:, :], banks[0][:, P:2 * P])
                    v.tensor_copy(identb[:, :], ident[:, :])
                    v.tensor_copy(WlrT[:, :, :], banks[0][:, 2 * P:4 * P].rearrange("p (a f) -> p a f", a=2))
                    q.add(v.tensor_tensor_scan(number1[:, :], number1[:, :], number1[:, :], 0.0, ALU.mult, ALU.add))
                    q.add(v.tensor_copy(put_w[:, :, :].rearrange("p q c -> p (q c)"), zero[:, :]))
                    q.add(v.tensor_copy(put_m[:, :, :].rearrange("p q c -> p (q c)"), zero[:, :]))
                    q.add(v.tensor_reduce(mk[:, :], tri[:, :], AX.X, ALU.add))
                    q.wait()
                    q.add(v.tensor_scalar(mk[:, :], mk[:, :], MARK, None, ALU.mult))
                    q.wait()
                    H = Q * HEADS
                    for k in range(Q):
                        q.add(v.tensor_scalar(put_w[:, k, HEADS * k:HEADS * (k + 1)], hsel[:, :], wcol[:, 0:1], None, ALU.mult))
                        q.add(v.tensor_copy(put_m[:, k, H + HEADS * k:H + HEADS * (k + 1)], mk[:, :].broadcast_to([P, HEADS])))
                    q.add(v.tensor_reduce(rmean[:, 0:1], W2c[:, :], AX.X, ALU.add))
                    q.add(v.tensor_reduce(rmean[:, 1:2], b2r[:, :], AX.X, ALU.add))
                    q.wait()
                    q.add(v.tensor_scalar(rmean[:, :], rmean[:, :], -1.0 / P, None, ALU.mult))
                    q.wait()
                    q.add(v.tensor_scalar(W2c[:, :], W2c[:, :], rmean[:, 0:1], None, ALU.add))
                    q.add(v.tensor_scalar(b2c[:, :], b2r[:, :], rmean[:, 1:2], None, ALU.add))
                    q.wait()
                    q.add(v.tensor_copy(bh[:, 0, :], b2c[:, :]))
                    q.wait()
                    q.add(v.tensor_tensor(bp[:, 0, :], b2c[:, :], bh[:, 0, :], ALU.subtract))
                    q.wait()
                    q.add(v.tensor_copy(bh[:, 1, :], bp[:, 0, :]))
                    q.wait()
                    q.add(v.tensor_tensor(bp[:, 1, :], bp[:, 0, :], bh[:, 1, :], ALU.subtract))
                    q.wait()
                    q.add(v.tensor_copy(bh[:, 2, :], bp[:, 1, :]))
                    q.wait()
                    q.add(v.tensor_scalar(pick[:, 0, :], bh[0:3, 0, :], ident[0:3, 0:1], None, ALU.mult))
                    q.wait()
                    for k in (1, 2):
                        q.add(v.scalar_tensor_tensor(pick[:, k, :], bh[0:3, k, :], ident[0:3, k:k + 1], pick[:, k - 1, :],
                                                     ALU.mult, ALU.add))
                        q.wait()
                    q.add(v.tensor_copy(b2x[:, :], pick[:, 2, :]))
                    q.wait()

        e.cur = cur
        e.sqsum = sqsum
        e.rstd = rstd
        e.eps = eps
        e.ident = ident
        e.M = M
        e.WvT = WvT
        e.W1s = W1s
        e.W2c = W2c
        e.b2c = b2c
        e.b1c = b1c
        e.gam = gam
        e.bet = bet
        e.W3 = W3
        e.bia = bia
        e.hsel = hsel
        e.wcol = wcol
        e.WlrT = WlrT
        e.put_w = put_w
        e.put_m = put_m
        e.ones = ones
        e.ones3 = ones3
        e.b2x = b2x
        e.number1 = number1
        e.deg = deg
        e.first = first
        e.unfirst = unfirst
        e.identb = identb
        e.end = end
        e.general = general
        e.wide = wide
        e.banks = banks
        layer0(nc, e)
        staged.close()
        prepare(nc, e)
        flag = nc.values_load(general[0:1, 0:1], min_val=0, max_val=1)
        before = nc.snapshot_sems()
        with nc.If(flag > 0):
            middle_general(nc, e)
        nc.restore_sems(before)
        with nc.Else():
            middle_packed(nc, e)
        nc.end_ifs()
        roots(nc, e, "rc_")
        layer3(nc, e)


def middle_general(nc, e):
    normalise(nc, e, "na_")
    layer1_dense(nc, e)
    normalise(nc, e, "nb_")
    layer2_dense(nc, e)


def middle_packed(nc, e):
    roots(nc, e, "ra_")
    layer1_packed(nc, e)
    roots(nc, e, "rb_")
    layer2_packed(nc, e)


_INS = ['x', 'adj', 'L0_gnn_Wq', 'L0_gnn_Wk', 'L0_gnn_Wv', 'L1_gnn_W_l', 'L1_gnn_W_r', 'L1_gnn_w_attn',
        'L2_gnn_W1', 'L2_gnn_b1', 'L2_gnn_W2', 'L2_gnn_b2', 'L2_gnn_gamma', 'L2_gnn_beta',
        'L3_gnn_weight', 'L3_gnn_bias']
_OUTS = [((B, P, P), 'float32')]


def kernel(**inputs):
    import numpy as _np
    import concourse.bacc as _bacc
    from concourse import mybir as _mybir
    from concourse.bass_utils import run_bass_kernel_spmd as _run

    nc = _bacc.Bacc("TRN2", target_bir_lowering=False, num_devices=1)
    arrays, args = {}, []
    for name in _INS:
        a = _np.ascontiguousarray(inputs[name])
        arrays[f"in_{name}_dram"] = a
        args.append(nc.dram_tensor(f"in_{name}_dram", a.shape, _mybir.dt.from_np(a.dtype), kind="ExternalInput").ap())
    for i, (shape, dtype) in enumerate(_OUTS):
        dt = _mybir.dt.from_np(_np.dtype(dtype))
        args.append(nc.dram_tensor(f"out_{i}_dram", shape, dt, kind="ExternalOutput").ap())
    adjacency_stack(nc, *args)
    r = _run(nc, [arrays], core_ids=[0])
    got = tuple(r.results[0][f"out_{i}_dram"] for i in range(len(_OUTS)))
    return got[0]
```
